# Optimizing a Trainium2 kernel written in Bass

```python
import numpy as np
import jax
import jax.numpy as jnp

def _softmax(x, axis=-1):
    return jax.nn.softmax(x, axis=axis)

def _gelu(x):
    return jax.nn.gelu(x, approximate=True)

def _silu(x):
    return jax.nn.silu(x)

def _sigmoid(x):
    return jax.nn.sigmoid(x)

def _layernorm(x, axis=-1, eps=1e-05):
    m = jnp.mean(x, axis=axis, keepdims=True)
    v = jnp.var(x, axis=axis, keepdims=True)
    return (x - m) / jnp.sqrt(v + eps)

def _scatter_add(tgt, idx, src, axis=0):
    return tgt.at[idx].add(src)

def _segment_sum(src, seg, n):
    return jax.ops.segment_sum(src, seg, n)
kernel_name = 'mk_macaron_d2_jaxref_r4_31dafa'

def setup_inputs(seed: int=0):
    np.random.seed(seed)
    _w = jnp.asarray

    def _L0_attn_setup():
        import jax, jax.numpy as jnp
        import numpy as np
        B, N, E, D = (2, 1024, 256, 128)
        H = E // D
        LN_EPS = 1e-05

        def _gla_scan(q, k, v, g):

            def step(S, inp):
                qt, kt, vt, gt = inp
                S = jnp.exp(gt)[..., None] * S + kt[..., None] * vt[..., None, :]
                ot = jnp.einsum('bhd,bhde->bhe', qt, S)
                return (S, ot)
            xs = tuple((jnp.moveaxis(a, 2, 0) for a in (q, k, v, g)))
            S0 = jnp.zeros(q.shape[:2] + (q.shape[-1], v.shape[-1]), q.dtype)
            _, o = jax.lax.scan(step, S0, xs)
            return jnp.moveaxis(o, 0, 2)
        key = jax.random.key(seed)
        ks = jax.random.split(key, 6)
        s = 0.02
        return {'x': jax.random.normal(ks[0], (B, N, E), jnp.float32), 'W_in': jax.random.normal(ks[1], (3 * E, E), jnp.float32) * s, 'W_out': jax.random.normal(ks[2], (E, E), jnp.float32) * s, 'W_g1': jax.random.normal(ks[3], (D, E), jnp.float32) * s, 'W_g2': jax.random.normal(ks[4], (E, D), jnp.float32) * s, 'ln_w': jnp.ones((E,), jnp.float32)}
    _L0_attn_in = _L0_attn_setup()

    def _L0_ffn_setup():
        import jax, jax.numpy as jnp
        import numpy as np

        def _bitlinear(x, w_latent):
            scale = jax.lax.stop_gradient(jnp.clip(jnp.mean(jnp.abs(w_latent), axis=1, keepdims=True), 1e-05, None))
            tern = jnp.clip(jnp.round(w_latent / scale), -1.0, 1.0)
            w = w_latent + jax.lax.stop_gradient(tern - w_latent)
            return x @ (w * scale).T
        key = jax.random.key(seed)
        ks = jax.random.split(key, 6)
        dim, hidden, rank = (256, 1024, 16)
        B, S = (4, 1024)
        x = jax.random.normal(ks[0], (B, S, dim), dtype=jnp.float32)
        w_fc = 0.02 * jax.random.normal(ks[1], (hidden, dim), dtype=jnp.float32)
        w_proj = 0.02 * jax.random.normal(ks[2], (dim, hidden), dtype=jnp.float32)
        u = 0.02 * jax.random.normal(ks[3], (hidden, rank), dtype=jnp.float32)
        v = 0.02 * jax.random.normal(ks[4], (rank, dim), dtype=jnp.float32)
        fast_b = jax.random.normal(ks[5], (rank, rank), dtype=jnp.float32)
        gate = jnp.float32(0.05)
        return {'x': x, 'fast_b': fast_b, 'w_fc': w_fc, 'w_proj': w_proj, 'u': u, 'v': v, 'gate': gate}
    _L0_ffn_in = _L0_ffn_setup()

    def _L1_attn_setup():
        import jax, jax.numpy as jnp
        import numpy as np
        import math
        D_MODEL = 256
        N_HEADS = 16
        HEAD_DIM = D_MODEL // N_HEADS
        BAND_RADIUS = 2
        BAND_VAL = 0.1

        def _band_mask(S, dtype):
            i = jnp.arange(S)
            band = (jnp.abs(i[:, None] - i[None, :]) <= BAND_RADIUS).astype(dtype) * BAND_VAL
            return band[None, None, :, :]
        key = jax.random.key(seed)
        ks = jax.random.split(key, 12)
        B, S = (4, 512)
        scale = 1.0 / math.sqrt(D_MODEL)
        inp = {'x': jax.random.normal(ks[0], (B, S, D_MODEL), dtype=jnp.float32), 'ocr_context': jax.random.normal(ks[1], (B, S, D_MODEL), dtype=jnp.float32), 'Wq': jax.random.normal(ks[2], (D_MODEL, D_MODEL), dtype=jnp.float32) * scale, 'bq': jnp.zeros((D_MODEL,), dtype=jnp.float32), 'Wk': jax.random.normal(ks[3], (D_MODEL, D_MODEL), dtype=jnp.float32) * scale, 'bk': jnp.zeros((D_MODEL,), dtype=jnp.float32), 'Wv': jax.random.normal(ks[4], (D_MODEL, D_MODEL), dtype=jnp.float32) * scale, 'bv': jnp.zeros((D_MODEL,), dtype=jnp.float32), 'Wo': jax.random.normal(ks[5], (D_MODEL, D_MODEL), dtype=jnp.float32) * scale, 'bo': jnp.zeros((D_MODEL,), dtype=jnp.float32), 'ocr_bias': jax.random.normal(ks[6], (D_MODEL,), dtype=jnp.float32)}
        return inp
    _L1_attn_in = _L1_attn_setup()

    def _L1_ffn_setup():
        import jax, jax.numpy as jnp
        import numpy as np
        BEST_K = 2

        def _expert(xf, w1, w3, w2):
            return jax.nn.silu(xf @ w1) * (xf @ w3) @ w2
        key = jax.random.key(seed)
        ks = jax.random.split(key, 9)
        E, S_sh, D, H = (8, 2, 256, 128)
        B, S = (2, 512)
        w = lambda k, shape: jax.random.normal(k, shape, dtype=jnp.float32) * 0.02
        return {'x': jax.random.normal(ks[0], (B, S, D), dtype=jnp.float32), 'router_w': w(ks[1], (D, E)), 'router_b': jnp.zeros((E,), dtype=jnp.float32), 'routed_w1': w(ks[2], (E, D, H)), 'routed_w3': w(ks[3], (E, D, H)), 'routed_w2': w(ks[4], (E, H, D)), 'shared_w1': w(ks[5], (S_sh, D, H)), 'shared_w3': w(ks[6], (S_sh, D, H)), 'shared_w2': w(ks[7], (S_sh, H, D))}
    _L1_ffn_in = _L1_ffn_setup()
    _d = {'L0_attn_x': _L0_attn_in['x'], 'L0_attn_W_in': _L0_attn_in['W_in'], 'L0_attn_W_out': _L0_attn_in['W_out'], 'L0_attn_W_g1': _L0_attn_in['W_g1'], 'L0_attn_W_g2': _L0_attn_in['W_g2'], 'L0_attn_ln_w': _L0_attn_in['ln_w'], 'L0_ffn_fast_b': _L0_ffn_in['fast_b'], 'L0_ffn_w_fc': _L0_ffn_in['w_fc'], 'L0_ffn_w_proj': _L0_ffn_in['w_proj'], 'L0_ffn_u': _L0_ffn_in['u'], 'L0_ffn_v': _L0_ffn_in['v'], 'L0_ffn_gate': _L0_ffn_in['gate'], 'L1_attn_ocr_context': _L1_attn_in['ocr_context'], 'L1_attn_Wq': _L1_attn_in['Wq'], 'L1_attn_bq': _L1_attn_in['bq'], 'L1_attn_Wk': _L1_attn_in['Wk'], 'L1_attn_bk': _L1_attn_in['bk'], 'L1_attn_Wv': _L1_attn_in['Wv'], 'L1_attn_bv': _L1_attn_in['bv'], 'L1_attn_Wo': _L1_attn_in['Wo'], 'L1_attn_bo': _L1_attn_in['bo'], 'L1_attn_ocr_bias': _L1_attn_in['ocr_bias'], 'L1_ffn_router_w': _L1_ffn_in['router_w'], 'L1_ffn_router_b': _L1_ffn_in['router_b'], 'L1_ffn_routed_w1': _L1_ffn_in['routed_w1'], 'L1_ffn_routed_w3': _L1_ffn_in['routed_w3'], 'L1_ffn_routed_w2': _L1_ffn_in['routed_w2'], 'L1_ffn_shared_w1': _L1_ffn_in['shared_w1'], 'L1_ffn_shared_w3': _L1_ffn_in['shared_w3'], 'L1_ffn_shared_w2': _L1_ffn_in['shared_w2']}
    _x0 = _d['L0_attn_x']
    _d['L0_attn_x'] = jax.random.normal(jax.random.fold_in(jax.random.key(seed), 1), (16, 512, 256), dtype=_x0.dtype)
    del _x0
    return _d

def reference(L0_attn_x, L0_attn_W_in, L0_attn_W_out, L0_attn_W_g1, L0_attn_W_g2, L0_attn_ln_w, L0_ffn_fast_b, L0_ffn_w_fc, L0_ffn_w_proj, L0_ffn_u, L0_ffn_v, L0_ffn_gate, L1_attn_ocr_context, L1_attn_Wq, L1_attn_bq, L1_attn_Wk, L1_attn_bk, L1_attn_Wv, L1_attn_bv, L1_attn_Wo, L1_attn_bo, L1_attn_ocr_bias, L1_ffn_router_w, L1_ffn_router_b, L1_ffn_routed_w1, L1_ffn_routed_w3, L1_ffn_routed_w2, L1_ffn_shared_w1, L1_ffn_shared_w3, L1_ffn_shared_w2):

    def _L0_attn_ref(x, W_in, W_out, W_g1, W_g2, ln_w):
        import jax, jax.numpy as jnp
        import numpy as np
        B, N, E, D = (2, 1024, 256, 128)
        H = E // D
        LN_EPS = 1e-05

        def _gla_scan(q, k, v, g):

            def step(S, inp):
                qt, kt, vt, gt = inp
                S = jnp.exp(gt)[..., None] * S + kt[..., None] * vt[..., None, :]
                ot = jnp.einsum('bhd,bhde->bhe', qt, S)
                return (S, ot)
            xs = tuple((jnp.moveaxis(a, 2, 0) for a in (q, k, v, g)))
            S0 = jnp.zeros(q.shape[:2] + (q.shape[-1], v.shape[-1]), q.dtype)
            _, o = jax.lax.scan(step, S0, xs)
            return jnp.moveaxis(o, 0, 2)
        b, n, e = x.shape
        u = x @ W_in.T
        v, q, lg = jnp.split(u, 3, axis=-1)
        q = jax.nn.silu(q)
        f = jax.nn.sigmoid(lg)
        k = 1.0 - f
        g = jax.nn.log_sigmoid(lg)

        def tohead(a):
            return a.reshape(b, n, H, D).transpose(0, 2, 1, 3)
        o = _gla_scan(tohead(q), tohead(k), tohead(v), tohead(g))
        o = o.transpose(0, 2, 1, 3).reshape(b, n, e)
        gate = jax.nn.sigmoid(x @ W_g1.T @ W_g2.T)
        o = o * gate
        mu = jnp.mean(o, axis=-1, keepdims=True)
        var = jnp.var(o, axis=-1, keepdims=True)
        o = (o - mu) * jax.lax.rsqrt(var + LN_EPS) * ln_w
        return o @ W_out.T

    def _L0_ffn_ref(x, fast_b, w_fc, w_proj, u, v, gate):
        import jax, jax.numpy as jnp
        import numpy as np

        def _bitlinear(x, w_latent):
            scale = jax.lax.stop_gradient(jnp.clip(jnp.mean(jnp.abs(w_latent), axis=1, keepdims=True), 1e-05, None))
            tern = jnp.clip(jnp.round(w_latent / scale), -1.0, 1.0)
            w = w_latent + jax.lax.stop_gradient(tern - w_latent)
            return x @ (w * scale).T
        h = _bitlinear(x, w_fc) + gate * (x @ v.T @ fast_b.T @ u.T)
        r = jnp.maximum(h, 0.0)
        return _bitlinear(r * r, w_proj)

    def _L1_attn_ref(x, ocr_context, Wq, bq, Wk, bk, Wv, bv, Wo, bo, ocr_bias):
        import jax, jax.numpy as jnp
        import numpy as np
        import math
        D_MODEL = 256
        N_HEADS = 16
        HEAD_DIM = D_MODEL // N_HEADS
        BAND_RADIUS = 2
        BAND_VAL = 0.1

        def _band_mask(S, dtype):
            i = jnp.arange(S)
            band = (jnp.abs(i[:, None] - i[None, :]) <= BAND_RADIUS).astype(dtype) * BAND_VAL
            return band[None, None, :, :]
        B, S, _ = x.shape
        q = x @ Wq.T + bq + ocr_bias
        k = x @ Wk.T + bk
        v = x @ Wv.T + bv
        q = q.reshape(B, S, N_HEADS, HEAD_DIM).transpose(0, 2, 1, 3)
        k = k.reshape(B, S, N_HEADS, HEAD_DIM).transpose(0, 2, 1, 3)
        v = v.reshape(B, S, N_HEADS, HEAD_DIM).transpose(0, 2, 1, 3)
        scores = jnp.einsum('bhsd,bhtd->bhst', q, k) / math.sqrt(HEAD_DIM)
        scores = scores + _band_mask(S, scores.dtype)
        attn = jax.nn.softmax(scores, axis=-1)
        out = jnp.einsum('bhst,bhtd->bhsd', attn, v)
        out = out.transpose(0, 2, 1, 3).reshape(B, S, D_MODEL)
        return out @ Wo.T + bo

    def _L1_ffn_ref(x, router_w, router_b, routed_w1, routed_w3, routed_w2, shared_w1, shared_w3, shared_w2):
        import jax, jax.numpy as jnp
        import numpy as np
        BEST_K = 2

        def _expert(xf, w1, w3, w2):
            return jax.nn.silu(xf @ w1) * (xf @ w3) @ w2
        B, S, D = x.shape
        T = B * S
        xf = x.reshape(T, D)
        logits = xf @ router_w + router_b
        topk_vals, topk_idx = jax.lax.top_k(logits, BEST_K)
        sparse = jnp.full_like(logits, -jnp.inf)
        sparse = sparse.at[jnp.arange(T)[:, None], topk_idx].set(topk_vals)
        gates = jax.nn.softmax(sparse, axis=-1)
        routed = jax.vmap(_expert, in_axes=(None, 0, 0, 0))(xf, routed_w1, routed_w3, routed_w2)
        routed_out = jnp.einsum('etd,te->td', routed, gates)
        shared_out = jax.vmap(_expert, in_axes=(None, 0, 0, 0))(xf, shared_w1, shared_w3, shared_w2).sum(axis=0)
        return (routed_out + shared_out).reshape(B, S, D)
    x = L0_attn_x
    x = x + 0.5 * _L0_ffn_ref(_layernorm(x, axis=-1), L0_ffn_fast_b, L0_ffn_w_fc, L0_ffn_w_proj, L0_ffn_u, L0_ffn_v, L0_ffn_gate)
    x = x + _L0_attn_ref(_layernorm(x, axis=-1), L0_attn_W_in, L0_attn_W_out, L0_attn_W_g1, L0_attn_W_g2, L0_attn_ln_w)
    x = x + 0.5 * _L0_ffn_ref(_layernorm(x, axis=-1), L0_ffn_fast_b, L0_ffn_w_fc, L0_ffn_w_proj, L0_ffn_u, L0_ffn_v, L0_ffn_gate)
    x = x + 0.5 * _L1_ffn_ref(_layernorm(x, axis=-1), L1_ffn_router_w, L1_ffn_router_b, L1_ffn_routed_w1, L1_ffn_routed_w3, L1_ffn_routed_w2, L1_ffn_shared_w1, L1_ffn_shared_w3, L1_ffn_shared_w2)
    x = x + _L1_attn_ref(_layernorm(x, axis=-1), L1_attn_ocr_context, L1_attn_Wq, L1_attn_bq, L1_attn_Wk, L1_attn_bk, L1_attn_Wv, L1_attn_bv, L1_attn_Wo, L1_attn_bo, L1_attn_ocr_bias)
    x = x + 0.5 * _L1_ffn_ref(_layernorm(x, axis=-1), L1_ffn_router_w, L1_ffn_router_b, L1_ffn_routed_w1, L1_ffn_routed_w3, L1_ffn_routed_w2, L1_ffn_shared_w1, L1_ffn_shared_w3, L1_ffn_shared_w2)
    return x

_drawn_inputs = setup_inputs


def setup_inputs(seed=0):
    import zlib

    import numpy as np

    out = dict(_drawn_inputs(seed))
    spreads = {'L0_attn_ln_w': (1.0, 0.2),
     'L1_attn_bq': (0.0, 0.639),
     'L1_attn_bk': (0.0, 0.8),
     'L1_attn_bv': (0.0, 0.1),
     'L1_attn_bo': (0.0, 0.1),
     'L1_ffn_router_b': (0.0, 0.8)}
    factors = {'L0_attn_W_g1': 4.877,
     'L0_attn_W_g2': 4.87,
     'L0_ffn_fast_b': 8.0,
     'L0_ffn_u': 8.0,
     'L0_ffn_v': 8.0,
     'L1_ffn_router_w': 8.0,
     'L1_ffn_routed_w1': 7.446,
     'L1_ffn_routed_w3': 7.362,
     'L1_ffn_routed_w2': 7.361,
     'L1_ffn_shared_w1': 3.662,
     'L1_ffn_shared_w3': 3.617,
     'L1_ffn_shared_w2': 3.618}
    for name, (base, spread) in spreads.items():
        noise = np.random.default_rng([zlib.crc32(name.encode()), seed]).standard_normal(out[name].shape)
        drawn = base * np.exp(spread * noise) if base else spread * noise
        out[name] = jnp.asarray(drawn.astype(out[name].dtype))
    for name, factor in factors.items():
        out[name] = (out[name] * factor).astype(out[name].dtype)
    return out
```

```python
import math
from contextlib import ExitStack

import concourse.bass as bass
from concourse import mybir

F32 = mybir.dt.float32
F32R = mybir.dt.float32r
U8 = mybir.dt.uint8
ALU = mybir.AluOpType
ACT = mybir.ActivationFunctionType
AXIS_X = mybir.AxisListType.X

P = 128
TOKENS = 512
TILES = TOKENS // P
DM = 256
KT = DM // P
LN_EPS = 1e-5


class Core:

    def __init__(self, nc, ctx, batches):
        self.nc, self.batches = nc, batches
        self.ctx = ctx
        self.made = 0
        self.stage_sems = []
        sb = self.sbuf
        n = batches * TILES
        self.x = sb("x_resident", [P, n, DM])
        self.stat6 = sb("ln_stat6", [P, TILES, 6])
        self.mv4 = sb("ln_mean_var4", [P, TILES, 2])
        self.mv = sb("ln_mean_var", [P, n, 2])
        self.rstd = sb("ln_rstd", [P, n, 1])
        self.eps = sb("ln_eps", [P, 1])
        self.ident = sb("identity", [P, P])
        self.ones = sb("ones", [P, P])
        self.xn = sb("xn", [P, TILES, DM])
        self.xh = sb("xnT_hi", [P, KT, TOKENS], F32R)
        self.xl = sb("xnT_lo", [P, KT, TOKENS], F32R)

    def sbuf(self, name, shape, dt=F32, ctx=None):
        self.made += 1
        return (ctx or self.ctx).enter_context(self.nc.sbuf_tensor(f"{name}_sb{self.made}", shape, dt))

    def psum(self, name, shape, ctx):
        self.made += 1
        return ctx.enter_context(self.nc.psum_tensor(f"{name}_ps{self.made}", shape, F32))

    def sem(self, name):
        self.stage_sems.append(self.nc.alloc_semaphore(name=name))
        return self.stage_sems[-1]

    def end_stage(self):
        self.nc.clear_and_free_semaphores(self.stage_sems)
        self.nc.all_engine_barrier()
        self.stage_sems = []


def hold(engine, turns):
    engine.sem_inc(turns, 1)


def as_f32(ap):
    return ap.bitcast(F32)


def bcast(ap, shape):
    return ap.to_broadcast(shape)


def constants(core, x_dram):
    nc, s = core.nc, core.sem
    n = core.batches * TILES
    ident_zero, const_ready = s("ident_zero"), s("const_ready")
    x_loaded = [s(f"x_loaded{i}") for i in range(4)]
    stats_ready, aggr_ready = s("c_stats_ready"), s("c_aggr_ready")
    x_rows = x_dram.rearrange("(n p) d -> p n d", p=P)
    part = n // 4
    with nc.Block() as block:

        @block.sync
        def _(sp):
            for i in range(4):
                sp.dma_start(core.x[:, i * part:(i + 1) * part, :],
                             x_rows[:, i * part:(i + 1) * part, :]).then_inc(x_loaded[i], 16)

        @block.gpsimd
        def _(pool):
            nc.gpsimd.memset(core.ident[:, :], 0.0).then_inc(ident_zero, 1)
            nc.gpsimd.memset(core.ones[:, :], 1.0).then_inc(const_ready, 1)
            nc.gpsimd.memset(core.eps[:, :], LN_EPS).then_inc(const_ready, 1)
            pool.wait_ge(ident_zero, 1)
            nc.gpsimd.affine_select(out=core.ident[:, :], in_=core.ident[:, :], compare_op=ALU.not_equal,
                                    fill=1.0, base=0, pattern=[[-1, P]],
                                    channel_multiplier=1).then_inc(const_ready, 1)

        @block.vector
        def _(dve):
            for i in range(4):
                dve.wait_ge(x_loaded[i], 16)
                for t in range(i * part, (i + 1) * part):
                    if t:
                        dve.wait_ge(aggr_ready, t)
                    nc.vector.bn_stats(core.stat6[:, 0, :], core.x[:, t, :]).then_inc(stats_ready, 1)
                    dve.wait_ge(stats_ready, t + 1)
                    nc.vector.bn_aggr(core.mv[:, t, :], core.stat6[:, 0, :]).then_inc(aggr_ready, 1)


class Norm:

    def __init__(self, core, name, banks):
        self.c = core
        self.tp = banks
        self.xn_ready = core.sem(name + "_xn_ready")
        self.tp_ready = core.sem(name + "_tp_ready")
        self.xh_ready = core.sem(name + "_xh_ready")
        self.xl_ready = core.sem(name + "_xl_ready")

    def normalise(self, dve, b):
        c = self.c
        if not (isinstance(b, int) and b == 0):
            dve.wait_ge(self.tp_ready, b)
        for t in range(TILES):
            n = b * TILES + t
            op = c.nc.vector.tensor_scalar(c.xn[:, t, :], c.x[:, n, :], c.mv[:, n, 0:1], c.rstd[:, n, :],
                                           ALU.subtract, ALU.mult)
        op.then_inc(self.xn_ready, 1)

    def transpose(self, pe, b, tp_free=None):
        c = self.c
        pe.wait_ge(self.xn_ready, b + 1)
        if not (isinstance(b, int) and b == 0):
            pe.wait_ge(self.xl_ready, b)
        if tp_free is not None:
            tp_free()
        for k in range(KT):
            for t in range(TILES):
                op = c.nc.tensor.transpose(self.tp[:, k, t * P:(t + 1) * P], c.xn[:, t, k * P:(k + 1) * P],
                                           c.ident[:, :])
        op.then_inc(self.tp_ready, 1)

    def high(self, act, b, readers_done=None):
        c = self.c
        act.wait_ge(self.tp_ready, b + 1)
        if readers_done is not None:
            readers_done()
        c.nc.scalar.copy(c.xh[:, :, :], self.tp[:, :, :]).then_inc(self.xh_ready, 1)

    def low(self, dve, b):
        c = self.c
        dve.wait_ge(self.xh_ready, b + 1)
        c.nc.vector.tensor_tensor(c.xl[:, :, :], self.tp[:, :, :], as_f32(c.xh[:, :, :]),
                                  ALU.subtract).then_inc(self.xl_ready, 1)


def rstd_block(core, name):
    nc = core.nc
    sqrt_ready = core.sem(name + "_sqrt_ready")
    with nc.Block() as block:

        @block.scalar
        def _(act):
            nc.scalar.activation(core.rstd[:, :, 0], core.mv[:, :, 1], ACT.Sqrt,
                                 bias=core.eps[:, 0:1]).then_inc(sqrt_ready, 1)

        @block.vector
        def _(dve):
            dve.wait_ge(sqrt_ready, 1)
            nc.vector.reciprocal(core.rstd[:, :, 0], core.rstd[:, :, 0])


class Stats:

    def __init__(self, core, name):
        self.c = core
        self.stats = core.sem(name + "_bn_stats_ready")
        self.turns = core.sem(name + "_stats_turns")
        self.aggr = core.sem(name + "_bn_aggr_ready")

    def take(self, dve, b, updated):
        c = self.c
        updated()
        if not (isinstance(b, int) and b == 0):
            dve.wait_ge(self.aggr, 2 * b)
        hold(dve, self.turns)
        for t in range(TILES):
            op = c.nc.vector.bn_stats(c.stat6[:, t, :], c.x[:, b * TILES + t, :])
        op.then_inc(self.stats, 1)
        dve.wait_ge(self.stats, b + 1)
        hold(dve, self.turns)
        for t in range(TILES):
            op = c.nc.vector.bn_aggr(c.mv4[:, t, :], c.stat6[:, t, :])
        op.then_inc(self.aggr, 1)
        dve.wait_ge(self.aggr, 2 * b + 1)
        c.nc.vector.tensor_scalar(c.mv[:, bass.ds(b * TILES, TILES), :], c.mv4[:, :, :], 0.0, None,
                                  ALU.add).then_inc(self.aggr, 1)


def over_sequences(engine, batches, body):
    body(0, False, batches > 1)
    if batches > 2:
        with engine.Fori(1, batches - 1) as b:
            body(b, True, True)
    if batches > 1:
        body(batches - 1, True, False)


HIDDEN = 1024
JT = HIDDEN // P
RANK = 16
SCALE_MIN = 1e-5


class FfnWeights:
    def __init__(self, core, ctx):
        self.fc_h = core.sbuf("w_fc_hi", [P, KT, HIDDEN], F32R, ctx)
        self.fc_l = core.sbuf("w_fc_lo", [P, KT, HIDDEN], F32R, ctx)
        self.proj = core.sbuf("w_proj_tern", [P, JT, DM], F32R, ctx)
        self.half_scale = core.sbuf("half_scale", [P, DM], F32, ctx)


def ffn_weights(core, w, dram, name):
    nc, s = core.nc, core.sem
    w_fc, w_proj, u_t, v, fast_bt, gate = dram
    loaded = s(name + "_w_loaded")
    dve_step = s(name + "_w_dve_step")
    lowrank_ready = s(name + "_w_lowrank")
    tr_ready, high_ready, low_ready = s(name + "_w_transposed"), s(name + "_w_high"), s(name + "_w_low")
    bv_ready, row_ready, ptr_ready, pcopy = s(name + "_w_bv"), s(name + "_w_row"), s(name + "_w_ptr"), s(name + "_w_pcopy")
    fc_done = s(name + "_w_fc_done")
    proj_done = s(name + "_w_proj_done")
    with ExitStack() as ctx:
        wf = core.sbuf("wf_nat", [P, JT, DM], F32, ctx)
        wp = core.sbuf("wp_nat", [P, KT, HIDDEN], F32, ctx)
        ut = core.sbuf("u_t", [RANK, HIDDEN], F32, ctx)
        vs = core.sbuf("v_sb", [RANK, DM], F32, ctx)
        bt = core.sbuf("fast_bt", [RANK, RANK], F32, ctx)
        gt = core.sbuf("gate_sb", [RANK, 1], F32, ctx)
        bv = core.sbuf("gate_b_v", [RANK, DM], F32, ctx)
        neg = core.sbuf("w_neg", [P, HIDDEN], F32, ctx)
        tern = core.sbuf("w_tern", [P, HIDDEN], F32, ctx)
        NS = JT + KT
        ssum = core.sbuf("s_sum", [P, NS], F32, ctx)
        scale = core.sbuf("s_scale", [P, NS], F32, ctx)
        ph = core.sbuf("s_half", [P, NS], F32, ctx)
        nh = core.sbuf("s_neg_half", [P, NS], F32, ctx)
        weff = core.sbuf("w_eff", [P, JT, DM], F32, ctx)
        ptern = core.sbuf("p_tern", [P, KT, HIDDEN], F32, ctx)
        diag = core.sbuf("s_diag", [P, KT, P], F32, ctx)
        ps = [core.psum(f"wps{i}", [P, 512], ctx) for i in range(4)]
        with nc.Block() as block:

            @block.sync
            def _(sp):
                sp.dma_start(wf[:, :, :], w_fc.rearrange("(j p) d -> p j d", p=P)).then_inc(loaded, 16)
                sp.dma_start(wp[:, :, :], w_proj.rearrange("(k p) h -> p k h", p=P)).then_inc(loaded, 16)
                sp.dma_start(ut[:, :], u_t).then_inc(loaded, 16)
                sp.dma_start(vs[:, :], v).then_inc(loaded, 16)
                sp.dma_start(bt[:, :], fast_bt).then_inc(loaded, 16)
                for r in range(RANK):
                    sp.dma_start(gt[r:r + 1, :], gate).then_inc(loaded, 16)

            ALL = 16 * (5 + RANK)

            @block.tensor
            def _(pe):
                pe.wait_ge(loaded, ALL)
                nc.tensor.matmul(ps[0][0:RANK, 0:DM], bt[:, :], vs[:, :], start=True, stop=True).then_inc(bv_ready, 1)
                for j in range(JT):
                    pe.wait_ge(bv_ready, 2)
                    if j >= 2:
                        pe.wait_ge(fc_done, j - 1)
                    nc.tensor.matmul(ps[2 + j % 2][:, 0:DM], ut[:, j * P:(j + 1) * P], bv[:, :],
                                     start=True, stop=True).then_inc(lowrank_ready, 1)
                n = 0
                for j in range(JT):
                    pe.wait_ge(fc_done, j + 1)
                    if n >= 2:
                        pe.wait_ge(low_ready, n - 1)
                    for k in range(KT):
                        op = nc.tensor.transpose(ps[n % 2][:, k * P:(k + 1) * P], weff[:, j, k * P:(k + 1) * P],
                                                 core.ident[:, :])
                    op.then_inc(tr_ready, 1)
                    n += 1
                pe.wait_ge(proj_done, 1)
                for j in range(JT):
                    if j < 2:
                        pe.wait_ge(low_ready, JT)
                    else:
                        pe.wait_ge(pcopy, j - 1)
                    for k in range(KT):
                        op = nc.tensor.transpose(ps[j % 2][:, k * P:(k + 1) * P], ptern[:, k, j * P:(j + 1) * P],
                                                 core.ident[:, :])
                    op.then_inc(ptr_ready, 1)
                for k in range(KT):
                    op = nc.tensor.matmul(ps[2][:, k * P:(k + 1) * P], core.ones[:, :], diag[:, k, :],
                                          start=True, stop=True)
                op.then_inc(row_ready, 1)

            @block.scalar
            def _(act):
                for j in range(JT):
                    act.wait_ge(tr_ready, j + 1)
                    nc.scalar.copy(w.fc_h[:, :, j * P:(j + 1) * P],
                                   ps[j % 2][:, 0:DM].rearrange("p (k m) -> p k m", k=KT)).then_inc(high_ready, 1)
                for j in range(JT):
                    act.wait_ge(ptr_ready, j + 1)
                    nc.scalar.copy(w.proj[:, j, :], ps[j % 2][:, 0:DM]).then_inc(pcopy, 1)
                act.wait_ge(row_ready, 1)
                nc.scalar.mul(w.half_scale[:, :], ps[2][:, 0:DM], 0.5)

            @block.vector
            def _(dve):
                count = [0]

                def link(op):
                    count[0] += 1
                    op.then_inc(dve_step, 1)
                    dve.wait_ge(dve_step, count[0])

                dve.wait_ge(loaded, ALL)
                dve.wait_ge(bv_ready, 1)
                nc.vector.tensor_scalar(bv[:, :], ps[0][0:RANK, 0:DM], gt[:, 0:1], None, ALU.mult).then_inc(bv_ready, 1)
                blocks = [(wf[:, j, :], DM) for j in range(JT)] + [(wp[:, k, :], HIDDEN) for k in range(KT)]
                for i, (a, n) in enumerate(blocks):
                    link(nc.vector.tensor_reduce(ssum[:, i:i + 1], a, AXIS_X, ALU.add, apply_absolute_value=True))
                link(nc.vector.tensor_scalar(scale[:, 0:JT], ssum[:, 0:JT], 1.0 / DM, SCALE_MIN, ALU.mult, ALU.max))
                link(nc.vector.tensor_scalar(scale[:, JT:NS], ssum[:, JT:NS], 1.0 / HIDDEN, SCALE_MIN, ALU.mult, ALU.max))
                link(nc.vector.tensor_scalar(ph[:, :], scale[:, :], 0.5, None, ALU.mult))
                link(nc.vector.tensor_scalar(nh[:, :], scale[:, :], -0.5, None, ALU.mult))
                for i, (a, n) in enumerate(blocks):
                    link(nc.vector.tensor_scalar(neg[:, 0:n], a, nh[:, i:i + 1], None, ALU.is_lt))
                    out = tern[:, 0:n] if i < JT else ptern[:, i - JT, :]
                    link(nc.vector.scalar_tensor_tensor(out, a, ph[:, i:i + 1], neg[:, 0:n], ALU.is_gt, ALU.subtract))
                    if i < JT:
                        dve.wait_ge(lowrank_ready, i + 1)
                        nc.vector.scalar_tensor_tensor(weff[:, i, :], tern[:, 0:n], scale[:, i:i + 1],
                                                       ps[2 + i % 2][:, 0:DM], ALU.mult, ALU.add).then_inc(fc_done, 1)
                        dve.wait_ge(fc_done, i + 1)
                for k in range(KT):
                    op = nc.vector.tensor_scalar(diag[:, k, :], core.ident[:, :], scale[:, JT + k:JT + k + 1], None,
                                                 ALU.mult)
                op.then_inc(proj_done, 1)
                for j in range(JT):
                    dve.wait_ge(high_ready, j + 1)
                    nc.vector.tensor_tensor(w.fc_l[:, :, j * P:(j + 1) * P],
                                            ps[j % 2][:, 0:DM].rearrange("p (k m) -> p k m", k=KT),
                                            as_f32(w.fc_h[:, :, j * P:(j + 1) * P]), ALU.subtract).then_inc(low_ready, 1)


def ffn_stage(core, w, name):
    nc, s = core.nc, core.sem
    RING, LAG = 6, 4
    rstd_block(core, name)
    h_ready = s(name + "_h_ready")
    r_ready = s(name + "_relu_ready")
    sq_ready = s(name + "_sq_ready")
    high_ready = s(name + "_high_ready")
    low_ready = s(name + "_low_ready")
    proj_done = s(name + "_proj_done")
    y_free = s(name + "_y_free")
    x_done = s(name + "_x_updated")
    with ExitStack() as ctx:
        hp = [core.psum(f"{name}_hp{i}", [P, TOKENS], ctx) for i in range(2)]
        y = core.psum(f"{name}_y", [P, TILES, DM], ctx)
        tp = core.psum(f"{name}_tp", [P, KT, TOKENS], ctx)
        relu = core.sbuf("f_relu", [P, 2, TOKENS], F32, ctx)
        sq = core.sbuf("f_sq", [P, 2, TOKENS], F32, ctx)
        sqh = core.sbuf("f_sq_hi", [P, RING, TOKENS], F32R, ctx)
        sql = core.sbuf("f_sq_lo", [P, RING, TOKENS], F32R, ctx)
        ys = core.sbuf("f_y_scaled", [P, TILES, DM], F32, ctx)
        norm = Norm(core, name, tp)
        stats = Stats(core, name)
        slot = [j % RING for j in range(JT)]
        with nc.Block() as block:

            @block.tensor
            def _(pe):
                norm.transpose(pe, 0)
                pe.sem_inc(proj_done, RING)

                def fc(b, j):
                    if j == 0:
                        pe.wait_ge(norm.xl_ready, b + 1)
                    pe.wait_ge(sq_ready, b * JT + j + 1)
                    mm = [(w.fc_h, core.xh), (w.fc_l, core.xh), (w.fc_h, core.xl)]
                    for k in range(KT):
                        for i, (a, x) in enumerate(mm):
                            op = nc.tensor.matmul(hp[j % 2][:, :], a[:, k, j * P:(j + 1) * P], x[:, k, :],
                                                  start=(k == 0 and i == 0), stop=(k == KT - 1 and i == 2))
                    op.then_inc(h_ready, 1)

                def proj(b, j):
                    pe.wait_ge(low_ready, b * JT + j + 3)
                    if j == 0:
                        pe.wait_ge(y_free, b + 1)
                    for t in range(TILES):
                        for i, r in enumerate((sqh, sql)):
                            op = nc.tensor.matmul(y[:, t, :], r[:, slot[j], t * P:(t + 1) * P], w.proj[:, j, :],
                                                  start=(j == 0 and t % 2 == 0 and i == 0),
                                                  stop=(j == JT - 1 and i == 1), skip_group_check=True)
                    op.then_inc(proj_done, 1)

                def body(b, before, more):
                    for j in range(JT):
                        fc(b, j)
                        if j >= LAG:
                            proj(b, j - LAG)
                    if more:
                        norm.transpose(pe, b + 1)
                    for j in range(JT - LAG, JT):
                        proj(b, j)

                over_sequences(pe, core.batches, body)

            @block.scalar
            def _(act):
                norm.high(act, 0)

                def relu_of(b, j):
                    act.wait_ge(h_ready, b * JT + j + 1)
                    nc.scalar.activation(relu[:, j % 2, :], hp[j % 2][:, :], ACT.Relu).then_inc(r_ready, 1)

                def high_of(b, j):
                    act.wait_ge(sq_ready, b * JT + j + 3)
                    ago = RING if j >= RING else JT - RING if j + RING < JT else JT
                    act.wait_ge(proj_done, b * JT + j - ago + 1 + RING)
                    nc.scalar.copy(sqh[:, slot[j], :], sq[:, j % 2, :]).then_inc(high_ready, 1)

                def body(b, before, more):
                    for j in range(JT):
                        relu_of(b, j)
                        if j >= 1:
                            high_of(b, j - 1)
                    if more:
                        norm.high(act, b + 1, lambda: act.wait_ge(h_ready, (b + 1) * JT))
                    high_of(b, JT - 1)

                over_sequences(act, core.batches, body)

            @block.gpsimd
            def _(pool):
                pool.sem_inc(low_ready, 2)

                def body(b, before, more):
                    for j in range(JT):
                        pool.wait_ge(high_ready, b * JT + j + 1)
                        nc.gpsimd.tensor_tensor(sql[:, slot[j], :], sq[:, j % 2, :], as_f32(sqh[:, slot[j], :]),
                                                ALU.subtract).then_inc(low_ready, 1)
                        if before and j == 1:
                            add(b - 1)

                def add(b):
                    pool.wait_ge(y_free, b + 2)
                    xs = core.x[:, bass.ds(b * TILES, TILES), :]
                    nc.gpsimd.tensor_tensor(xs, xs, ys[:, :, :], ALU.add).then_inc(x_done, 1)

                over_sequences(pool, core.batches, body)
                add(core.batches - 1)

            @block.vector
            def _(dve):
                dve.sem_inc(sq_ready, 2)
                dve.sem_inc(y_free, 1)
                norm.normalise(dve, 0)
                norm.low(dve, 0)

                def square(b, j):
                    dve.wait_ge(r_ready, b * JT + j + 1)
                    dve.wait_ge(low_ready, b * JT + j + 1)
                    nc.vector.tensor_tensor(sq[:, j % 2, :], hp[j % 2][:, :], relu[:, j % 2, :],
                                            ALU.mult).then_inc(sq_ready, 1)

                def scale(b):
                    dve.wait_ge(proj_done, b * JT + JT + RING)
                    if not (isinstance(b, int) and b == 0):
                        dve.wait_ge(x_done, b)
                    nc.vector.tensor_tensor(ys[:, :, :], y[:, :, :],
                                            bcast(w.half_scale[:, :].unsqueeze(1), [P, TILES, DM]),
                                            ALU.mult).then_inc(y_free, 1)

                def body(b, before, more):
                    for j in range(JT):
                        square(b, j)
                        if before and j == 0:
                            scale(b - 1)
                        if before and j == 3:
                            stats.take(dve, b - 1, lambda: dve.wait_ge(x_done, b))
                        if more and j == 5:
                            norm.normalise(dve, b + 1)
                    if more:
                        norm.low(dve, b + 1)

                over_sequences(dve, core.batches, body)
                scale(core.batches - 1)
                stats.take(dve, core.batches - 1, lambda: dve.wait_ge(x_done, core.batches))


EXPERTS, SHARED = 8, 2
ALL_EXPERTS = EXPERTS + SHARED
TOP_K = 2


def split_pair(core, name, parts, ctx):
    nc, s = core.nc, core.sem
    loaded = [s(f"{name}_loaded{i}") for i in range(2)]
    high, low = s(name + "_w_high"), s(name + "_w_low")
    with ExitStack() as inner:
        width = max(h.free_size() for _, h, _ in parts)
        stage = core.sbuf(name + "_stage", [P, 2, width], F32, inner)
        with nc.Block() as block:

            @block.sync
            def _(sp):
                for i, (src, hi, lo) in enumerate(parts):
                    if i >= 2:
                        sp.wait_ge(low, i - 1)
                    n, rows = hi.free_size(), hi.shape[0]
                    shape = src.shape
                    dst = stage[0:rows, i % 2, 0:n]
                    if len(shape) == 3:
                        dst = dst.rearrange("p (a b) -> p a b", a=shape[1])
                    if i >= 2:
                        sp.wait_ge(loaded[i % 2], 16 * (i // 2))
                    sp.dma_start(dst, src).then_inc(loaded[i % 2], 16)

            def view(i, like):
                n, rows = like.free_size(), like.shape[0]
                v = stage[0:rows, i % 2, 0:n]
                if len(like.shape) == 3:
                    v = v.rearrange("p (a b) -> p a b", a=like.shape[1])
                return v

            @block.scalar
            def _(act):
                for i, (src, hi, lo) in enumerate(parts):
                    act.wait_ge(loaded[i % 2], 16 * (i // 2 + 1))
                    nc.scalar.copy(hi, view(i, hi)).then_inc(high, 1)

            @block.vector
            def _(dve):
                for i, (src, hi, lo) in enumerate(parts):
                    dve.wait_ge(high, i + 1)
                    nc.vector.tensor_tensor(lo, view(i, hi), as_f32(hi), ALU.subtract).then_inc(low, 1)


def moe_stage(core, a, name, last=False):
    nc, s = core.nc, core.sem
    E, H = ALL_EXPERTS, P
    RING, LAG = 4, 2
    with ExitStack() as ctx:
        w1h, w1l, w3h, w3l = (core.sbuf(n, [P, E, KT, H], F32R, ctx) for n in ("w1h", "w1l", "w3h", "w3l"))
        w2h, w2l = (core.sbuf(n, [P, E, DM], F32R, ctx) for n in ("w2h", "w2l"))
        rwh, rwl = (core.sbuf(n, [P, KT, EXPERTS], F32R, ctx) for n in ("rwh", "rwl"))
        parts = []
        for e in range(E):
            kind, i = ("routed", e) if e < EXPERTS else ("shared", e - EXPERTS)
            for n, hi, lo in (("w1", w1h, w1l), ("w3", w3h, w3l)):
                parts.append((a[f"{kind}_{n}"][i].rearrange("(k p) h -> p k h", p=P), hi[:, e, :, :], lo[:, e, :, :]))
            parts.append((a[f"{kind}_w2"][i], w2h[:, e, :], w2l[:, e, :]))
        parts.append((a["router_w"].rearrange("(k p) e -> p k e", p=P), rwh[:, :, :], rwl[:, :, :]))
        split_pair(core, name, parts, ctx)
        rstd_block(core, name)

        rb = core.sbuf("router_b", [P, EXPERTS], F32, ctx)
        earlier = core.sbuf("earlier", [P, EXPERTS, EXPERTS], F32, ctx)
        rb_loaded, earlier_one, earlier_ready = s(name + "_rb_loaded"), s(name + "_e_one"), s(name + "_earlier")
        lg = core.sbuf("logits", [P, TILES, EXPERTS], F32, ctx)
        big = [TILES, EXPERTS, EXPERTS]
        above, notless = core.sbuf("above", [P] + big, F32, ctx), core.sbuf("notless", [P] + big, F32, ctx)
        rank = core.sbuf("rank", [P, TILES, EXPERTS], F32, ctx)
        chosen = core.sbuf("chosen", [P, TILES, EXPERTS], F32, ctx)
        picked = core.sbuf("picked", [P, TILES, EXPERTS], F32, ctx)
        both = core.sbuf("both", [P, TILES, 1], F32, ctx)
        margin = core.sbuf("margin", [P, TILES, EXPERTS], F32, ctx)
        share = core.sbuf("share", [P, TILES, EXPERTS], F32, ctx)
        gates = core.sbuf("gates", [P, TILES, EXPERTS], F32, ctx)
        silu = core.sbuf("m_silu", [P, 2, TOKENS], F32, ctx)
        act_f = core.sbuf("m_act", [P, 2, TOKENS], F32, ctx)
        ah = core.sbuf("m_act_hi", [P, RING, TOKENS], F32R, ctx)
        al = core.sbuf("m_act_lo", [P, RING, TOKENS], F32R, ctx)
        h1 = [core.psum(f"{name}_h1{i}", [P, TOKENS], ctx) for i in range(2)]
        h3 = [core.psum(f"{name}_h3{i}", [P, TOKENS], ctx) for i in range(2)]
        y = core.psum(f"{name}_y", [P, TILES, DM], ctx)
        tp = core.psum(f"{name}_tp", [P, KT, TOKENS], ctx)
        logit_ps = tp[:, 0, 0:TILES * EXPERTS].rearrange("p (t e) -> p t e", t=TILES)

        h_ready = s(name + "_h_ready")
        silu_ready = s(name + "_silu_ready")
        act_ready = s(name + "_act_ready")
        high_ready = s(name + "_high_ready")
        low_ready = s(name + "_low_ready")
        y_ready = s(name + "_y_ready")
        y_free = s(name + "_y_free")
        logits_ready = s(name + "_logits_ready")
        margin_ready = s(name + "_margin_ready")
        share_ready = s(name + "_share_ready")
        route = s(name + "_route_step")
        YS = 2 * (EXPERTS + 1)
        norm = Norm(core, name, tp)
        stats = Stats(core, name)
        ROUTE = 9

        def slot(e):
            return e % RING

        with nc.Block() as block:

            @block.sync
            def _(sp):
                sp.dma_start(rb[:, :], a["router_b"].to_broadcast([P, EXPERTS])).then_inc(rb_loaded, 16)

            @block.tensor
            def _(pe):
                norm.transpose(pe, 0)

                def router(b):
                    pe.wait_ge(norm.xl_ready, b + 1)
                    mm = [(core.xh, rwh), (core.xh, rwl), (core.xl, rwh)]
                    for t in range(TILES):
                        for k in range(KT):
                            for i, (x, w) in enumerate(mm):
                                op = nc.tensor.matmul(logit_ps[:, t, :], x[:, k, t * P:(t + 1) * P], w[:, k, :],
                                                      start=(k == 0 and i == 0), stop=(k == KT - 1 and i == 2))
                    op.then_inc(logits_ready, 1)

                def hidden(b, e):
                    pe.wait_ge(act_ready, b * E + e + 1)
                    for wh, wl, out in ((w1h, w1l, h1), (w3h, w3l, h3)):
                        for k in range(KT):
                            for i, (w, x) in enumerate([(wh, core.xh), (wl, core.xh), (wh, core.xl)]):
                                op = nc.tensor.matmul(out[e % 2][:, :], w[:, e, k, :], x[:, k, :],
                                                      start=(k == 0 and i == 0), stop=(k == KT - 1 and i == 2))
                    op.then_inc(h_ready, 1)

                def output(b, e):
                    pe.wait_ge(low_ready, b * E + e + 3)
                    for half in range(2):
                        if e <= EXPERTS:
                            pe.wait_ge(y_free, b * YS + 2 * e + half + 1)
                        for t in (2 * half, 2 * half + 1):
                            for i, (x, w) in enumerate([(ah, w2h), (ah, w2l), (al, w2h)]):
                                op = nc.tensor.matmul(y[:, t, :], x[:, slot(e), t * P:(t + 1) * P], w[:, e, :],
                                                      start=(e <= EXPERTS and t % 2 == 0 and i == 0),
                                                      stop=(i == 2 and e != EXPERTS), skip_group_check=True)
                        if e != EXPERTS:
                            op.then_inc(y_ready, 1)

                def body(b, before, more):
                    router(b)
                    for e in range(E):
                        hidden(b, e)
                        if e >= LAG:
                            output(b, e - LAG)
                    if more:
                        norm.transpose(pe, b + 1, lambda: pe.wait_ge(route, b * ROUTE + 1))
                    for e in range(E - LAG, E):
                        output(b, e)

                over_sequences(pe, core.batches, body)

            @block.scalar
            def _(act):
                norm.high(act, 0)

                def silu_of(b, e):
                    act.wait_ge(h_ready, b * E + e + 1)
                    nc.scalar.activation(silu[:, e % 2, :], h1[e % 2][:, :], ACT.Silu).then_inc(silu_ready, 1)

                def high_of(b, e):
                    act.wait_ge(act_ready, b * E + e + 3)
                    if e >= RING:
                        act.wait_ge(y_ready, b * YS + 2 * (e - RING + 1))
                    elif before_any(b):
                        act.wait_ge(y_ready, b * YS)
                    nc.scalar.copy(ah[:, slot(e), :], act_f[:, e % 2, :]).then_inc(high_ready, 1)

                def before_any(b):
                    return not (isinstance(b, int) and b == 0)

                def body(b, before, more):
                    for e in range(E):
                        silu_of(b, e)
                        if e >= 1:
                            high_of(b, e - 1)
                        if e == 1:
                            act.wait_ge(margin_ready, b + 1)
                            nc.scalar.activation(share[:, :, :], margin[:, :, :], ACT.Sigmoid).then_inc(share_ready, 1)
                    if more:
                        norm.high(act, b + 1, lambda: act.wait_ge(h_ready, (b + 1) * E))
                    high_of(b, E - 1)

                over_sequences(act, core.batches, body)

            @block.gpsimd
            def _(pool):
                pool.sem_inc(low_ready, 2)
                nc.gpsimd.memset(earlier[:, :, :], 1.0).then_inc(earlier_one, 1)
                pool.wait_ge(earlier_one, 1)
                nc.gpsimd.affine_select(out=earlier[:, :, :], in_=earlier[:, :, :], compare_op=ALU.is_gt, fill=0.0,
                                        base=0, pattern=[[1, EXPERTS], [-1, EXPERTS]],
                                        channel_multiplier=0).then_inc(earlier_ready, 1)

                def body(b, before, more):
                    for e in range(E):
                        pool.wait_ge(high_ready, b * E + e + 1)
                        nc.gpsimd.tensor_tensor(al[:, slot(e), :], act_f[:, e % 2, :], as_f32(ah[:, slot(e), :]),
                                                ALU.subtract).then_inc(low_ready, 1)

                over_sequences(pool, core.batches, body)

            @block.vector
            def _(dve):
                dve.sem_inc(act_ready, 2)
                dve.sem_inc(y_free, 2)
                norm.normalise(dve, 0)
                norm.low(dve, 0)
                dve.wait_ge(rb_loaded, 16)
                dve.wait_ge(earlier_ready, 1)

                def router(b):
                    step = [0]

                    def link(op):
                        step[0] += 1
                        op.then_inc(route, 1)
                        dve.wait_ge(route, b * ROUTE + step[0])

                    dve.wait_ge(logits_ready, b + 1)
                    if not (isinstance(b, int) and b == 0):
                        dve.wait_ge(share_ready, b)
                    link(nc.vector.tensor_tensor(lg[:, :, :], logit_ps, bcast(rb[:, :].unsqueeze(1), [P, TILES, EXPERTS]),
                                                 ALU.add))
                    other = bcast(lg[:, :, :].unsqueeze(2), [P] + big)
                    own = bcast(lg[:, :, :].unsqueeze(3), [P] + big)
                    nc.vector.tensor_tensor(above[:, :, :, :], other, own, ALU.is_gt)
                    link(nc.vector.tensor_tensor(notless[:, :, :, :], other, own, ALU.is_ge))
                    link(nc.vector.tensor_tensor(notless[:, :, :, :], notless[:, :, :, :],
                                                 bcast(earlier[:, :, :].unsqueeze(1), [P] + big), ALU.mult))
                    link(nc.vector.tensor_tensor(above[:, :, :, :], above[:, :, :, :], notless[:, :, :, :], ALU.max))
                    link(nc.vector.tensor_reduce(rank[:, :, :], above[:, :, :, :], AXIS_X, ALU.add))
                    link(nc.vector.tensor_scalar(chosen[:, :, :], rank[:, :, :], float(TOP_K), None, ALU.is_lt))
                    link(nc.vector.tensor_tensor(picked[:, :, :], chosen[:, :, :], lg[:, :, :], ALU.mult))
                    link(nc.vector.tensor_reduce(both[:, :, :], picked[:, :, :], AXIS_X, ALU.add))
                    nc.vector.scalar_tensor_tensor(margin[:, :, :], lg[:, :, :], 2.0,
                                                   bcast(both[:, :, :], [P, TILES, EXPERTS]), ALU.mult,
                                                   ALU.subtract).then_inc(margin_ready, 1)

                def gate(b):
                    dve.wait_ge(share_ready, b + 1)
                    nc.vector.scalar_tensor_tensor(gates[:, :, :], share[:, :, :], 0.5, chosen[:, :, :], ALU.mult,
                                                   ALU.mult).then_inc(route, 1)
                    dve.wait_ge(route, b * ROUTE + ROUTE)

                def product(b, e):
                    dve.wait_ge(silu_ready, b * E + e + 1)
                    dve.wait_ge(low_ready, b * E + e + 1)
                    nc.vector.tensor_tensor(act_f[:, e % 2, :], h3[e % 2][:, :], silu[:, e % 2, :],
                                            ALU.mult).then_inc(act_ready, 1)

                def add(b, e):
                    for half in range(2):
                        dve.wait_ge(y_ready, b * YS + 2 * e + half + 1)
                        if e:
                            dve.wait_ge(y_free, b * YS + 2 * e + half + 1)
                        for t in (2 * half, 2 * half + 1):
                            xt = core.x[:, b * TILES + t, :]
                            gain = gates[:, t, e:e + 1] if e < EXPERTS else 0.5
                            op = nc.vector.scalar_tensor_tensor(xt, y[:, t, :], gain, xt, ALU.mult, ALU.add)
                        op.then_inc(y_free, 1)

                def body(b, before, more):
                    for e in range(E):
                        if e == 2:
                            gate(b)
                        if e > LAG:
                            add(b, e - LAG - 1)
                        product(b, e)
                        if e == 0:
                            router(b)
                        if before and e == 3:
                            stats.take(dve, b - 1, lambda: dve.wait_ge(y_free, b * YS + 2))
                        if more and e == 5:
                            norm.normalise(dve, b + 1)
                    add(b, EXPERTS - 1)
                    if more:
                        norm.low(dve, b + 1)
                    add(b, EXPERTS)

                over_sequences(dve, core.batches, body)
                stats.take(dve, core.batches - 1, lambda: dve.wait_ge(y_free, core.batches * YS + 2))


HEADS = 16
HD = DM // HEADS
GROUPS, GH = 4, 4
STEPS = GROUPS * TILES
BAND, BAND_VAL = 2, 0.1
AHEAD = 6
STACK = 3 * HD


def att_stage(core, a, name):
    nc, s = core.nc, core.sem
    SCALE = HD ** -0.5
    WIDE = P + 2 * BAND
    with ExitStack() as ctx:
        wh, wl = {}, {}
        parts = []
        for n in ("q", "k", "v", "o"):
            wh[n] = core.sbuf(f"W{n}_hi", [P, KT, DM], F32R, ctx)
            wl[n] = core.sbuf(f"W{n}_lo", [P, KT, DM], F32R, ctx)
            parts.append((a[f"w{n}_t"].rearrange("(k p) m -> p k m", p=P), wh[n][:, :, :], wl[n][:, :, :]))
        split_pair(core, name, parts, ctx)
        rstd_block(core, name)

        bq, bk, ocr, bv = (core.sbuf(n, [P, KT], F32, ctx) for n in ("bq_sb", "bk_sb", "ocr_sb", "bv_sb"))
        crow = core.sbuf("out_bias", [P, DM], F32, ctx)
        bvs = core.sbuf("bv_spread", [P, KT, P], F32R, ctx)
        bvl = core.sbuf("bv_spread_lo", [P, KT, P], F32R, ctx)
        band = core.sbuf("band", [P, WIDE], F32, ctx)
        qs = core.sbuf("q_stack", [P, HEADS // 2, TOKENS], F32R, ctx)
        ks = core.sbuf("k_stack", [P, HEADS // 2, TOKENS], F32R, ctx)
        one_f = core.sbuf("one_f", [P, 1], F32, ctx)
        full = core.sbuf("qk_full", [P, KT, TOKENS], F32, ctx)
        qh, ql, kh, kl = (core.sbuf(n, [P, KT, TOKENS], F32R, ctx) for n in ("qh", "ql", "kh", "kl"))
        nm = core.sbuf("neg_max", [P, 2, TILES, GH], F32, ctx)
        nmt = core.sbuf("neg_max_t", [GH, 2, TOKENS], F32R, ctx)
        vaug = core.sbuf("v_ones", [P, TILES, HEADS, 2 * HD], F32, ctx)
        prob = core.sbuf("prob", [P, TILES, GH, TOKENS], F32, ctx)
        ot = core.sbuf("o_t", [P, TOKENS], F32, ctx)
        rec = core.sbuf("sum_rec", [P, TILES, GH, 1], F32, ctx)
        on = core.sbuf("o_norm", [P, TILES, DM], F32, ctx)
        oh, ol = (core.sbuf(n, [P, KT, TOKENS], F32R, ctx) for n in ("oh", "ol"))
        ys = full[:, :, :].rearrange("p k (u d) -> p (k u) d", u=2)

        s1p = [core.psum(f"s1_{i}", [P, TOKENS], ctx) for i in range(2)]
        s2p = [core.psum(f"s2_{i}", [P, TOKENS], ctx) for i in range(2)]
        pvp = core.psum("pv", [P, TOKENS], ctx)
        mp = core.psum("misc", [P, TOKENS], ctx)
        tp = core.psum("tp", [P, KT, TOKENS], ctx)
        tpy = tp[:, :, :].rearrange("p k (u d) -> p (k u) d", u=2)

        turns = s(name + "_turns")
        loaded_b, spread, spread_h, spread_done = s(name + "_biases"), s(name + "_spread"), s(name + "_spread_h"), s(name + "_spread_l")
        crow_ps, crow_ready = s(name + "_crow_ps"), s(name + "_crow")
        pool_step, ks_one, va_one = s(name + "_pool_step"), s(name + "_ks_one"), s(name + "_va_one")
        s1_ready = s(name + "_s1_ready")
        max_done = s(name + "_max_done")
        s2_ready = s(name + "_s2_ready")
        exp_done = s(name + "_exp_done")
        band_done = s(name + "_band_done")
        pv_done = s(name + "_pv_done")
        nm_ready = s(name + "_nm_ready")
        nmt_ready = s(name + "_nmt_ready")
        rowed = [s(f"{name}_max_row{g}") for g in range(GROUPS)]
        loaded = [s(f"{name}_stack{g}") for g in range(GROUPS)]
        ot_ready = s(name + "_ot_ready")
        tr_ready = s(name + "_tr_ready")
        rec_ready = s(name + "_rec_ready")
        on_ready = s(name + "_on_ready")
        q_ps, k_ps, v_ps, o_ps, y_ps = (s(f"{name}_{n}_in_psum") for n in "qkvoy")
        full_ready = s(name + "_full_ready")
        qkh_ready = s(name + "_qk_hi")
        qkl_ready = s(name + "_qk_lo")
        v_ready = s(name + "_v_ready")
        oh_ready, ol_ready = s(name + "_oh_ready"), s(name + "_ol_ready")
        y_ready = s(name + "_y_ready")
        x_done = s(name + "_x_updated")
        norm = Norm(core, name, tp)
        stats = Stats(core, name)
        PER_LOAD = 16 * 6 * GH
        first = lambda b: isinstance(b, int) and b == 0

        def rows(stack, h, slot, n=HD):
            p0 = 64 * (h % 2) + HD * slot
            return stack[p0:p0 + n, h // 2, :]

        with nc.Block() as block:

            @block.sync
            def _(sp):
                for d, n in ((bq, "bq"), (bk, "bk"), (ocr, "ocr_bias"), (bv, "bv")):
                    for k in range(KT):
                        sp.dma_start(d[:, k:k + 1], a[n][:, k * P:(k + 1) * P].rearrange("a p -> p a")).then_inc(loaded_b, 16)
                sp.dma_start(crow[:, :], a["bo"].to_broadcast([P, DM])).then_inc(loaded_b, 16)
                sp.wait_ge(ks_one, 1)

                def load(b, g):
                    sp.wait_ge(qkl_ready, 2 * b + 2)
                    hold(sp, turns)
                    if not first(b):
                        sp.wait_ge(s2_ready, (b - 1) * STEPS * GH + TILES * GH * (g + 1))
                    for h in range(GH * g, GH * g + GH):
                        src = slice(HD * (h % 8), HD * (h % 8) + HD), h // 8
                        for stack, order in ((qs, (qh, qh, ql)), (ks, (kh, kl, kh))):
                            for i, part in enumerate(order):
                                sp.dma_start(as_f32(rows(stack, h, i)), as_f32(part[src[0], src[1], :])).then_inc(loaded[g], 16)

                def max_row(b, g):
                    sp.wait_ge(nmt_ready, b * GROUPS + g + 1)
                    for i in range(GH):
                        sp.dma_start(as_f32(rows(qs, GH * g + i, 3, 1)), as_f32(nmt[i:i + 1, g % 2, :])).then_inc(rowed[g], 16)

                for g in range(GROUPS):
                    load(0, g)
                max_row(0, 0)

                def body(b, before, more):
                    for g in range(GROUPS):
                        if g < GROUPS - 1:
                            max_row(b, g + 1)
                        elif more:
                            max_row(b + 1, 0)
                        if more:
                            load(b + 1, g)

                over_sequences(sp, core.batches, body)

            @block.gpsimd
            def _(pool):
                nc.gpsimd.memset(one_f[:, :], 1.0).then_inc(pool_step, 1)
                nc.gpsimd.memset(band[:, :], 1.0).then_inc(pool_step, 1)
                nc.gpsimd.memset(vaug[:, :, :, :], 1.0).then_inc(va_one, 1)
                nc.gpsimd.memset(as_f32(ks[:, :, :]), 1.0).then_inc(ks_one, 1)
                pool.wait_ge(pool_step, 2)
                factor = math.exp(BAND_VAL)
                nc.gpsimd.memset(band[:, :], factor).then_inc(pool_step, 1)
                pool.wait_ge(pool_step, 3)
                nc.gpsimd.affine_select(out=band[:, :], in_=band[:, :], compare_op=ALU.is_ge, fill=1.0, base=0,
                                        pattern=[[1, WIDE]], channel_multiplier=-1).then_inc(pool_step, 1)
                pool.wait_ge(pool_step, 4)
                nc.gpsimd.affine_select(out=band[:, :], in_=band[:, :], compare_op=ALU.is_ge, fill=1.0, base=2 * BAND,
                                        pattern=[[-1, WIDE]], channel_multiplier=1).then_inc(pool_step, 1)
                pool.wait_ge(pool_step, 5)

                def band_factor(b, st):
                    kt = st % TILES
                    pool.wait_ge(exp_done, (b * STEPS + st) * GH + GH + 2)
                    lo, hi = max(0, kt * P - BAND), min(TOKENS, kt * P + P + BAND)
                    off = lo - (kt * P - BAND)
                    pr = prob[:, kt, :, lo:hi]
                    nc.gpsimd.tensor_tensor(pr, pr, bcast(band[:, off:off + hi - lo].unsqueeze(1), [P, GH, hi - lo]),
                                            ALU.mult).then_inc(band_done, 1)

                def low_part(b, i):
                    pool.wait_ge(qkh_ready, 2 * b + i + 1)
                    hi, lo = ((qh, ql), (kh, kl))[i]
                    nc.gpsimd.tensor_tensor(lo[:, :, :], full[:, :, :], as_f32(hi[:, :, :]), ALU.subtract).then_inc(qkl_ready, 1)

                def add(b):
                    pool.wait_ge(y_ready, b + 2)
                    xs = core.x[:, bass.ds(b * TILES, TILES), :]
                    nc.gpsimd.tensor_tensor(xs, xs, ys, ALU.add).then_inc(x_done, 1)

                low_part(0, 0)
                low_part(0, 1)

                def body(b, before, more):
                    for st in range(STEPS):
                        band_factor(b, st)
                        if more and st in (3, 4):
                            low_part(b + 1, st - 3)
                        if before and st == 7:
                            add(b - 1)

                over_sequences(pool, core.batches, body)
                add(core.batches - 1)

            @block.tensor
            def _(pe):
                pe.wait_ge(spread_done, 2)
                n = 0
                for x, w in ((bvs, "h"), (bvs, "l"), (bvl, "h")):
                    for k in range(KT):
                        op = nc.tensor.matmul(tpy[:, 0, :], x[:, k, :], (wh if w == "h" else wl)["o"][:, k, :],
                                              start=(n == 0), stop=(n == 5))
                        n += 1
                op.then_inc(crow_ps, 1)
                pe.wait_ge(crow_ready, 1)

                def project_t(b, n, done):
                    for m in range(KT):
                        for k in range(KT):
                            for i, (w, x) in enumerate([(wh, core.xh), (wl, core.xh), (wh, core.xl)]):
                                op = nc.tensor.matmul(tp[:, m, :], w[n][:, k, m * P:(m + 1) * P], x[:, k, :],
                                                      start=(k == 0 and i == 0), stop=(k == KT - 1 and i == 2))
                    op.then_inc(done, 1)

                def tokens(out, xh, xl, n, done):
                    for t in range(TILES):
                        for k in range(KT):
                            for i, (x, w) in enumerate([(xh, wh), (xh, wl), (xl, wh)]):
                                op = nc.tensor.matmul(out[:, t, :], x[:, k, t * P:(t + 1) * P], w[n][:, k, :],
                                                      start=(k == 0 and i == 0), stop=(k == KT - 1 and i == 2))
                    op.then_inc(done, 1)

                def q_proj(b):
                    pe.wait_ge(norm.xl_ready, b + 1)
                    project_t(b, "q", q_ps)

                def k_proj(b):
                    pe.wait_ge(full_ready, 2 * b + 1)
                    project_t(b, "k", k_ps)

                def v_proj(b):
                    pe.wait_ge(full_ready, 2 * b + 2)
                    if not first(b):
                        pe.wait_ge(y_ready, b)
                    tokens(tpy, core.xh, core.xl, "v", v_ps)

                def s1(b, st):
                    g, qt = st // TILES, st % TILES
                    if qt == 0:
                        pe.wait_ge(loaded[g], PER_LOAD * b + PER_LOAD)
                    for i in range(GH):
                        yield lambda i=i: s1_unit(b, st, g, qt, i)

                def s1_unit(b, st, g, qt, i):
                    h = GH * g + i
                    pe.wait_ge(max_done, (b * STEPS + st) * GH + i + 1)
                    r = slice(64 * (h % 2), 64 * (h % 2) + STACK)
                    nc.tensor.matmul(s1p[i % 2][:, :], qs[r, h // 2, qt * P:(qt + 1) * P], ks[r, h // 2, :],
                                     start=True, stop=True).then_inc(s1_ready, 1)

                def s2_unit(b, st, i):
                    g, kt = st // TILES, st % TILES
                    h = GH * g + i
                    if kt == 0 and i == 0:
                        pe.wait_ge(rowed[g], 16 * GH * b + 16 * GH)
                    pe.wait_ge(exp_done, (b * STEPS + st) * GH + i + 1)
                    r = slice(64 * (h % 2), 64 * (h % 2) + STACK + 1)
                    nc.tensor.matmul(s2p[i % 2][:, :], ks[r, h // 2, kt * P:(kt + 1) * P], qs[r, h // 2, :],
                                     start=True, stop=True).then_inc(s2_ready, 1)

                def max_t(b, g):
                    pe.wait_ge(max_done, (b * GROUPS + g) * TILES * GH + TILES * GH + 2)
                    if first(b) and g in (1, 2):
                        pe.wait_ge(nmt_ready, g)
                    elif not (first(b) and g == 0):
                        pe.wait_ge(on_ready, b * GROUPS + g - 2)
                    for qt in range(TILES):
                        op = nc.tensor.transpose(mp[0:GH, qt * P:(qt + 1) * P], nm[:, g % 2, qt, :], core.ident[:, :])
                    op.then_inc(nm_ready, 1)

                def pv(b, st):
                    g, kt = st // TILES, st % TILES
                    pe.wait_ge(band_done, b * STEPS + st + 1)
                    if st == 0:
                        pe.wait_ge(v_ready, b + 1)
                    if kt == 0 and not (first(b) and g == 0):
                        pe.wait_ge(ot_ready, b * GROUPS + g)
                    for i in range(GH):
                        op = nc.tensor.matmul(pvp[2 * HD * i:2 * HD * (i + 1), :], vaug[:, kt, GH * g + i, :], prob[:, kt, i, :],
                                              start=(kt == 0), stop=(kt == TILES - 1))
                    op.then_inc(pv_done, 1)

                def out_t(b, g):
                    pe.wait_ge(ot_ready, b * GROUPS + g + 1)
                    if isinstance(b, int) and b == core.batches - 1 and g >= 2:
                        pe.wait_ge(on_ready, b * GROUPS + g)
                    else:
                        pe.wait_ge(nmt_ready, b * GROUPS + g + 3)
                    for qt in range(TILES):
                        op = nc.tensor.transpose(mp[:, qt * P:(qt + 1) * P], ot[:, qt * P:(qt + 1) * P], core.ident[:, :])
                    op.then_inc(tr_ready, 1)

                def o_transpose(b):
                    pe.wait_ge(on_ready, b * GROUPS + GROUPS)
                    if not isinstance(b, int) or b < core.batches - 2:
                        pe.wait_ge(full_ready, 2 * b + 6)
                    elif b == core.batches - 2 or b == 0:
                        pe.wait_ge(v_ready, core.batches)
                    else:
                        pe.wait_ge(y_ready, b + 1)
                    for k in range(KT):
                        for t in range(TILES):
                            op = nc.tensor.transpose(tp[:, k, t * P:(t + 1) * P], on[:, t, k * P:(k + 1) * P], core.ident[:, :])
                    op.then_inc(o_ps, 1)

                def o_project(b):
                    pe.wait_ge(ol_ready, b + 1)
                    tokens(tpy, oh, ol, "o", y_ps)

                norm.transpose(pe, 0)
                q_proj(0)
                k_proj(0)
                for st in range(AHEAD):
                    for unit in s1(0, st):
                        unit()
                    if st == TILES - 1:
                        max_t(0, 0)

                def body(b, before, more):
                    for st in range(STEPS):
                        ahead = st + AHEAD
                        if ahead < STEPS:
                            units = s1(b, ahead)
                        elif more:
                            units = s1(b + 1, ahead - STEPS)
                        else:
                            units = None
                        for i in range(GH):
                            s2_unit(b, st, i)
                            if units is not None:
                                next(units)()
                        if st:
                            pv(b, st - 1)
                        elif before:
                            pv(b - 1, STEPS - 1)
                        if st == 0:
                            v_proj(b)
                        if st % TILES == 1:
                            g = ahead // TILES
                            if g < GROUPS:
                                max_t(b, g)
                            elif more:
                                max_t(b + 1, g - GROUPS)
                        if st % TILES == 2:
                            if st > 2:
                                out_t(b, st // TILES - 1)
                            elif before:
                                out_t(b - 1, GROUPS - 1)
                        if st == 2 and more:
                            norm.transpose(pe, b + 1, lambda: pe.wait_ge(v_ready, b + 1))
                        if st == 3 and more:
                            q_proj(b + 1)
                        if st == 4 and more:
                            k_proj(b + 1)
                        if st == 5 and before:
                            o_transpose(b - 1)
                        if st == 6 and before:
                            o_project(b - 1)

                over_sequences(pe, core.batches, body)
                last = core.batches - 1
                pv(last, STEPS - 1)
                out_t(last, GROUPS - 1)
                o_transpose(last)
                o_project(last)

            @block.scalar
            def _(act):
                act.wait_ge(spread, 1)
                nc.scalar.copy(bvs[:, :, :], full[:, :, 0:P]).then_inc(spread_h, 1)
                norm.high(act, 0)

                def high_part(b, i):
                    act.wait_ge(full_ready, 2 * b + i + 1)
                    if not first(b):
                        for g in range(GROUPS):
                            act.wait_ge(loaded[g], PER_LOAD * b)
                    nc.scalar.copy((qh, kh)[i][:, :, :], full[:, :, :]).then_inc(qkh_ready, 1)

                def exp_unit(b, st, i):
                    kt = st % TILES
                    n = b * STEPS + st
                    act.wait_ge(s2_ready, n * GH + i + 1)
                    if i == 0 and not (first(b) and st < TILES):
                        act.wait_ge(pv_done, n - TILES + 1)
                    nc.scalar.activation(prob[:, kt, i, :], s2p[i % 2][:, :], ACT.Exp).then_inc(exp_done, 1)

                def max_copy(b, g):
                    act.wait_ge(nm_ready, b * GROUPS + g + 1)
                    if not (first(b) and g < 2):
                        if g >= 2:
                            act.wait_ge(rowed[g - 2], 16 * GH * b + 16 * GH)
                        else:
                            act.wait_ge(rowed[g + 2], 16 * GH * b)
                    nc.scalar.copy(nmt[:, g % 2, :], mp[0:GH, :]).then_inc(nmt_ready, 1)

                def v_copy(b):
                    act.wait_ge(v_ps, b + 1)
                    if first(b):
                        act.wait_ge(va_one, 1)
                    else:
                        act.wait_ge(pv_done, b * STEPS)
                    for t in range(TILES):
                        op = nc.scalar.copy(vaug[:, t, :, 0:HD], tpy[:, t, :].rearrange("p (h d) -> p h d", h=HEADS))
                    op.then_inc(v_ready, 1)

                def o_high(b):
                    act.wait_ge(o_ps, b + 1)
                    if not first(b):
                        act.wait_ge(y_ps, b)
                    nc.scalar.copy(oh[:, :, :], tp[:, :, :]).then_inc(oh_ready, 1)

                high_part(0, 0)
                high_part(0, 1)
                max_copy(0, 0)

                def body(b, before, more):
                    for st in range(STEPS):
                        for i in range(GH):
                            exp_unit(b, st, i)
                        if st == 0:
                            v_copy(b)
                        if st % TILES == 1:
                            g = (st + AHEAD) // TILES
                            if g < GROUPS:
                                max_copy(b, g)
                            elif more:
                                max_copy(b + 1, g - GROUPS)
                        if st == 2 and more:
                            norm.high(act, b + 1, lambda: act.wait_ge(v_ps, b + 1))
                        if st in (3, 4) and more:
                            high_part(b + 1, st - 3)
                        if st == 5 and before:
                            o_high(b - 1)

                act.sem_inc(exp_done, 2)
                over_sequences(act, core.batches, body)
                o_high(core.batches - 1)

            @block.vector
            def _(dve):
                dve.wait_ge(loaded_b, 16 * (4 * KT + 1))
                dve.wait_ge(pool_step, 2)
                nc.vector.tensor_tensor(bq[:, :], bq[:, :], ocr[:, :], ALU.add)
                for k in range(KT):
                    op = nc.vector.tensor_scalar(full[:, k, 0:P], core.ones[:, :], bv[:, k:k + 1], None, ALU.mult)
                op.then_inc(spread, 1)
                dve.wait_ge(spread_h, 1)
                nc.vector.tensor_tensor(bvl[:, :, :], full[:, :, 0:P], as_f32(bvs[:, :, :]), ALU.subtract).then_inc(spread_done, 2)
                dve.wait_ge(crow_ps, 1)
                nc.vector.tensor_tensor(crow[:, :], crow[:, :], tpy[:, 0, :], ALU.add).then_inc(crow_ready, 1)
                dve.sem_inc(max_done, 2)
                dve.sem_inc(y_ready, 1)

                def full_part(b, i):
                    dve.wait_ge((q_ps, k_ps)[i], b + 1)
                    if not first(b) or i == 1:
                        dve.wait_ge(qkl_ready, 2 * b + i)
                    for m in range(KT):
                        if i == 0:
                            op = nc.vector.tensor_scalar(full[:, m, :], tp[:, m, :], bq[:, m:m + 1], SCALE, ALU.add, ALU.mult)
                        else:
                            op = nc.vector.tensor_scalar(full[:, m, :], tp[:, m, :], bk[:, m:m + 1], None, ALU.add)
                    op.then_inc(full_ready, 1)

                def max_step(b, st):
                    g, qt = st // TILES, st % TILES
                    for i in range(GH):
                        dve.wait_ge(s1_ready, (b * STEPS + st) * GH + i + 1)
                        nc.vector.tensor_reduce(nm[:, g % 2, qt, i:i + 1], s1p[i % 2][:, :], AXIS_X, ALU.max,
                                                negate=True).then_inc(max_done, 1)

                def ot_copy(b, g):
                    dve.wait_ge(pv_done, b * STEPS + TILES * (g + 1))
                    if not (first(b) and g == 0):
                        dve.wait_ge(tr_ready, b * GROUPS + g)
                    nc.vector.tensor_copy(ot[:, :], pvp[:, :]).then_inc(ot_ready, 1)

                def normalise_out(b, g):
                    dve.wait_ge(tr_ready, b * GROUPS + g + 1)
                    if g == 0 and not first(b):
                        dve.wait_ge(o_ps, b)
                    m4 = mp[:, :].rearrange("p (t h d) -> p t h d", t=TILES, h=GH)
                    nc.vector.reciprocal(rec[:, :, :, :], m4[:, :, :, HD:HD + 1]).then_inc(rec_ready, 1)
                    dve.wait_ge(rec_ready, b * GROUPS + g + 1)
                    out = on[:, :, g * GH * HD:(g + 1) * GH * HD].rearrange("p t (h d) -> p t h d", h=GH)
                    nc.vector.tensor_tensor(out, m4[:, :, :, 0:HD], bcast(rec[:, :, :, :], [P, TILES, GH, HD]),
                                            ALU.mult).then_inc(on_ready, 1)

                def o_low(b):
                    dve.wait_ge(oh_ready, b + 1)
                    nc.vector.tensor_tensor(ol[:, :, :], tp[:, :, :], as_f32(oh[:, :, :]), ALU.subtract).then_inc(ol_ready, 1)

                def y_out(b, split):
                    dve.wait_ge(y_ps, b + 1)
                    dve.wait_ge(qkl_ready, 2 * split)
                    nc.vector.tensor_tensor(ys, tpy, bcast(crow[:, :].unsqueeze(1), [P, TILES, DM]),
                                            ALU.add).then_inc(y_ready, 1)

                norm.normalise(dve, 0)
                norm.low(dve, 0)
                full_part(0, 0)
                full_part(0, 1)
                for st in range(AHEAD):
                    max_step(0, st)

                def body(b, before, more):
                    for st in range(STEPS):
                        if st + AHEAD < STEPS:
                            max_step(b, st + AHEAD)
                        elif more:
                            max_step(b + 1, st + AHEAD - STEPS)
                        if st % TILES == 0:
                            if st:
                                ot_copy(b, st // TILES - 1)
                            elif before:
                                ot_copy(b - 1, GROUPS - 1)
                        if st % TILES == 2:
                            if st > 2:
                                normalise_out(b, st // TILES - 1)
                            elif before:
                                normalise_out(b - 1, GROUPS - 1)
                        if st == 1 and more:
                            norm.normalise(dve, b + 1)
                        if st == 2 and more:
                            norm.low(dve, b + 1)
                        if st in (3, 4) and more:
                            full_part(b + 1, st - 3)
                        if st == 5 and before:
                            o_low(b - 1)
                        if st == 6 and before:
                            y_out(b - 1, b + 2 if more else b + 1)
                        if st == 9 and before:
                            stats.take(dve, b - 1, lambda: dve.wait_ge(x_done, b))

                over_sequences(dve, core.batches, body)
                last = core.batches - 1
                ot_copy(last, GROUPS - 1)
                normalise_out(last, GROUPS - 1)
                o_low(last)
                y_out(last, core.batches)
                stats.take(dve, last, lambda: dve.wait_ge(x_done, core.batches))


GH0 = 2
CHUNK = P
SUB = 32
LEVELS = [0, 1, 2, 4, 8, 16, 32, 64]
SMALL = 6


def level_masks():
    import numpy as np

    m = np.zeros((SMALL, SUB, SUB), np.float32)
    for i, size in enumerate(LEVELS[:SMALL]):
        for s in range(SUB):
            for t in range(SUB):
                if size == 0:
                    m[i, s, t] = s == t
                else:
                    same = s // (2 * size) == t // (2 * size)
                    m[i, s, t] = same and s % (2 * size) < size <= t % (2 * size)
    return np.ascontiguousarray(np.tile(m.transpose(1, 0, 2), (P // SUB, 1, 1)))


def gla_stage(core, a, name):
    nc, s = core.nc, core.sem
    NC = TOKENS // CHUNK
    with ExitStack() as ctx:
        wih, wil = (core.sbuf(n, [P, KT, 3 * DM], F32R, ctx) for n in ("wih", "wil"))
        g1h, g1l = (core.sbuf(n, [P, KT, P], F32R, ctx) for n in ("wg1h", "wg1l"))
        g2h, g2l = (core.sbuf(n, [P, DM], F32R, ctx) for n in ("wg2h", "wg2l"))
        woh, wol = (core.sbuf(n, [P, KT, DM], F32R, ctx) for n in ("gwoh", "gwol"))
        w_in = a["w_in_t"].rearrange("(k p) m -> p k m", p=P)
        split_pair(core, name, [(w_in[:, k, :], wih[:, k, :], wil[:, k, :]) for k in range(KT)]
                   + [(a["w_g1_t"].rearrange("(k p) m -> p k m", p=P), g1h[:, :, :], g1l[:, :, :]),
                      (a["w_g2_t"], g2h[:, :], g2l[:, :])], ctx)

        wo_loaded, wo_scaled, wo_high = s(name + "_wo_loaded"), s(name + "_wo_scaled"), s(name + "_wo_high")
        with ExitStack() as inner:
            wo = core.sbuf("wo_raw", [P, KT, DM], F32, inner)
            lnw = core.sbuf("ln_w", [P, KT], F32, inner)
            with nc.Block() as block:

                @block.sync
                def _(sp):
                    sp.dma_start(wo[:, :, :], a["w_out_t"].rearrange("(k p) m -> p k m", p=P)).then_inc(wo_loaded, 16)
                    for k in range(KT):
                        sp.dma_start(lnw[:, k:k + 1], a["ln_w"][k * P:(k + 1) * P, :]).then_inc(wo_loaded, 16)

                @block.scalar
                def _(act):
                    act.wait_ge(wo_scaled, 1)
                    nc.scalar.copy(woh[:, :, :], wo[:, :, :]).then_inc(wo_high, 1)

                @block.vector
                def _(dve):
                    dve.wait_ge(wo_loaded, 16 * (1 + KT))
                    for k in range(KT):
                        op = nc.vector.tensor_scalar(wo[:, k, :], wo[:, k, :], lnw[:, k:k + 1], None, ALU.mult)
                    op.then_inc(wo_scaled, 1)
                    dve.wait_ge(wo_high, 1)
                    nc.vector.tensor_tensor(wol[:, :, :], wo[:, :, :], as_f32(woh[:, :, :]), ALU.subtract)
        rstd_block(core, name)

        W2 = GH0 * TOKENS
        masks_f = core.sbuf("level_mask_f32", [P, SMALL, SUB], F32, ctx)
        masks = core.sbuf("level_mask", [P, SMALL, SUB], U8, ctx)
        sig = core.sbuf("g_sig", [P, W2], F32, ctx)
        q = core.sbuf("g_q", [P, W2], F32, ctx)
        f = core.sbuf("g_f", [P, W2], F32, ctx)
        qp = core.sbuf("g_qp", [P, W2], F32, ctx)
        ks = core.sbuf("g_ks", [P, W2], F32, ctx)
        tot = core.sbuf("g_tot", [P, W2], F32, ctx)
        v = core.sbuf("g_v", [P, NC, DM], F32, ctx)
        gate = core.sbuf("g_gate", [P, NC, DM], F32, ctx)
        ghi, glo = (core.sbuf(n, [P, TOKENS], F32R, ctx) for n in ("ghi", "glo"))
        diag = core.sbuf("g_diag", [P, GH0, NC, SUB], F32, ctx)
        at = core.sbuf("g_at", [P, GH0, NC, CHUNK], F32, ctx)
        kst = core.sbuf("g_kst", [P, GH0, NC - 1, P], F32, ctx)
        st = core.sbuf("g_state", [P, GH0, NC - 1, P], F32, ctx)
        og = core.sbuf("g_og", [P, NC, DM], F32, ctx)
        o6 = core.sbuf("g_stat6", [P, NC, 6], F32, ctx)
        omv = core.sbuf("g_mv", [P, NC, 2], F32, ctx)
        osd = core.sbuf("g_sd", [P, NC], F32, ctx)
        ors = core.sbuf("g_rstd", [P, NC], F32, ctx)
        oh, ol = (core.sbuf(n, [P, KT, TOKENS], F32R, ctx) for n in ("g_oh", "g_ol"))

        ab = core.psum("g_a", [P, 2, TOKENS], ctx)
        hb = core.psum("g_h", [P, GH0, TOKENS], ctx)
        ob = core.psum("g_o", [P, NC, DM], ctx)
        tp = core.psum("g_tp", [P, KT, TOKENS], ctx)
        aby = ab[:, :, :].rearrange("p k (u d) -> p (k u) d", u=2)
        hbc = hb[:, :, :].rearrange("p h (c t) -> p h c t", c=NC)
        hd = hbc[:, :, :, 0:SUB]

        def total(size):
            if size == 1:
                return f[:, :]
            off = W2 - 2 * W2 // size
            return tot[:, off:off + W2 // size]

        a_free = [s(f"{name}_a{i}_free") for i in range(2)]
        lg_ps, q_ps, v_ps, g1_ps, gate_ps, y_ps = (s(f"{name}_{n}_ps") for n in ("lg", "q", "v", "g1", "gate", "y"))
        f_ready, k_ready, sig_ready, q_ready, qp_ready = (s(f"{name}_{n}") for n in ("f", "k", "sig", "q", "qp"))
        v_ready, ghi_ready, glo_ready, gate_ready = (s(f"{name}_{n}") for n in ("v", "g1hi", "g1lo", "gate"))
        level_done = s(name + "_level_done")
        merged = s(name + "_merged")
        up_q, up_k, up_t = (s(f"{name}_up_{n}") for n in ("q", "k", "t"))
        diag_copied = s(name + "_diag_copied")
        at_ready = s(name + "_at_ready")
        kst_ps, kst_ready = s(name + "_kst_ps"), s(name + "_kst_ready")
        kv_ps, s0_ready, st_ready = s(name + "_kv_ps"), s(name + "_s0_ready"), s(name + "_st_ready")
        o_ready, og_ready, o_stat, o_aggr, o_sd, o_rs, on_ready = (
            s(f"{name}_{n}") for n in ("o_ps", "og", "o_stat", "o_aggr", "o_sd", "o_rs", "on"))
        ot_ps, oh_ready, ol_ready, x_done = (s(f"{name}_{n}") for n in ("ot_ps", "oh", "ol", "x_updated"))
        turns = s(name + "_turns")
        masks_in, zeroed = s(name + "_masks"), s(name + "_zeroed")
        NL = len(LEVELS)
        norm = Norm(core, name, tp)
        stats = Stats(core, name)
        first = lambda b: isinstance(b, int) and b == 0

        with nc.Block() as block:

            @block.sync
            def _(sp):
                sp.dma_start(masks_f[:, :, :], a["level_masks"]).then_inc(masks_in, 16)

            @block.tensor
            def _(pe):
                pairs = lambda wh, wl, xh, xl: [(wh, xh), (wl, xh), (wh, xl)]

                def bank(b, i, use, uses):
                    pe.wait_ge(a_free[i], (b * uses - (0 if first(b) else 1)) + use + 1)

                def channels(b, col, i, use, done):
                    bank(b, i, use, (5, 4)[i])
                    for k in range(KT):
                        for n, (w, x) in enumerate(pairs(wih, wil, core.xh, core.xl)):
                            op = nc.tensor.matmul(ab[:, i, :], w[:, k, col:col + P], x[:, k, :],
                                                  start=(k == 0 and n == 0), stop=(k == KT - 1 and n == 2))
                    op.then_inc(done, 1)

                def v_proj(b, half):
                    bank(b, half, 2, (5, 4)[half])
                    for t in (2 * half, 2 * half + 1):
                        for k in range(KT):
                            for n, (w, x) in enumerate(pairs(wih, wil, core.xh, core.xl)):
                                op = nc.tensor.matmul(aby[:, t, :], x[:, k, t * P:(t + 1) * P], w[:, k, 0:DM],
                                                      start=(k == 0 and n == 0), stop=(k == KT - 1 and n == 2))
                    op.then_inc(v_ps, 1)

                def g1_proj(b):
                    bank(b, 0, 3, 5)
                    for k in range(KT):
                        for n, (w, x) in enumerate(pairs(g1h, g1l, core.xh, core.xl)):
                            op = nc.tensor.matmul(ab[:, 0, :], w[:, k, :], x[:, k, :],
                                                  start=(k == 0 and n == 0), stop=(k == KT - 1 and n == 2))
                    op.then_inc(g1_ps, 1)

                def gate_proj(b):
                    pe.wait_ge(glo_ready, b + 1)
                    if not first(b):
                        pe.wait_ge(og_ready, b)
                    for t in range(NC):
                        for n, (w, x) in enumerate(pairs(g2h, g2l, ghi, glo)):
                            op = nc.tensor.matmul(ob[:, t, :], x[:, t * P:(t + 1) * P], w[:, :],
                                                  start=(n == 0), stop=(n == 2))
                    op.then_inc(gate_ps, 1)

                def level(b, i):
                    size = LEVELS[i]
                    if i == 0:
                        pe.wait_ge(q_ready, 2 * b + 2)
                        pe.wait_ge(k_ready, 2 * b + 2)
                        if not first(b):
                            pe.wait_ge(st_ready, b)
                    elif i == 1:
                        pe.wait_ge(qp_ready, b + 1)
                    else:
                        pe.wait_ge(up_q, 7 * b + i - 1)
                        pe.wait_ge(up_k, 7 * b + i - 1)
                    if 1 <= i <= SMALL:
                        pe.wait_ge(merged, SMALL * b + i)
                    qq = q if i == 0 else qp
                    for h in range(GH0):
                        for c in range(NC):
                            base = h * TOKENS + c * CHUNK
                            if i < SMALL:
                                for j in range(CHUNK // SUB):
                                    r = slice(base + SUB * j, base + SUB * (j + 1))
                                    op = nc.tensor.matmul(hd[SUB * j:SUB * (j + 1), h, c, :], ks[:, r], qq[:, r],
                                                          start=True, stop=True)
                            else:
                                for j in range(0, CHUNK, 2 * size):
                                    op = nc.tensor.matmul(hbc[j:j + size, h, c, j + size:j + 2 * size],
                                                          ks[:, base + j:base + j + size],
                                                          qp[:, base + j + size:base + j + 2 * size],
                                                          start=True, stop=True)
                    op.then_inc(level_done, 1)

                def kst_t(b):
                    pe.wait_ge(up_k, 7 * b + 7)
                    if not first(b):
                        pe.wait_ge(ol_ready, b)
                    else:
                        pe.wait_ge(norm.xl_ready, 1)
                    for h in range(GH0):
                        for c in range(NC - 1):
                            base = h * TOKENS + c * CHUNK
                            op = nc.tensor.transpose(tp[:, h, c * P:(c + 1) * P], ks[:, base:base + P], core.ident[:, :])
                    op.then_inc(kst_ps, 1)

                def kv(b):
                    pe.wait_ge(kst_ready, b + 1)
                    pe.wait_ge(v_ready, 2 * b + 2)
                    pe.wait_ge(at_ready, b + 1)
                    for h in range(GH0):
                        for c in range(NC - 1):
                            op = nc.tensor.matmul(hb[:, h, c * P:(c + 1) * P], kst[:, h, c, :],
                                                  v[:, c, h * P:(h + 1) * P], start=True, stop=True)
                    op.then_inc(kv_ps, 1)

                def output(b):
                    pe.wait_ge(gate_ready, b + 1)
                    pe.wait_ge(diag_copied, b + 1)
                    pe.wait_ge(up_q, 7 * b + 7)
                    for c in range(NC):
                        for h in range(GH0):
                            out = ob[:, c, h * P:(h + 1) * P]
                            nc_last = c == 0
                            op = nc.tensor.matmul(out, at[:, h, c, :], v[:, c, h * P:(h + 1) * P], start=True, stop=nc_last)
                            if c:
                                if c == 1 and h == 0:
                                    pe.wait_ge(st_ready, b + 1)
                                base = h * TOKENS + c * CHUNK
                                op = nc.tensor.matmul(out, qp[:, base:base + P], st[:, h, c - 1, :], start=False, stop=True)
                    op.then_inc(o_ready, 1)

                def o_transpose(b):
                    pe.wait_ge(on_ready, b + 1)
                    pe.wait_ge(norm.xl_ready, b + 2 if not (isinstance(b, int) and b == core.batches - 1) else b + 1)
                    if isinstance(b, int) and b == core.batches - 1:
                        pe.wait_ge(kst_ready, core.batches)
                    for k in range(KT):
                        for t in range(NC):
                            op = nc.tensor.transpose(tp[:, k, t * P:(t + 1) * P], og[:, t, k * P:(k + 1) * P], core.ident[:, :])
                    op.then_inc(ot_ps, 1)

                def o_project(b, free):
                    pe.wait_ge(ol_ready, b + 1)
                    pe.wait_ge(a_free[0], free[0])
                    pe.wait_ge(a_free[1], free[1])
                    for t in range(NC):
                        for k in range(KT):
                            for n, (w, x) in enumerate(pairs(woh, wol, oh, ol)):
                                op = nc.tensor.matmul(aby[:, t, :], x[:, k, t * P:(t + 1) * P], w[:, k, :],
                                                      start=(k == 0 and n == 0), stop=(k == KT - 1 and n == 2))
                    op.then_inc(y_ps, 1)

                norm.transpose(pe, 0)

                def body(b, before, more):
                    pe.wait_ge(norm.xl_ready, b + 1)
                    channels(b, 2 * DM, 0, 0, lg_ps)
                    channels(b, 2 * DM + P, 1, 0, lg_ps)
                    channels(b, DM, 0, 1, q_ps)
                    channels(b, DM + P, 1, 1, q_ps)
                    v_proj(b, 0)
                    level(b, 0)
                    v_proj(b, 1)
                    level(b, 1)
                    g1_proj(b)
                    level(b, 2)
                    level(b, 3)
                    if before:
                        o_transpose(b - 1)
                    level(b, 4)
                    gate_proj(b)
                    level(b, 5)
                    if before:
                        o_project(b - 1, (5 * b + 4, 4 * b + 3))
                    level(b, 6)
                    level(b, 7)
                    kst_t(b)
                    if more:
                        norm.transpose(pe, b + 1, lambda: pe.wait_ge(kst_ready, b + 1))
                    kv(b)
                    output(b)

                over_sequences(pe, core.batches, body)
                last = core.batches - 1
                o_transpose(last)
                o_project(last, (5 * last + 4 + (last > 0), 4 * last + 3 + (last > 0)) if last else (5, 4))

            @block.scalar
            def _(act):
                act.sem_inc(a_free[0], 1)
                act.sem_inc(a_free[1], 1)
                norm.high(act, 0)

                def decay(b, h):
                    act.wait_ge(lg_ps, 2 * b + h + 1)
                    r = slice(h * TOKENS, (h + 1) * TOKENS)
                    if h == 0 and not first(b):
                        act.wait_ge(o_ready, b)
                        act.wait_ge(up_t, 7 * b)
                    nc.scalar.activation(f[:, r], ab[:, h, :], ACT.Sigmoid).then_inc(f_ready, 1)
                    nc.scalar.activation(ks[:, r], ab[:, h, :], ACT.Sigmoid, scale=-1.0).then_inc(k_ready, 1)
                    act.wait_ge(k_ready, 2 * b + h + 1)
                    act.sem_inc(a_free[h], 1)

                def q_sig(b, h):
                    act.wait_ge(q_ps, 2 * b + h + 1)
                    if not first(b):
                        act.wait_ge(q_ready, 2 * b)
                    nc.scalar.activation(sig[:, h * TOKENS:(h + 1) * TOKENS], ab[:, h, :], ACT.Sigmoid).then_inc(sig_ready, 1)

                def v_copy(b, half):
                    act.wait_ge(v_ps, 2 * b + half + 1)
                    nc.scalar.copy(v[:, 2 * half:2 * half + 2, :], aby[:, 2 * half:2 * half + 2, :]).then_inc(v_ready, 1)
                    act.wait_ge(v_ready, 2 * b + half + 1)
                    act.sem_inc(a_free[half], 1)

                def g1_high(b):
                    act.wait_ge(g1_ps, b + 1)
                    if not first(b):
                        act.wait_ge(gate_ps, b)
                    nc.scalar.copy(ghi[:, :], ab[:, 0, :]).then_inc(ghi_ready, 1)

                def gate_sig(b):
                    act.wait_ge(gate_ps, b + 1)
                    nc.scalar.activation(gate[:, :, :], ob[:, :, :], ACT.Sigmoid).then_inc(gate_ready, 1)

                def diag_copy(b):
                    act.wait_ge(merged, SMALL * b + SMALL)
                    if first(b):
                        act.wait_ge(zeroed, 2)
                    else:
                        act.wait_ge(o_ready, b)
                    for j in range(CHUNK // SUB):
                        r = slice(SUB * j, SUB * (j + 1))
                        op = nc.scalar.copy(at[r, :, :, r], diag[r, :, :, :])
                    op.then_inc(diag_copied, 1)

                def at_rest(b):
                    act.wait_ge(level_done, NL * b + NL)
                    if first(b):
                        act.wait_ge(zeroed, 2)
                    else:
                        act.wait_ge(o_ready, b)
                    for r0, n in ((0, 64), (0, 32), (64, 32)):
                        op = nc.scalar.copy(at[r0:r0 + n, :, :, r0 + n:r0 + 2 * n], hbc[r0:r0 + n, :, :, r0 + n:r0 + 2 * n])
                    op.then_inc(at_ready, 1)

                def kst_copy(b):
                    act.wait_ge(kst_ps, b + 1)
                    w = (NC - 1) * P
                    nc.scalar.copy(kst[:, :, :, :].rearrange("p h c d -> p h (c d)"), tp[:, :, 0:w]).then_inc(kst_ready, 1)

                def state0(b):
                    act.wait_ge(kv_ps, b + 1)
                    nc.scalar.copy(st[:, :, 0, :], hb[:, :, 0:P]).then_inc(s0_ready, 1)

                def o_sqrt(b):
                    act.wait_ge(o_aggr, b + 1)
                    nc.scalar.activation(osd[:, :], omv[:, :, 1], ACT.Sqrt, bias=core.eps[:, 0:1]).then_inc(o_sd, 1)

                def o_high(b):
                    act.wait_ge(ot_ps, b + 1)
                    if not first(b):
                        act.wait_ge(y_ps, b)
                    nc.scalar.copy(oh[:, :, :], tp[:, :, :]).then_inc(oh_ready, 1)

                def body(b, before, more):
                    if before:
                        o_sqrt(b - 1)
                    decay(b, 0)
                    decay(b, 1)
                    q_sig(b, 0)
                    q_sig(b, 1)
                    v_copy(b, 0)
                    v_copy(b, 1)
                    g1_high(b)
                    if before:
                        o_high(b - 1)
                    gate_sig(b)
                    diag_copy(b)
                    at_rest(b)
                    kst_copy(b)
                    if more:
                        norm.high(act, b + 1, lambda: act.wait_ge(g1_ps, b + 1))
                    state0(b)

                over_sequences(act, core.batches, body)
                o_sqrt(core.batches - 1)
                o_high(core.batches - 1)

            @block.gpsimd
            def _(pool):
                nc.gpsimd.memset(diag[:, :, :, :], 0.0).then_inc(zeroed, 1)
                nc.gpsimd.memset(at[:, :, :, :], 0.0).then_inc(zeroed, 1)

                def raise_k(b, i):
                    size = LEVELS[i]
                    pool.wait_ge(level_done, NL * b + i + 1)
                    if i == 1:
                        pool.wait_ge(f_ready, 2 * b + 2)
                    else:
                        pool.wait_ge(up_t, 7 * b + i - 1)
                        pool.wait_ge(up_k, 7 * b + i - 1)
                    n = W2 // (2 * size)
                    left = ks[:, :].rearrange("p (n s l) -> p n s l", s=2, l=size)[:, :, 0, :]
                    tt = total(size).rearrange("p (n s) -> p n s", s=2)[:, :, 1:2]
                    nc.gpsimd.tensor_tensor(left, left, bcast(tt, [P, n, size]), ALU.mult).then_inc(up_k, 1)

                def body(b, before, more):
                    for i in range(1, NL):
                        raise_k(b, i)

                over_sequences(pool, core.batches, body)

            @block.vector
            def _(dve):
                norm.normalise(dve, 0)
                norm.low(dve, 0)
                dve.wait_ge(masks_in, 16)
                nc.vector.tensor_copy(masks[:, :, :], masks_f[:, :, :])
                dve.wait_ge(zeroed, 1)

                def gated(b):
                    dve.wait_ge(o_ready, b + 1)
                    if not first(b):
                        dve.wait_ge(ot_ps, b)
                    nc.vector.tensor_tensor(og[:, :, :], ob[:, :, :], gate[:, :, :], ALU.mult).then_inc(og_ready, 1)
                    dve.wait_ge(og_ready, b + 1)
                    if not first(b):
                        dve.wait_ge(o_aggr, b)
                    for t in range(NC):
                        op = nc.vector.bn_stats(o6[:, t, :], og[:, t, :])
                    op.then_inc(o_stat, 1)
                    dve.wait_ge(o_stat, b + 1)
                    hold(dve, turns)
                    for t in range(NC):
                        op = nc.vector.bn_aggr(omv[:, t, :], o6[:, t, :])
                    op.then_inc(o_aggr, 1)

                def o_norm(b):
                    dve.wait_ge(o_sd, b + 1)
                    nc.vector.reciprocal(ors[:, :], osd[:, :]).then_inc(o_rs, 1)
                    dve.wait_ge(o_rs, b + 1)
                    for t in range(NC):
                        op = nc.vector.tensor_scalar(og[:, t, :], og[:, t, :], omv[:, t, 0:1], ors[:, t:t + 1],
                                                     ALU.subtract, ALU.mult)
                    op.then_inc(on_ready, 1)

                def q_silu(b, h):
                    dve.wait_ge(sig_ready, 2 * b + h + 1)
                    r = slice(h * TOKENS, (h + 1) * TOKENS)
                    nc.vector.tensor_tensor(q[:, r], ab[:, h, :], sig[:, r], ALU.mult).then_inc(q_ready, 1)
                    dve.wait_ge(q_ready, 2 * b + h + 1)
                    dve.sem_inc(a_free[h], 1)

                def q_first(b):
                    dve.wait_ge(f_ready, 2 * b + 2)
                    nc.vector.tensor_tensor(qp[:, :], q[:, :], f[:, :], ALU.mult).then_inc(qp_ready, 1)

                def merge(b, i):
                    dve.wait_ge(level_done, NL * b + i + 1)
                    if i == 0 and not first(b):
                        dve.wait_ge(diag_copied, b)
                    if i:
                        dve.wait_ge(merged, SMALL * b + i)
                    hold(dve, turns)
                    nc.vector.copy_predicated(diag[:, :, :, :],
                                              bcast(masks[:, i, :].unsqueeze(1).unsqueeze(1), [P, GH0, NC, SUB]),
                                              hd).then_inc(merged, 1)

                def raise_q(b, i):
                    size = LEVELS[i]
                    dve.wait_ge(level_done, NL * b + i + 1)
                    if i == 1:
                        dve.wait_ge(qp_ready, b + 1)
                    else:
                        dve.wait_ge(up_q, 7 * b + i - 1)
                        dve.wait_ge(up_t, 7 * b + i - 1)
                    n = W2 // (2 * size)
                    right = qp[:, :].rearrange("p (n s l) -> p n s l", s=2, l=size)[:, :, 1, :]
                    tt = total(size).rearrange("p (n s) -> p n s", s=2)
                    nc.vector.tensor_tensor(right, right, bcast(tt[:, :, 0:1], [P, n, size]), ALU.mult).then_inc(up_q, 1)
                    if not first(b):
                        dve.wait_ge(up_k, 7 * b)
                    nc.vector.tensor_tensor(total(2 * size), tt[:, :, 0], tt[:, :, 1], ALU.mult).then_inc(up_t, 1)

                def g1_low(b):
                    dve.wait_ge(ghi_ready, b + 1)
                    nc.vector.tensor_tensor(glo[:, :], ab[:, 0, :], as_f32(ghi[:, :]), ALU.subtract).then_inc(glo_ready, 1)
                    dve.wait_ge(glo_ready, b + 1)
                    dve.sem_inc(a_free[0], 1)

                def states(b):
                    dve.wait_ge(s0_ready, b + 1)
                    dve.wait_ge(up_t, 7 * b + 7)
                    decay = total(CHUNK).rearrange("p (h c) -> p h c", h=GH0)
                    for c in range(1, NC - 1):
                        for h in range(GH0):
                            op = nc.vector.scalar_tensor_tensor(st[:, h, c, :], st[:, h, c - 1, :], decay[:, h, c:c + 1],
                                                                hb[:, h, c * P:(c + 1) * P], ALU.mult, ALU.add)
                        if c < NC - 2:
                            op.then_inc(st_step, 1)
                            dve.wait_ge(st_step, b + 1)
                    op.then_inc(st_ready, 1)

                def o_low(b):
                    dve.wait_ge(oh_ready, b + 1)
                    nc.vector.tensor_tensor(ol[:, :, :], tp[:, :, :], as_f32(oh[:, :, :]), ALU.subtract).then_inc(ol_ready, 1)

                def update(b):
                    dve.wait_ge(y_ps, b + 1)
                    xs = core.x[:, bass.ds(b * TILES, TILES), :]
                    nc.vector.tensor_tensor(xs, xs, aby, ALU.add).then_inc(x_done, 1)
                    dve.wait_ge(x_done, b + 1)
                    dve.sem_inc(a_free[0], 1)
                    dve.sem_inc(a_free[1], 1)
                    stats.take(dve, b, lambda: dve.wait_ge(x_done, b + 1))

                st_step = s(name + "_st_step")

                def body(b, before, more):
                    if before:
                        gated(b - 1)
                    q_silu(b, 0)
                    q_silu(b, 1)
                    q_first(b)
                    if before:
                        o_norm(b - 1)
                    merge(b, 0)
                    merge(b, 1)
                    raise_q(b, 1)
                    g1_low(b)
                    merge(b, 2)
                    raise_q(b, 2)
                    merge(b, 3)
                    raise_q(b, 3)
                    if before:
                        o_low(b - 1)
                    merge(b, 4)
                    raise_q(b, 4)
                    merge(b, 5)
                    raise_q(b, 5)
                    raise_q(b, 6)
                    if before:
                        update(b - 1)
                    raise_q(b, 7)
                    if more:
                        norm.normalise(dve, b + 1)
                        norm.low(dve, b + 1)
                    states(b)

                over_sequences(dve, core.batches, body)
                last = core.batches - 1
                gated(last)
                o_norm(last)
                o_low(last)
                update(last)


def final_store(core, out_dram):
    stored = core.sem("x_stored")
    rows = out_dram.rearrange("(n p) d -> p n d", p=P)
    with core.nc.Block() as block:

        @block.sync
        def _(sp):
            sp.dma_start(rows, core.x[:, :, :]).then_inc(stored, 16)
            sp.wait_ge(stored, 16)


def program(nc, a, out, batches=16, stages=("ffn", "gla", "ffn", "moe", "att", "moe")):
    with ExitStack() as ctx:
        core = Core(nc, ctx, batches)
        constants(core, a["x"])
        core.end_stage()
        weights = None
        with ExitStack() as ffn_ctx:
            for i, stage in enumerate(stages):
                name = f"{stage}{i}"
                if stage == "ffn":
                    if weights is None:
                        weights = FfnWeights(core, ffn_ctx)
                        ffn_weights(core, weights, [a[k] for k in ("w_fc", "w_proj", "u_t", "v", "fast_bt", "gate")], name)
                    ffn_stage(core, weights, name)
                elif stage == "gla":
                    gla_stage(core, a, name)
                else:
                    break
                core.end_stage()
        for i, stage in enumerate(stages):
            name = f"{stage}{i}"
            if stage == "moe":
                moe_stage(core, a, name)
            elif stage == "att":
                att_stage(core, a, name)
            else:
                continue
            core.end_stage()
        final_store(core, out)


def layout(i):
    import numpy as np

    def f32(a):
        return np.ascontiguousarray(np.asarray(a))

    arrays = {
        "x": f32(i["L0_attn_x"]).reshape(-1, 256),
        "w_fc": f32(i["L0_ffn_w_fc"]),
        "w_proj": f32(i["L0_ffn_w_proj"]),
        "u_t": f32(np.asarray(i["L0_ffn_u"]).T),
        "v": f32(i["L0_ffn_v"]),
        "fast_bt": f32(np.asarray(i["L0_ffn_fast_b"]).T),
        "gate": f32(i["L0_ffn_gate"]).reshape(1, 1),
        "w_in_t": f32(np.asarray(i["L0_attn_W_in"]).T),
        "w_out_t": f32(np.asarray(i["L0_attn_W_out"]).T),
        "w_g1_t": f32(np.asarray(i["L0_attn_W_g1"]).T),
        "w_g2_t": f32(np.asarray(i["L0_attn_W_g2"]).T),
        "ln_w": f32(i["L0_attn_ln_w"]).reshape(-1, 1),
        "router_w": f32(i["L1_ffn_router_w"]),
        "router_b": f32(i["L1_ffn_router_b"]).reshape(1, -1),
        "routed_w1": f32(i["L1_ffn_routed_w1"]),
        "routed_w3": f32(i["L1_ffn_routed_w3"]),
        "routed_w2": f32(i["L1_ffn_routed_w2"]),
        "shared_w1": f32(i["L1_ffn_shared_w1"]),
        "shared_w3": f32(i["L1_ffn_shared_w3"]),
        "shared_w2": f32(i["L1_ffn_shared_w2"]),
    }
    arrays["level_masks"] = level_masks()
    for n in ("Wq", "Wk", "Wv", "Wo"):
        arrays[n.lower() + "_t"] = f32(np.asarray(i["L1_attn_" + n]).T)
    for n in ("bq", "bk", "bv", "bo", "ocr_bias"):
        arrays[n] = f32(i["L1_attn_" + n]).reshape(1, -1)
    return arrays


def kernel(**inputs):
    import concourse.bacc as _bacc
    from concourse import mybir as _mybir
    from concourse.bass_utils import run_bass_kernel_spmd as _run

    nc = _bacc.Bacc("TRN2", target_bir_lowering=False, num_devices=1)
    arrays = layout(inputs)
    args = {name: nc.dram_tensor(name, a.shape, _mybir.dt.from_np(a.dtype), kind="ExternalInput").ap()
            for name, a in arrays.items()}
    out = nc.dram_tensor("out", arrays["x"].shape, _mybir.dt.float32, kind="ExternalOutput").ap()
    program(nc, args, out)
    r = _run(nc, [arrays], core_ids=[0])
    return r.results[0]["out"].reshape(16, 512, 256)
```

```python
import math
from contextlib import ExitStack

import concourse.bass as bass
from concourse import mybir

F32 = mybir.dt.float32
F32R = mybir.dt.float32r
U8 = mybir.dt.uint8
ALU = mybir.AluOpType
ACT = mybir.ActivationFunctionType
AXIS_X = mybir.AxisListType.X

P = 128
TOKENS = 512
TILES = TOKENS // P
DM = 256
KT = DM // P
LN_EPS = 1e-5


class Core:

    def __init__(self, nc, ctx, batches):
        self.nc, self.batches = nc, batches
        self.ctx = ctx
        self.made = 0
        self.stage_sems = []
        sb = self.sbuf
        n = batches * TILES
        self.x = sb("x_resident", [P, n, DM])
        self.stat6 = sb("ln_stat6", [P, TILES, 6])
        self.mv4 = sb("ln_mean_var4", [P, TILES, 2])
        self.mv = sb("ln_mean_var", [P, n, 2])
        self.rstd = sb("ln_rstd", [P, n, 1])
        self.eps = sb("ln_eps", [P, 1])
        self.ident = sb("identity", [P, P])
        self.ones = sb("ones", [P, P])
        self.xn = sb("xn", [P, TILES, DM])
        self.xh = sb("xnT_hi", [P, KT, TOKENS], F32R)
        self.xl = sb("xnT_lo", [P, KT, TOKENS], F32R)

    def sbuf(self, name, shape, dt=F32, ctx=None):
        self.made += 1
        return (ctx or self.ctx).enter_context(self.nc.sbuf_tensor(f"{name}_sb{self.made}", shape, dt))

    def psum(self, name, shape, ctx):
        self.made += 1
        return ctx.enter_context(self.nc.psum_tensor(f"{name}_ps{self.made}", shape, F32))

    def sem(self, name):
        self.stage_sems.append(self.nc.alloc_semaphore(name=name))
        return self.stage_sems[-1]

    def end_stage(self):
        self.nc.clear_and_free_semaphores(self.stage_sems)
        self.nc.all_engine_barrier()
        self.stage_sems = []


def hold(engine, turns):
    engine.sem_inc(turns, 1)


def as_f32(ap):
    return ap.bitcast(F32)


def bcast(ap, shape):
    return ap.to_broadcast(shape)


def constants(core, x_dram):
    nc, s = core.nc, core.sem
    n = core.batches * TILES
    ident_zero, const_ready = s("ident_zero"), s("const_ready")
    x_loaded = [s(f"x_loaded{i}") for i in range(4)]
    stats_ready, aggr_ready = s("c_stats_ready"), s("c_aggr_ready")
    x_rows = x_dram.rearrange("(n p) d -> p n d", p=P)
    part = n // 4
    with nc.Block() as block:

        @block.sync
        def _(sp):
            for i in range(4):
                sp.dma_start(core.x[:, i * part:(i + 1) * part, :],
                             x_rows[:, i * part:(i + 1) * part, :]).then_inc(x_loaded[i], 16)

        @block.gpsimd
        def _(pool):
            nc.gpsimd.memset(core.ident[:, :], 0.0).then_inc(ident_zero, 1)
            nc.gpsimd.memset(core.ones[:, :], 1.0).then_inc(const_ready, 1)
            nc.gpsimd.memset(core.eps[:, :], LN_EPS).then_inc(const_ready, 1)
            pool.wait_ge(ident_zero, 1)
            nc.gpsimd.affine_select(out=core.ident[:, :], in_=core.ident[:, :], compare_op=ALU.not_equal,
                                    fill=1.0, base=0, pattern=[[-1, P]],
                                    channel_multiplier=1).then_inc(const_ready, 1)

        @block.vector
        def _(dve):
            for i in range(4):
                dve.wait_ge(x_loaded[i], 16)
                for t in range(i * part, (i + 1) * part):
                    if t:
                        dve.wait_ge(aggr_ready, t)
                    nc.vector.bn_stats(core.stat6[:, 0, :], core.x[:, t, :]).then_inc(stats_ready, 1)
                    dve.wait_ge(stats_ready, t + 1)
                    nc.vector.bn_aggr(core.mv[:, t, :], core.stat6[:, 0, :]).then_inc(aggr_ready, 1)


class Norm:

    def __init__(self, core, name, banks):
        self.c = core
        self.tp = banks
        self.xn_ready = core.sem(name + "_xn_ready")
        self.tp_ready = core.sem(name + "_tp_ready")
        self.xh_ready = core.sem(name + "_xh_ready")
        self.xl_ready = core.sem(name + "_xl_ready")

    def normalise(self, dve, b, tiles=range(TILES)):
        c = self.c
        if not (isinstance(b, int) and b == 0) and tiles[0] == 0:
            dve.wait_ge(self.tp_ready, b)
        for t in tiles:
            n = b * TILES + t
            op = c.nc.vector.tensor_scalar(c.xn[:, t, :], c.x[:, n, :], c.mv[:, n, 0:1], c.rstd[:, n, :],
                                           ALU.subtract, ALU.mult)
        if tiles[-1] == TILES - 1:
            op.then_inc(self.xn_ready, 1)

    def transpose(self, pe, b, tp_free=None, halves=range(KT)):
        c = self.c
        if halves[0] == 0:
            pe.wait_ge(self.xn_ready, b + 1)
            if not (isinstance(b, int) and b == 0):
                pe.wait_ge(self.xl_ready, b)
            if tp_free is not None:
                tp_free()
        for k in halves:
            for t in range(TILES):
                op = c.nc.tensor.transpose(self.tp[:, k, t * P:(t + 1) * P], c.xn[:, t, k * P:(k + 1) * P],
                                           c.ident[:, :])
        if halves[-1] == KT - 1:
            op.then_inc(self.tp_ready, 1)

    def high(self, act, b, readers_done=None, halves=range(KT)):
        c = self.c
        k = slice(halves[0], halves[-1] + 1)
        if k.start == 0:
            act.wait_ge(self.tp_ready, b + 1)
            if readers_done is not None:
                readers_done()
        op = c.nc.scalar.copy(c.xh[:, k, :], self.tp[:, k, :])
        if k.stop == KT:
            op.then_inc(self.xh_ready, 1)

    def low(self, dve, b, halves=range(KT)):
        c = self.c
        k = slice(halves[0], halves[-1] + 1)
        if k.start == 0:
            dve.wait_ge(self.xh_ready, b + 1)
        op = c.nc.vector.tensor_tensor(c.xl[:, k, :], self.tp[:, k, :], as_f32(c.xh[:, k, :]), ALU.subtract)
        if k.stop == KT:
            op.then_inc(self.xl_ready, 1)


def rstd_block(core, name):
    nc = core.nc
    sqrt_ready = core.sem(name + "_sqrt_ready")
    with nc.Block() as block:

        @block.scalar
        def _(act):
            nc.scalar.activation(core.rstd[:, :, 0], core.mv[:, :, 1], ACT.Sqrt,
                                 bias=core.eps[:, 0:1]).then_inc(sqrt_ready, 1)

        @block.vector
        def _(dve):
            dve.wait_ge(sqrt_ready, 1)
            nc.vector.reciprocal(core.rstd[:, :, 0], core.rstd[:, :, 0])


class Stats:

    def __init__(self, core, name):
        self.c = core
        self.stats = core.sem(name + "_bn_stats_ready")
        self.turns = core.sem(name + "_stats_turns")
        self.aggr = core.sem(name + "_bn_aggr_ready")

    def tiles(self, dve, b, updated, tiles=range(TILES)):
        c = self.c
        if tiles[0] == 0:
            updated()
            hold(dve, self.turns)
        for t in tiles:
            op = c.nc.vector.bn_stats(c.stat6[:, t, :], c.x[:, b * TILES + t, :])
        if tiles[-1] == TILES - 1:
            op.then_inc(self.stats, 1)

    def finish(self, dve, b):
        c = self.c
        dve.wait_ge(self.stats, b + 1)
        hold(dve, self.turns)
        for t in range(TILES):
            op = c.nc.vector.bn_aggr(c.mv4[:, t, :], c.stat6[:, t, :])
        op.then_inc(self.aggr, 1)
        dve.wait_ge(self.aggr, 2 * b + 1)
        c.nc.vector.tensor_scalar(c.mv[:, bass.ds(b * TILES, TILES), :], c.mv4[:, :, :], 0.0, None,
                                  ALU.add).then_inc(self.aggr, 1)

    def take(self, dve, b, updated):
        self.tiles(dve, b, updated)
        self.finish(dve, b)


def over_sequences(engine, batches, body):
    body(0, False, batches > 1)
    if batches > 2:
        with engine.Fori(1, batches - 1) as b:
            body(b, True, True)
    if batches > 1:
        body(batches - 1, True, False)


HIDDEN = 1024
JT = HIDDEN // P
RANK = 16
SCALE_MIN = 1e-5


class FfnWeights:
    def __init__(self, core, ctx):
        self.fc_h = core.sbuf("w_fc_hi", [P, KT, HIDDEN], F32R, ctx)
        self.fc_l = core.sbuf("w_fc_lo", [P, KT, HIDDEN], F32R, ctx)
        self.proj = core.sbuf("w_proj_tern", [P, JT, DM], F32R, ctx)
        self.half_scale = core.sbuf("half_scale", [P, DM], F32, ctx)


def ffn_weights(core, w, dram, name):
    nc, s = core.nc, core.sem
    w_fc, w_proj, u_t, v, fast_bt, gate = dram
    loaded = s(name + "_w_loaded")
    dve_step = s(name + "_w_dve_step")
    lowrank_ready = s(name + "_w_lowrank")
    tr_ready, high_ready, low_ready = s(name + "_w_transposed"), s(name + "_w_high"), s(name + "_w_low")
    bv_ready, row_ready, ptr_ready, pcopy = s(name + "_w_bv"), s(name + "_w_row"), s(name + "_w_ptr"), s(name + "_w_pcopy")
    fc_done = s(name + "_w_fc_done")
    proj_done = s(name + "_w_proj_done")
    with ExitStack() as ctx:
        wf = core.sbuf("wf_nat", [P, JT, DM], F32, ctx)
        wp = core.sbuf("wp_nat", [P, KT, HIDDEN], F32, ctx)
        ut = core.sbuf("u_t", [RANK, HIDDEN], F32, ctx)
        vs = core.sbuf("v_sb", [RANK, DM], F32, ctx)
        bt = core.sbuf("fast_bt", [RANK, RANK], F32, ctx)
        gt = core.sbuf("gate_sb", [RANK, 1], F32, ctx)
        bv = core.sbuf("gate_b_v", [RANK, DM], F32, ctx)
        neg = core.sbuf("w_neg", [P, HIDDEN], F32, ctx)
        tern = core.sbuf("w_tern", [P, HIDDEN], F32, ctx)
        NS = JT + KT
        ssum = core.sbuf("s_sum", [P, NS], F32, ctx)
        scale = core.sbuf("s_scale", [P, NS], F32, ctx)
        ph = core.sbuf("s_half", [P, NS], F32, ctx)
        nh = core.sbuf("s_neg_half", [P, NS], F32, ctx)
        weff = core.sbuf("w_eff", [P, JT, DM], F32, ctx)
        ptern = core.sbuf("p_tern", [P, KT, HIDDEN], F32, ctx)
        diag = core.sbuf("s_diag", [P, KT, P], F32, ctx)
        ps = [core.psum(f"wps{i}", [P, 512], ctx) for i in range(4)]
        with nc.Block() as block:

            @block.sync
            def _(sp):
                sp.dma_start(wf[:, :, :], w_fc.rearrange("(j p) d -> p j d", p=P)).then_inc(loaded, 16)
                sp.dma_start(wp[:, :, :], w_proj.rearrange("(k p) h -> p k h", p=P)).then_inc(loaded, 16)
                sp.dma_start(ut[:, :], u_t).then_inc(loaded, 16)
                sp.dma_start(vs[:, :], v).then_inc(loaded, 16)
                sp.dma_start(bt[:, :], fast_bt).then_inc(loaded, 16)
                for r in range(RANK):
                    sp.dma_start(gt[r:r + 1, :], gate).then_inc(loaded, 16)

            ALL = 16 * (5 + RANK)

            @block.tensor
            def _(pe):
                pe.wait_ge(loaded, ALL)
                nc.tensor.matmul(ps[0][0:RANK, 0:DM], bt[:, :], vs[:, :], start=True, stop=True).then_inc(bv_ready, 1)
                for j in range(JT):
                    pe.wait_ge(bv_ready, 2)
                    if j >= 2:
                        pe.wait_ge(fc_done, j - 1)
                    nc.tensor.matmul(ps[2 + j % 2][:, 0:DM], ut[:, j * P:(j + 1) * P], bv[:, :],
                                     start=True, stop=True).then_inc(lowrank_ready, 1)
                n = 0
                for j in range(JT):
                    pe.wait_ge(fc_done, j + 1)
                    if n >= 2:
                        pe.wait_ge(low_ready, n - 1)
                    for k in range(KT):
                        op = nc.tensor.transpose(ps[n % 2][:, k * P:(k + 1) * P], weff[:, j, k * P:(k + 1) * P],
                                                 core.ident[:, :])
                    op.then_inc(tr_ready, 1)
                    n += 1
                pe.wait_ge(proj_done, 1)
                for j in range(JT):
                    if j < 2:
                        pe.wait_ge(low_ready, JT)
                    else:
                        pe.wait_ge(pcopy, j - 1)
                    for k in range(KT):
                        op = nc.tensor.transpose(ps[j % 2][:, k * P:(k + 1) * P], ptern[:, k, j * P:(j + 1) * P],
                                                 core.ident[:, :])
                    op.then_inc(ptr_ready, 1)
                for k in range(KT):
                    op = nc.tensor.matmul(ps[2][:, k * P:(k + 1) * P], core.ones[:, :], diag[:, k, :],
                                          start=True, stop=True)
                op.then_inc(row_ready, 1)

            @block.scalar
            def _(act):
                for j in range(JT):
                    act.wait_ge(tr_ready, j + 1)
                    nc.scalar.copy(w.fc_h[:, :, j * P:(j + 1) * P],
                                   ps[j % 2][:, 0:DM].rearrange("p (k m) -> p k m", k=KT)).then_inc(high_ready, 1)
                for j in range(JT):
                    act.wait_ge(ptr_ready, j + 1)
                    nc.scalar.copy(w.proj[:, j, :], ps[j % 2][:, 0:DM]).then_inc(pcopy, 1)
                act.wait_ge(row_ready, 1)
                nc.scalar.mul(w.half_scale[:, :], ps[2][:, 0:DM], 0.5)

            @block.vector
            def _(dve):
                count = [0]

                def link(op):
                    count[0] += 1
                    op.then_inc(dve_step, 1)
                    dve.wait_ge(dve_step, count[0])

                dve.wait_ge(loaded, ALL)
                dve.wait_ge(bv_ready, 1)
                nc.vector.tensor_scalar(bv[:, :], ps[0][0:RANK, 0:DM], gt[:, 0:1], None, ALU.mult).then_inc(bv_ready, 1)
                blocks = [(wf[:, j, :], DM) for j in range(JT)] + [(wp[:, k, :], HIDDEN) for k in range(KT)]
                for i, (a, n) in enumerate(blocks):
                    link(nc.vector.tensor_reduce(ssum[:, i:i + 1], a, AXIS_X, ALU.add, apply_absolute_value=True))
                link(nc.vector.tensor_scalar(scale[:, 0:JT], ssum[:, 0:JT], 1.0 / DM, SCALE_MIN, ALU.mult, ALU.max))
                link(nc.vector.tensor_scalar(scale[:, JT:NS], ssum[:, JT:NS], 1.0 / HIDDEN, SCALE_MIN, ALU.mult, ALU.max))
                link(nc.vector.tensor_scalar(ph[:, :], scale[:, :], 0.5, None, ALU.mult))
                link(nc.vector.tensor_scalar(nh[:, :], scale[:, :], -0.5, None, ALU.mult))
                for i, (a, n) in enumerate(blocks):
                    link(nc.vector.tensor_scalar(neg[:, 0:n], a, nh[:, i:i + 1], None, ALU.is_lt))
                    out = tern[:, 0:n] if i < JT else ptern[:, i - JT, :]
                    link(nc.vector.scalar_tensor_tensor(out, a, ph[:, i:i + 1], neg[:, 0:n], ALU.is_gt, ALU.subtract))
                    if i < JT:
                        dve.wait_ge(lowrank_ready, i + 1)
                        nc.vector.scalar_tensor_tensor(weff[:, i, :], tern[:, 0:n], scale[:, i:i + 1],
                                                       ps[2 + i % 2][:, 0:DM], ALU.mult, ALU.add).then_inc(fc_done, 1)
                        dve.wait_ge(fc_done, i + 1)
                for k in range(KT):
                    op = nc.vector.tensor_scalar(diag[:, k, :], core.ident[:, :], scale[:, JT + k:JT + k + 1], None,
                                                 ALU.mult)
                op.then_inc(proj_done, 1)
                for j in range(JT):
                    dve.wait_ge(high_ready, j + 1)
                    nc.vector.tensor_tensor(w.fc_l[:, :, j * P:(j + 1) * P],
                                            ps[j % 2][:, 0:DM].rearrange("p (k m) -> p k m", k=KT),
                                            as_f32(w.fc_h[:, :, j * P:(j + 1) * P]), ALU.subtract).then_inc(low_ready, 1)


def ffn_stage(core, w, name):
    nc, s = core.nc, core.sem
    RING, LAG = 6, 4
    rstd_block(core, name)
    h_ready = s(name + "_h_ready")
    r_ready = s(name + "_relu_ready")
    sq_ready = s(name + "_sq_ready")
    high_ready = s(name + "_high_ready")
    low_ready = s(name + "_low_ready")
    proj_done = s(name + "_proj_done")
    y_free = s(name + "_y_free")
    x_done = s(name + "_x_updated")
    with ExitStack() as ctx:
        hp = [core.psum(f"{name}_hp{i}", [P, TOKENS], ctx) for i in range(2)]
        y = core.psum(f"{name}_y", [P, TILES, DM], ctx)
        tp = core.psum(f"{name}_tp", [P, KT, TOKENS], ctx)
        relu = core.sbuf("f_relu", [P, 2, TOKENS], F32, ctx)
        sq = core.sbuf("f_sq", [P, 2, TOKENS], F32, ctx)
        sqh = core.sbuf("f_sq_hi", [P, RING, TOKENS], F32R, ctx)
        sql = core.sbuf("f_sq_lo", [P, RING, TOKENS], F32R, ctx)
        ys = core.sbuf("f_y_scaled", [P, TILES, DM], F32, ctx)
        norm = Norm(core, name, tp)
        stats = Stats(core, name)
        slot = [j % RING for j in range(JT)]
        with nc.Block() as block:

            @block.tensor
            def _(pe):
                norm.transpose(pe, 0)
                pe.sem_inc(proj_done, RING)

                def fc(b, j):
                    if j == 0:
                        pe.wait_ge(norm.xl_ready, b + 1)
                    pe.wait_ge(sq_ready, b * JT + j + 1)
                    mm = [(w.fc_h, core.xh), (w.fc_l, core.xh), (w.fc_h, core.xl)]
                    for k in range(KT):
                        for i, (a, x) in enumerate(mm):
                            op = nc.tensor.matmul(hp[j % 2][:, :], a[:, k, j * P:(j + 1) * P], x[:, k, :],
                                                  start=(k == 0 and i == 0), stop=(k == KT - 1 and i == 2))
                    op.then_inc(h_ready, 1)

                def proj(b, j):
                    pe.wait_ge(low_ready, b * JT + j + 3)
                    if j == 0:
                        pe.wait_ge(y_free, b + 1)
                    for t in range(TILES):
                        for i, r in enumerate((sqh, sql)):
                            op = nc.tensor.matmul(y[:, t, :], r[:, slot[j], t * P:(t + 1) * P], w.proj[:, j, :],
                                                  start=(j == 0 and t % 2 == 0 and i == 0),
                                                  stop=(j == JT - 1 and i == 1), skip_group_check=True)
                    op.then_inc(proj_done, 1)

                def body(b, before, more):
                    for j in range(JT):
                        fc(b, j)
                        if j >= LAG:
                            proj(b, j - LAG)
                    if more:
                        norm.transpose(pe, b + 1)
                    for j in range(JT - LAG, JT):
                        proj(b, j)

                over_sequences(pe, core.batches, body)

            @block.scalar
            def _(act):
                norm.high(act, 0)

                def relu_of(b, j):
                    act.wait_ge(h_ready, b * JT + j + 1)
                    nc.scalar.activation(relu[:, j % 2, :], hp[j % 2][:, :], ACT.Relu).then_inc(r_ready, 1)

                def high_of(b, j):
                    act.wait_ge(sq_ready, b * JT + j + 3)
                    ago = RING if j >= RING else JT - RING if j + RING < JT else JT
                    act.wait_ge(proj_done, b * JT + j - ago + 1 + RING)
                    nc.scalar.copy(sqh[:, slot[j], :], sq[:, j % 2, :]).then_inc(high_ready, 1)

                def body(b, before, more):
                    for j in range(JT):
                        relu_of(b, j)
                        if j >= 1:
                            high_of(b, j - 1)
                    if more:
                        norm.high(act, b + 1, lambda: act.wait_ge(h_ready, (b + 1) * JT))
                    high_of(b, JT - 1)

                over_sequences(act, core.batches, body)

            @block.gpsimd
            def _(pool):
                pool.sem_inc(low_ready, 2)

                def body(b, before, more):
                    for j in range(JT):
                        pool.wait_ge(high_ready, b * JT + j + 1)
                        nc.gpsimd.tensor_tensor(sql[:, slot[j], :], sq[:, j % 2, :], as_f32(sqh[:, slot[j], :]),
                                                ALU.subtract).then_inc(low_ready, 1)
                        if before and j == 1:
                            add(b - 1)

                def add(b):
                    pool.wait_ge(y_free, b + 2)
                    xs = core.x[:, bass.ds(b * TILES, TILES), :]
                    nc.gpsimd.tensor_tensor(xs, xs, ys[:, :, :], ALU.add).then_inc(x_done, 1)

                over_sequences(pool, core.batches, body)
                add(core.batches - 1)

            @block.vector
            def _(dve):
                dve.sem_inc(sq_ready, 2)
                dve.sem_inc(y_free, 1)
                norm.normalise(dve, 0)
                norm.low(dve, 0)

                def square(b, j):
                    dve.wait_ge(r_ready, b * JT + j + 1)
                    dve.wait_ge(low_ready, b * JT + j + 1)
                    nc.vector.tensor_tensor(sq[:, j % 2, :], hp[j % 2][:, :], relu[:, j % 2, :],
                                            ALU.mult).then_inc(sq_ready, 1)

                def scale(b):
                    dve.wait_ge(proj_done, b * JT + JT + RING)
                    nc.vector.tensor_tensor(ys[:, :, :], y[:, :, :],
                                            bcast(w.half_scale[:, :].unsqueeze(1), [P, TILES, DM]),
                                            ALU.mult).then_inc(y_free, 1)

                def body(b, before, more):
                    for j in range(JT):
                        square(b, j)
                        if before and j == 0:
                            scale(b - 1)
                        if before and j == 3:
                            stats.take(dve, b - 1, lambda: dve.wait_ge(x_done, b))
                        if more and j == 5:
                            norm.normalise(dve, b + 1)
                    if more:
                        norm.low(dve, b + 1)

                over_sequences(dve, core.batches, body)
                scale(core.batches - 1)
                stats.take(dve, core.batches - 1, lambda: dve.wait_ge(x_done, core.batches))


EXPERTS, SHARED = 8, 2
ALL_EXPERTS = EXPERTS + SHARED
TOP_K = 2


def split_pair(core, name, parts, ctx):
    nc, s = core.nc, core.sem
    loaded = [s(f"{name}_loaded{i}") for i in range(2)]
    high, low = s(name + "_w_high"), s(name + "_w_low")
    with ExitStack() as inner:
        width = max(h.free_size() for _, h, _ in parts)
        stage = core.sbuf(name + "_stage", [P, 2, width], F32, inner)
        with nc.Block() as block:

            @block.sync
            def _(sp):
                for i, (src, hi, lo) in enumerate(parts):
                    if i >= 2:
                        sp.wait_ge(low, i - 1)
                    n, rows = hi.free_size(), hi.shape[0]
                    shape = src.shape
                    dst = stage[0:rows, i % 2, 0:n]
                    if len(shape) == 3:
                        dst = dst.rearrange("p (a b) -> p a b", a=shape[1])
                    if i >= 2:
                        sp.wait_ge(loaded[i % 2], 16 * (i // 2))
                    sp.dma_start(dst, src).then_inc(loaded[i % 2], 16)

            def view(i, like):
                n, rows = like.free_size(), like.shape[0]
                v = stage[0:rows, i % 2, 0:n]
                if len(like.shape) == 3:
                    v = v.rearrange("p (a b) -> p a b", a=like.shape[1])
                return v

            @block.scalar
            def _(act):
                for i, (src, hi, lo) in enumerate(parts):
                    act.wait_ge(loaded[i % 2], 16 * (i // 2 + 1))
                    nc.scalar.copy(hi, view(i, hi)).then_inc(high, 1)

            @block.vector
            def _(dve):
                for i, (src, hi, lo) in enumerate(parts):
                    dve.wait_ge(high, i + 1)
                    nc.vector.tensor_tensor(lo, view(i, hi), as_f32(hi), ALU.subtract).then_inc(low, 1)


def moe_stage(core, a, name, last=False):
    nc, s = core.nc, core.sem
    E, H = ALL_EXPERTS, P
    RING, LAG = 4, 2
    with ExitStack() as ctx:
        w1h, w1l, w3h, w3l = (core.sbuf(n, [P, E, KT, H], F32R, ctx) for n in ("w1h", "w1l", "w3h", "w3l"))
        w2h, w2l = (core.sbuf(n, [P, E, DM], F32R, ctx) for n in ("w2h", "w2l"))
        rwh, rwl = (core.sbuf(n, [P, KT, EXPERTS], F32R, ctx) for n in ("rwh", "rwl"))
        parts = []
        for e in range(E):
            kind, i = ("routed", e) if e < EXPERTS else ("shared", e - EXPERTS)
            for n, hi, lo in (("w1", w1h, w1l), ("w3", w3h, w3l)):
                parts.append((a[f"{kind}_{n}"][i].rearrange("(k p) h -> p k h", p=P), hi[:, e, :, :], lo[:, e, :, :]))
            parts.append((a[f"{kind}_w2"][i], w2h[:, e, :], w2l[:, e, :]))
        parts.append((a["router_w"].rearrange("(k p) e -> p k e", p=P), rwh[:, :, :], rwl[:, :, :]))
        split_pair(core, name, parts, ctx)
        rstd_block(core, name)

        rb = core.sbuf("router_b", [P, EXPERTS], F32, ctx)
        earlier = core.sbuf("earlier", [P, EXPERTS, EXPERTS], F32, ctx)
        rb_loaded, earlier_one, earlier_ready = s(name + "_rb_loaded"), s(name + "_e_one"), s(name + "_earlier")
        lg = core.sbuf("logits", [P, TILES, EXPERTS], F32, ctx)
        big = [TILES, EXPERTS, EXPERTS]
        above, notless = core.sbuf("above", [P] + big, F32, ctx), core.sbuf("notless", [P] + big, F32, ctx)
        rank = core.sbuf("rank", [P, TILES, EXPERTS], F32, ctx)
        chosen = core.sbuf("chosen", [P, TILES, EXPERTS], F32, ctx)
        picked = core.sbuf("picked", [P, TILES, EXPERTS], F32, ctx)
        both = core.sbuf("both", [P, TILES, 1], F32, ctx)
        margin = core.sbuf("margin", [P, TILES, EXPERTS], F32, ctx)
        share = core.sbuf("share", [P, TILES, EXPERTS], F32, ctx)
        gates = core.sbuf("gates", [P, TILES, EXPERTS], F32, ctx)
        silu = core.sbuf("m_silu", [P, 2, TOKENS], F32, ctx)
        act_f = core.sbuf("m_act", [P, 2, TOKENS], F32, ctx)
        ah = core.sbuf("m_act_hi", [P, RING, TOKENS], F32R, ctx)
        al = core.sbuf("m_act_lo", [P, RING, TOKENS], F32R, ctx)
        h1 = [core.psum(f"{name}_h1{i}", [P, TOKENS], ctx) for i in range(2)]
        h3 = [core.psum(f"{name}_h3{i}", [P, TOKENS], ctx) for i in range(2)]
        y = core.psum(f"{name}_y", [P, TILES, DM], ctx)
        tp = core.psum(f"{name}_tp", [P, KT, TOKENS], ctx)
        logit_ps = tp[:, 0, 0:TILES * EXPERTS].rearrange("p (t e) -> p t e", t=TILES)

        h_ready = s(name + "_h_ready")
        silu_ready = s(name + "_silu_ready")
        act_ready = s(name + "_act_ready")
        high_ready = s(name + "_high_ready")
        low_ready = s(name + "_low_ready")
        y_ready = s(name + "_y_ready")
        y_free = s(name + "_y_free")
        logits_ready = s(name + "_logits_ready")
        margin_ready = s(name + "_margin_ready")
        share_ready = s(name + "_share_ready")
        route = s(name + "_route_step")
        YS = 2 * (EXPERTS + 1)
        norm = Norm(core, name, tp)
        stats = Stats(core, name)
        ROUTE = 9

        def slot(e):
            return e % RING

        with nc.Block() as block:

            @block.sync
            def _(sp):
                sp.dma_start(rb[:, :], a["router_b"].to_broadcast([P, EXPERTS])).then_inc(rb_loaded, 16)

            @block.tensor
            def _(pe):
                norm.transpose(pe, 0)

                def router(b):
                    pe.wait_ge(norm.xl_ready, b + 1)
                    mm = [(core.xh, rwh), (core.xh, rwl), (core.xl, rwh)]
                    for t in range(TILES):
                        for k in range(KT):
                            for i, (x, w) in enumerate(mm):
                                op = nc.tensor.matmul(logit_ps[:, t, :], x[:, k, t * P:(t + 1) * P], w[:, k, :],
                                                      start=(k == 0 and i == 0), stop=(k == KT - 1 and i == 2))
                    op.then_inc(logits_ready, 1)

                def hidden(b, e):
                    pe.wait_ge(act_ready, b * E + e + 1)
                    for wh, wl, out in ((w1h, w1l, h1), (w3h, w3l, h3)):
                        for k in range(KT):
                            for i, (w, x) in enumerate([(wh, core.xh), (wl, core.xh), (wh, core.xl)]):
                                op = nc.tensor.matmul(out[e % 2][:, :], w[:, e, k, :], x[:, k, :],
                                                      start=(k == 0 and i == 0), stop=(k == KT - 1 and i == 2))
                    op.then_inc(h_ready, 1)

                def output(b, e):
                    pe.wait_ge(low_ready, b * E + e + 3)
                    for half in range(2):
                        if e <= EXPERTS:
                            pe.wait_ge(y_free, b * YS + 2 * e + half + 1)
                        for t in (2 * half, 2 * half + 1):
                            for i, (x, w) in enumerate([(ah, w2h), (ah, w2l), (al, w2h)]):
                                op = nc.tensor.matmul(y[:, t, :], x[:, slot(e), t * P:(t + 1) * P], w[:, e, :],
                                                      start=(e <= EXPERTS and t % 2 == 0 and i == 0),
                                                      stop=(i == 2 and e != EXPERTS), skip_group_check=True)
                        if e != EXPERTS:
                            op.then_inc(y_ready, 1)

                def body(b, before, more):
                    router(b)
                    for e in range(E):
                        hidden(b, e)
                        if e >= LAG:
                            output(b, e - LAG)
                    if more:
                        norm.transpose(pe, b + 1, lambda: pe.wait_ge(route, b * ROUTE + 1))
                    for e in range(E - LAG, E):
                        output(b, e)

                over_sequences(pe, core.batches, body)

            @block.scalar
            def _(act):
                norm.high(act, 0)

                def silu_of(b, e):
                    act.wait_ge(h_ready, b * E + e + 1)
                    nc.scalar.activation(silu[:, e % 2, :], h1[e % 2][:, :], ACT.Silu).then_inc(silu_ready, 1)

                def high_of(b, e):
                    act.wait_ge(act_ready, b * E + e + 3)
                    if e >= RING:
                        act.wait_ge(y_ready, b * YS + 2 * (e - RING + 1))
                    elif before_any(b):
                        act.wait_ge(y_ready, b * YS)
                    nc.scalar.copy(ah[:, slot(e), :], act_f[:, e % 2, :]).then_inc(high_ready, 1)

                def before_any(b):
                    return not (isinstance(b, int) and b == 0)

                def body(b, before, more):
                    for e in range(E):
                        silu_of(b, e)
                        if e >= 1:
                            high_of(b, e - 1)
                        if e == 1:
                            act.wait_ge(margin_ready, b + 1)
                            nc.scalar.activation(share[:, :, :], margin[:, :, :], ACT.Sigmoid).then_inc(share_ready, 1)
                    if more:
                        norm.high(act, b + 1, lambda: act.wait_ge(h_ready, (b + 1) * E))
                    high_of(b, E - 1)

                over_sequences(act, core.batches, body)

            @block.gpsimd
            def _(pool):
                pool.sem_inc(low_ready, 2)
                nc.gpsimd.memset(earlier[:, :, :], 1.0).then_inc(earlier_one, 1)
                pool.wait_ge(earlier_one, 1)
                nc.gpsimd.affine_select(out=earlier[:, :, :], in_=earlier[:, :, :], compare_op=ALU.is_gt, fill=0.0,
                                        base=0, pattern=[[1, EXPERTS], [-1, EXPERTS]],
                                        channel_multiplier=0).then_inc(earlier_ready, 1)

                def body(b, before, more):
                    for e in range(E):
                        pool.wait_ge(high_ready, b * E + e + 1)
                        nc.gpsimd.tensor_tensor(al[:, slot(e), :], act_f[:, e % 2, :], as_f32(ah[:, slot(e), :]),
                                                ALU.subtract).then_inc(low_ready, 1)

                over_sequences(pool, core.batches, body)

            @block.vector
            def _(dve):
                dve.sem_inc(act_ready, 2)
                dve.sem_inc(y_free, 2)
                norm.normalise(dve, 0)
                norm.low(dve, 0)
                dve.wait_ge(rb_loaded, 16)
                dve.wait_ge(earlier_ready, 1)

                def router(b):
                    step = [0]

                    def link(op):
                        step[0] += 1
                        op.then_inc(route, 1)
                        dve.wait_ge(route, b * ROUTE + step[0])

                    dve.wait_ge(logits_ready, b + 1)
                    if not (isinstance(b, int) and b == 0):
                        dve.wait_ge(share_ready, b)
                    link(nc.vector.tensor_tensor(lg[:, :, :], logit_ps, bcast(rb[:, :].unsqueeze(1), [P, TILES, EXPERTS]),
                                                 ALU.add))
                    other = bcast(lg[:, :, :].unsqueeze(2), [P] + big)
                    own = bcast(lg[:, :, :].unsqueeze(3), [P] + big)
                    nc.vector.tensor_tensor(above[:, :, :, :], other, own, ALU.is_gt)
                    link(nc.vector.tensor_tensor(notless[:, :, :, :], other, own, ALU.is_ge))
                    link(nc.vector.tensor_tensor(notless[:, :, :, :], notless[:, :, :, :],
                                                 bcast(earlier[:, :, :].unsqueeze(1), [P] + big), ALU.mult))
                    link(nc.vector.tensor_tensor(above[:, :, :, :], above[:, :, :, :], notless[:, :, :, :], ALU.max))
                    link(nc.vector.tensor_reduce(rank[:, :, :], above[:, :, :, :], AXIS_X, ALU.add))
                    link(nc.vector.tensor_scalar(chosen[:, :, :], rank[:, :, :], float(TOP_K), None, ALU.is_lt))
                    link(nc.vector.tensor_tensor(picked[:, :, :], chosen[:, :, :], lg[:, :, :], ALU.mult))
                    link(nc.vector.tensor_reduce(both[:, :, :], picked[:, :, :], AXIS_X, ALU.add))
                    nc.vector.scalar_tensor_tensor(margin[:, :, :], lg[:, :, :], 2.0,
                                                   bcast(both[:, :, :], [P, TILES, EXPERTS]), ALU.mult,
                                                   ALU.subtract).then_inc(margin_ready, 1)

                def gate(b):
                    dve.wait_ge(share_ready, b + 1)
                    nc.vector.scalar_tensor_tensor(gates[:, :, :], share[:, :, :], 0.5, chosen[:, :, :], ALU.mult,
                                                   ALU.mult).then_inc(route, 1)
                    dve.wait_ge(route, b * ROUTE + ROUTE)

                def product(b, e):
                    dve.wait_ge(silu_ready, b * E + e + 1)
                    dve.wait_ge(low_ready, b * E + e + 1)
                    nc.vector.tensor_tensor(act_f[:, e % 2, :], h3[e % 2][:, :], silu[:, e % 2, :],
                                            ALU.mult).then_inc(act_ready, 1)

                def add(b, e):
                    for half in range(2):
                        dve.wait_ge(y_ready, b * YS + 2 * e + half + 1)
                        if e:
                            dve.wait_ge(y_free, b * YS + 2 * e + half + 1)
                        for t in (2 * half, 2 * half + 1):
                            xt = core.x[:, b * TILES + t, :]
                            gain = gates[:, t, e:e + 1] if e < EXPERTS else 0.5
                            op = nc.vector.scalar_tensor_tensor(xt, y[:, t, :], gain, xt, ALU.mult, ALU.add)
                        op.then_inc(y_free, 1)

                def body(b, before, more):
                    for e in range(E):
                        if e == 2:
                            gate(b)
                        if e > LAG:
                            add(b, e - LAG - 1)
                        product(b, e)
                        if e == 0:
                            router(b)
                        if before and e == 3:
                            stats.take(dve, b - 1, lambda: dve.wait_ge(y_free, b * YS + 2))
                        if more and e == 5:
                            norm.normalise(dve, b + 1)
                    add(b, EXPERTS - 1)
                    if more:
                        norm.low(dve, b + 1)
                    add(b, EXPERTS)

                over_sequences(dve, core.batches, body)
                stats.take(dve, core.batches - 1, lambda: dve.wait_ge(y_free, core.batches * YS + 2))


HEADS = 16
HD = DM // HEADS
GROUPS, GH = 4, 4
STEPS = GROUPS * TILES
BAND, BAND_VAL = 2, 0.1
XT_AT = [(1, 2), (2, 1)]
QK_AT = [[(3, 2), (4, 0), (4, 1), (4, 2)], [(8, 0), (8, 1), (8, 2), (9, 0)]]
OT_AT = [(6, 1), (6, 2)]
Y_AT = [(10, 0), (10, 1), (10, 2), (11, 0)]
V_AT = [(12, 1), (12, 2), (13, 0), (13, 2)]
AHEAD = 7
STACK = 3 * HD


def att_stage(core, a, name):
    nc, s = core.nc, core.sem
    SCALE = HD ** -0.5
    WIDE = P + 2 * BAND
    with ExitStack() as ctx:
        wh, wl = {}, {}
        parts = []
        for n in ("q", "k", "v", "o"):
            wh[n] = core.sbuf(f"W{n}_hi", [P, KT, DM], F32R, ctx)
            wl[n] = core.sbuf(f"W{n}_lo", [P, KT, DM], F32R, ctx)
            parts.append((a[f"w{n}_t"].rearrange("(k p) m -> p k m", p=P), wh[n][:, :, :], wl[n][:, :, :]))
        split_pair(core, name, parts, ctx)
        rstd_block(core, name)

        bq, bk, ocr, bv = (core.sbuf(n, [P, KT], F32, ctx) for n in ("bq_sb", "bk_sb", "ocr_sb", "bv_sb"))
        crow = core.sbuf("out_bias", [P, DM], F32, ctx)
        bvs = core.sbuf("bv_spread", [P, KT, P], F32R, ctx)
        bvl = core.sbuf("bv_spread_lo", [P, KT, P], F32R, ctx)
        band = core.sbuf("band", [P, WIDE], F32, ctx)
        qs = core.sbuf("q_stack", [P, KT, GH, TOKENS], F32R, ctx)
        ks = core.sbuf("k_stack", [P, KT, GH, TOKENS], F32R, ctx)
        one_f = core.sbuf("one_f", [P, 1], F32, ctx)
        full = core.sbuf("qk_full", [P, 2, TOKENS], F32, ctx)
        qkh, qkl = (core.sbuf(n, [P, KT, 2, TOKENS], F32R, ctx) for n in ("qk_hi", "qk_lo"))
        scratch = nc.dram_tensor("qk_scratch", (KT, 2, 3, HD, HEADS // KT, TOKENS), F32).ap()
        nm = core.sbuf("neg_max", [P, 2, TILES, GH], F32, ctx)
        nmt = core.sbuf("neg_max_t", [GH, 2, TOKENS], F32R, ctx)
        vaug = core.sbuf("v_ones", [P, TILES, HEADS, 2 * HD], F32, ctx)
        prob = core.sbuf("prob", [P, TILES, GH, TOKENS], F32, ctx)
        ot = core.sbuf("o_t", [P, TOKENS], F32, ctx)
        rec = core.sbuf("sum_rec", [P, TILES, GH, 1], F32, ctx)
        on = core.sbuf("o_norm", [P, TILES, DM], F32, ctx)
        oh, ol = (core.sbuf(n, [P, KT, TOKENS], F32R, ctx) for n in ("oh", "ol"))
        ys = full[:, :, :].rearrange("p k (u d) -> p (k u) d", u=2)

        s1p = [core.psum(f"s1_{i}", [P, TOKENS], ctx) for i in range(2)]
        s2p = [core.psum(f"s2_{i}", [P, TOKENS], ctx) for i in range(2)]
        pvp = core.psum("pv", [P, TOKENS], ctx)
        mp = core.psum("misc", [P, TOKENS], ctx)
        tp = core.psum("tp", [P, KT, TOKENS], ctx)
        tpy = tp[:, :, :].rearrange("p k (u d) -> p (k u) d", u=2)

        turns = s(name + "_turns")
        loaded_b, spread, spread_h, spread_done = s(name + "_biases"), s(name + "_spread"), s(name + "_spread_h"), s(name + "_spread_l")
        crow_ps, crow_ready = s(name + "_crow_ps"), s(name + "_crow")
        pool_step, ks_one, va_one = s(name + "_pool_step"), s(name + "_ks_one"), s(name + "_va_one")
        s1_ready = s(name + "_s1_ready")
        max_done = s(name + "_max_done")
        s2_ready = s(name + "_s2_ready")
        exp_done = s(name + "_exp_done")
        band_done = s(name + "_band_done")
        pv_done = s(name + "_pv_done")
        nm_ready = s(name + "_nm_ready")
        nmt_ready = s(name + "_nmt_ready")
        rowed = [s(f"{name}_max_row{g}") for g in range(GROUPS)]
        loaded = [s(f"{name}_stack{g}") for g in range(GROUPS)]
        written = [s(f"{name}_written{m}") for m in range(KT)]
        ot_ready = s(name + "_ot_ready")
        tr_ready = s(name + "_tr_ready")
        rec_ready = s(name + "_rec_ready")
        on_ready = s(name + "_on_ready")
        qk_ps = s(name + "_qk_in_psum")
        v_ps, o_ps, y_ps = (s(f"{name}_{n}_in_psum") for n in "voy")
        full_ready = s(name + "_full_ready")
        qkh_ready = s(name + "_qk_hi")
        qkl_ready = s(name + "_qk_lo")
        v_ready = s(name + "_v_ready")
        oh_ready, ol_ready = s(name + "_oh_ready"), s(name + "_ol_ready")
        y_ready = s(name + "_y_ready")
        x_done = s(name + "_x_updated")
        norm = Norm(core, name, tp)
        stats = Stats(core, name)
        PER_LOAD, PER_WRITE = 16 * 2, 16 * 6
        first = lambda b: isinstance(b, int) and b == 0

        def stack_rows(g, n):
            return slice(64 * (g % 2), 64 * (g % 2) + n)

        with nc.Block() as block:

            @block.sync
            def _(sp):
                for d, n in ((bq, "bq"), (bk, "bk"), (ocr, "ocr_bias"), (bv, "bv")):
                    for k in range(KT):
                        sp.dma_start(d[:, k:k + 1], a[n][:, k * P:(k + 1) * P].rearrange("a p -> p a")).then_inc(loaded_b, 16)
                sp.dma_start(crow[:, :], a["bo"].to_broadcast([P, DM])).then_inc(loaded_b, 16)
                sp.wait_ge(ks_one, 1)

                def write(b, m, part, ready):
                    sp.wait_ge(ready, KT * b + m + 1)
                    hold(sp, turns)
                    if part == 0 and not first(b):
                        for g in (2 * m, 2 * m + 1):
                            sp.wait_ge(loaded[g], PER_LOAD * b)
                    src = (qkh, qkl)[part]
                    for x, slots in enumerate((((0, 1), (0, 2)), ((2,), (1,)))[part]):
                        for slot in slots:
                            sp.dma_start(scratch[m, x, slot].rearrange("r h c -> h r c"),
                                         as_f32(src[:, m, x, :])).then_inc(written[m], 16)

                def load(b, g):
                    m = g // 2
                    sp.wait_ge(written[m], PER_WRITE * b + PER_WRITE)
                    hold(sp, turns)
                    if not first(b):
                        sp.wait_ge(s2_ready, (b - 1) * STEPS * GH + TILES * GH * (g + 1))
                    heads = slice(GH * (g % 2), GH * (g % 2) + GH)
                    for x, stack in enumerate((qs, ks)):
                        sp.dma_start(as_f32(stack[stack_rows(g, STACK), m, :, :]),
                                     scratch[m, x, :, :, heads, :]).then_inc(loaded[g], 16)

                def max_row(b, g):
                    sp.wait_ge(nmt_ready, b * GROUPS + g + 1)
                    row = 64 * (g % 2) + STACK
                    sp.dma_start(as_f32(qs[row:row + 1, g // 2, :, :]), as_f32(nmt[:, g % 2, :])).then_inc(rowed[g], 16)

                for m in range(KT):
                    write(0, m, 0, qkh_ready)
                    write(0, m, 1, qkl_ready)
                    load(0, 2 * m)
                    load(0, 2 * m + 1)
                max_row(0, 0)

                def body(b, before, more):
                    max_row(b, 1)
                    if more:
                        write(b + 1, 0, 0, qkh_ready)
                        write(b + 1, 0, 1, qkl_ready)
                    max_row(b, 2)
                    if more:
                        load(b + 1, 0)
                        load(b + 1, 1)
                        write(b + 1, 1, 0, qkh_ready)
                        write(b + 1, 1, 1, qkl_ready)
                    max_row(b, 3)
                    if more:
                        load(b + 1, 2)
                        max_row(b + 1, 0)
                        load(b + 1, 3)

                over_sequences(sp, core.batches, body)

            @block.gpsimd
            def _(pool):
                nc.gpsimd.memset(one_f[:, :], 1.0).then_inc(pool_step, 1)
                nc.gpsimd.memset(band[:, :], 1.0).then_inc(pool_step, 1)
                nc.gpsimd.memset(vaug[:, :, :, :], 1.0).then_inc(va_one, 1)
                nc.gpsimd.memset(as_f32(ks[:, :, :]), 1.0).then_inc(ks_one, 1)
                pool.wait_ge(pool_step, 2)
                factor = math.exp(BAND_VAL)
                nc.gpsimd.memset(band[:, :], factor).then_inc(pool_step, 1)
                pool.wait_ge(pool_step, 3)
                nc.gpsimd.affine_select(out=band[:, :], in_=band[:, :], compare_op=ALU.is_ge, fill=1.0, base=0,
                                        pattern=[[1, WIDE]], channel_multiplier=-1).then_inc(pool_step, 1)
                pool.wait_ge(pool_step, 4)
                nc.gpsimd.affine_select(out=band[:, :], in_=band[:, :], compare_op=ALU.is_ge, fill=1.0, base=2 * BAND,
                                        pattern=[[-1, WIDE]], channel_multiplier=1).then_inc(pool_step, 1)
                pool.wait_ge(pool_step, 5)

                def band_factor(b, st):
                    kt = st % TILES
                    pool.wait_ge(exp_done, (b * STEPS + st) * GH + GH + 2)
                    lo, hi = max(0, kt * P - BAND), min(TOKENS, kt * P + P + BAND)
                    off = lo - (kt * P - BAND)
                    pr = prob[:, kt, :, lo:hi]
                    nc.gpsimd.tensor_tensor(pr, pr, bcast(band[:, off:off + hi - lo].unsqueeze(1), [P, GH, hi - lo]),
                                            ALU.mult).then_inc(band_done, 1)

                def low_part(b, m):
                    pool.wait_ge(qkh_ready, KT * b + m + 1)
                    if not first(b):
                        pool.wait_ge(written[m], PER_WRITE * b)
                    nc.gpsimd.tensor_tensor(qkl[:, m, :, :], full[:, :, :], as_f32(qkh[:, m, :, :]),
                                            ALU.subtract).then_inc(qkl_ready, 1)

                def add(b):
                    pool.wait_ge(y_ready, b + 2)
                    xs = core.x[:, bass.ds(b * TILES, TILES), :]
                    nc.gpsimd.tensor_tensor(xs, xs, ys, ALU.add).then_inc(x_done, 1)

                low_part(0, 0)
                low_part(0, 1)

                def body(b, before, more):
                    for st in range(STEPS):
                        band_factor(b, st)
                        if more and st in (4, 9):
                            low_part(b + 1, st // 8)
                        if before and st == 12:
                            add(b - 1)

                over_sequences(pool, core.batches, body)
                add(core.batches - 1)

            @block.tensor
            def _(pe):
                pe.wait_ge(spread_done, 2)
                n = 0
                for x, w in ((bvs, "h"), (bvs, "l"), (bvl, "h")):
                    for k in range(KT):
                        op = nc.tensor.matmul(tpy[:, 0, :], x[:, k, :], (wh if w == "h" else wl)["o"][:, k, :],
                                              start=(n == 0), stop=(n == 5))
                        n += 1
                op.then_inc(crow_ps, 1)
                pe.wait_ge(crow_ready, 1)

                def qk_proj(b, m, parts=range(4), after_o=False):
                    if parts[0] == 0 and m == 0:
                        pe.wait_ge(norm.xl_ready, b + 1)
                    elif parts[0] == 0:
                        pe.wait_ge(full_ready, KT * b + m)
                        if after_o:
                            pe.wait_ge(ol_ready, b - 1)
                    for part in parts:
                        x, k = part // 2, part % 2
                        n = "qk"[x]
                        for i, (w, act) in enumerate([(wh, core.xh), (wl, core.xh), (wh, core.xl)]):
                            op = nc.tensor.matmul(tp[:, x, :], w[n][:, k, m * P:(m + 1) * P], act[:, k, :],
                                                  start=(k == 0 and i == 0), stop=(k == KT - 1 and i == 2))
                    if parts[-1] == 3:
                        op.then_inc(qk_ps, 1)

                def tokens(t, xh, xl, n, done):
                    for k in range(KT):
                        for i, (x, w) in enumerate([(xh, wh), (xh, wl), (xl, wh)]):
                            op = nc.tensor.matmul(tpy[:, t, :], x[:, k, t * P:(t + 1) * P], w[n][:, k, :],
                                                  start=(k == 0 and i == 0), stop=(k == KT - 1 and i == 2))
                    if t == TILES - 1:
                        op.then_inc(done, 1)

                def v_proj(b, t, after_y):
                    if t == 0 and after_y:
                        pe.wait_ge(y_ready, b)
                    elif t == 0:
                        pe.wait_ge(full_ready, KT * b + KT)
                    tokens(t, core.xh, core.xl, "v", v_ps)

                def s1_unit(b, st, i):
                    g, qt = st // TILES, st % TILES
                    if qt == 0 and i == 0:
                        pe.wait_ge(loaded[g], PER_LOAD * b + PER_LOAD)
                    pe.wait_ge(max_done, (b * STEPS + st) * GH + i + 1)
                    r = stack_rows(g, STACK)
                    nc.tensor.matmul(s1p[i % 2][:, :], qs[r, g // 2, i, qt * P:(qt + 1) * P], ks[r, g // 2, i, :],
                                     start=True, stop=True).then_inc(s1_ready, 1)

                def s2_unit(b, st, i):
                    g, kt = st // TILES, st % TILES
                    if kt == 0 and i == 0:
                        pe.wait_ge(rowed[g], 16 * b + 16)
                    pe.wait_ge(exp_done, (b * STEPS + st) * GH + i + 1)
                    r = stack_rows(g, STACK + 1)
                    nc.tensor.matmul(s2p[i % 2][:, :], ks[r, g // 2, i, kt * P:(kt + 1) * P], qs[r, g // 2, i, :],
                                     start=True, stop=True).then_inc(s2_ready, 1)

                def max_t(b, g):
                    pe.wait_ge(max_done, (b * GROUPS + g) * TILES * GH + TILES * GH + 2)
                    if first(b) and g in (1, 2):
                        pe.wait_ge(nmt_ready, g)
                    elif not (first(b) and g == 0):
                        pe.wait_ge(on_ready, b * GROUPS + g - 2)
                    for qt in range(TILES):
                        op = nc.tensor.transpose(mp[0:GH, qt * P:(qt + 1) * P], nm[:, g % 2, qt, :], core.ident[:, :])
                    op.then_inc(nm_ready, 1)

                def pv(b, st):
                    g, kt = st // TILES, st % TILES
                    pe.wait_ge(band_done, b * STEPS + st + 1)
                    if st == 0:
                        pe.wait_ge(v_ready, b + 1)
                    if kt == 0 and not (first(b) and g == 0):
                        pe.wait_ge(ot_ready, b * GROUPS + g)
                    for i in range(GH):
                        op = nc.tensor.matmul(pvp[2 * HD * i:2 * HD * (i + 1), :], vaug[:, kt, GH * g + i, :], prob[:, kt, i, :],
                                              start=(kt == 0), stop=(kt == TILES - 1))
                    op.then_inc(pv_done, 1)

                def out_t(b, g):
                    pe.wait_ge(ot_ready, b * GROUPS + g + 1)
                    if isinstance(b, int) and b == core.batches - 1 and g >= 2:
                        pe.wait_ge(on_ready, b * GROUPS + g)
                    else:
                        pe.wait_ge(nmt_ready, b * GROUPS + g + 3)
                    for qt in range(TILES):
                        op = nc.tensor.transpose(mp[:, qt * P:(qt + 1) * P], ot[:, qt * P:(qt + 1) * P], core.ident[:, :])
                    op.then_inc(tr_ready, 1)

                def o_transpose(b, k, sem, count):
                    if k == 0:
                        pe.wait_ge(on_ready, b * GROUPS + GROUPS)
                        pe.wait_ge(sem, count)
                    for t in range(TILES):
                        op = nc.tensor.transpose(tp[:, k, t * P:(t + 1) * P], on[:, t, k * P:(k + 1) * P], core.ident[:, :])
                    if k == KT - 1:
                        op.then_inc(o_ps, 1)

                def o_project(b, t):
                    if t == 0:
                        pe.wait_ge(ol_ready, b + 1)
                    tokens(t, oh, ol, "o", y_ps)

                norm.transpose(pe, 0)
                qk_proj(0, 0)
                qk_proj(0, 1)
                for t in range(TILES):
                    v_proj(0, t, False)
                for st in range(AHEAD):
                    for i in range(GH):
                        s1_unit(0, st, i)
                    if st == TILES - 1:
                        max_t(0, 0)

                def body(b, before, more):
                    for st in range(STEPS):
                        ahead = st + AHEAD
                        for i in range(GH):
                            s2_unit(b, st, i)
                            if ahead < STEPS:
                                s1_unit(b, ahead, i)
                            elif more:
                                s1_unit(b + 1, ahead - STEPS, i)
                            at = (st, i)
                            if i == 3 and st:
                                pv(b, st - 1)
                            elif i == 3 and before:
                                pv(b - 1, STEPS - 1)
                            if st % TILES == 1 and i == 1:
                                g = ahead // TILES
                                if st + TILES < STEPS:
                                    max_t(b, st // TILES + 1)
                                elif more:
                                    max_t(b + 1, 0)
                            if st % TILES == 2 and i == 0:
                                if st > 2:
                                    out_t(b, st // TILES - 1)
                                elif before:
                                    out_t(b - 1, GROUPS - 1)
                            if more and at in XT_AT:
                                n = XT_AT.index(at)
                                norm.transpose(pe, b + 1, lambda: pe.wait_ge(v_ready, b + 1), range(n, n + 1))
                            if more and at in QK_AT[0]:
                                n = QK_AT[0].index(at)
                                qk_proj(b + 1, 0, range(n, n + 1))
                            if more and at in QK_AT[1]:
                                n = QK_AT[1].index(at)
                                qk_proj(b + 1, 1, range(n, n + 1), before)
                            if before and at in OT_AT:
                                if more:
                                    o_transpose(b - 1, OT_AT.index(at), full_ready, KT * b + KT + 1)
                                else:
                                    o_transpose(b - 1, OT_AT.index(at), v_ready, b + 1)
                            if before and at in Y_AT:
                                o_project(b - 1, Y_AT.index(at))
                            if more and at in V_AT:
                                v_proj(b + 1, V_AT.index(at), before)

                over_sequences(pe, core.batches, body)
                last = core.batches - 1
                pv(last, STEPS - 1)
                out_t(last, GROUPS - 1)
                for k in range(KT):
                    o_transpose(last, k, *((y_ready, last + 1) if last else (v_ready, 1)))
                for t in range(TILES):
                    o_project(last, t)

            @block.scalar
            def _(act):
                act.wait_ge(spread, 1)
                nc.scalar.copy(bvs[:, :, :], full[:, :, 0:P]).then_inc(spread_h, 1)
                norm.high(act, 0)

                def high_part(b, m, x):
                    if x == 0:
                        act.wait_ge(full_ready, KT * b + m + 1)
                        if not first(b):
                            act.wait_ge(written[m], PER_WRITE * b)
                    op = nc.scalar.copy(qkh[:, m, x, :], full[:, x, :])
                    if x:
                        op.then_inc(qkh_ready, 1)

                def exp_unit(b, st, i):
                    kt = st % TILES
                    n = b * STEPS + st
                    act.wait_ge(s2_ready, n * GH + i + 1)
                    if i == 0 and not (first(b) and st < TILES):
                        act.wait_ge(pv_done, n - TILES + 1)
                    nc.scalar.activation(prob[:, kt, i, :], s2p[i % 2][:, :], ACT.Exp).then_inc(exp_done, 1)

                def max_copy(b, g):
                    act.wait_ge(nm_ready, b * GROUPS + g + 1)
                    if not (first(b) and g < 2):
                        if g >= 2:
                            act.wait_ge(rowed[g - 2], 16 * b + 16)
                        else:
                            act.wait_ge(rowed[g + 2], 16 * b)
                    nc.scalar.copy(nmt[:, g % 2, :], mp[0:GH, :]).then_inc(nmt_ready, 1)

                def v_copy(b):
                    act.wait_ge(v_ps, b + 1)
                    if first(b):
                        act.wait_ge(va_one, 1)
                    else:
                        act.wait_ge(pv_done, b * STEPS)
                    for t in range(TILES):
                        op = nc.scalar.copy(vaug[:, t, :, 0:HD], tpy[:, t, :].rearrange("p (h d) -> p h d", h=HEADS))
                    op.then_inc(v_ready, 1)

                def o_high(b, k):
                    if k == 0:
                        act.wait_ge(o_ps, b + 1)
                    op = nc.scalar.copy(oh[:, k, :], tp[:, k, :])
                    if k == KT - 1:
                        op.then_inc(oh_ready, 1)

                for m in range(KT):
                    for x in range(2):
                        high_part(0, m, x)
                max_copy(0, 0)

                def body(b, before, more):
                    for st in range(STEPS):
                        for i in range(GH):
                            exp_unit(b, st, i)
                            if st == 0 and i == 3:
                                v_copy(b)
                            if st % TILES == 1 and i == 1:
                                if st + TILES < STEPS:
                                    max_copy(b, st // TILES + 1)
                                elif more:
                                    max_copy(b + 1, 0)
                            if more and st == 2 and i in (1, 2):
                                norm.high(act, b + 1, lambda: act.wait_ge(v_ps, b + 1), range(i - 1, i))
                            if more and (st, i) in ((5, 1), (5, 2), (9, 2), (9, 3)):
                                high_part(b + 1, st // 8, int((st, i) in ((5, 2), (9, 3))))
                            if before and (st, i) in ((6, 3), (7, 0)):
                                o_high(b - 1, st - 6)

                act.sem_inc(exp_done, 2)
                over_sequences(act, core.batches, body)
                for k in range(KT):
                    o_high(core.batches - 1, k)

            @block.vector
            def _(dve):
                dve.wait_ge(loaded_b, 16 * (4 * KT + 1))
                dve.wait_ge(pool_step, 2)
                nc.vector.tensor_tensor(bq[:, :], bq[:, :], ocr[:, :], ALU.add)
                for k in range(KT):
                    op = nc.vector.tensor_scalar(full[:, k, 0:P], core.ones[:, :], bv[:, k:k + 1], None, ALU.mult)
                op.then_inc(spread, 1)
                dve.wait_ge(spread_h, 1)
                nc.vector.tensor_tensor(bvl[:, :, :], full[:, :, 0:P], as_f32(bvs[:, :, :]), ALU.subtract).then_inc(spread_done, 2)
                dve.wait_ge(crow_ps, 1)
                nc.vector.tensor_tensor(crow[:, :], crow[:, :], tpy[:, 0, :], ALU.add).then_inc(crow_ready, 1)
                dve.sem_inc(max_done, 2)
                dve.sem_inc(y_ready, 1)

                def full_part(b, m, x):
                    if x == 0:
                        dve.wait_ge(qk_ps, KT * b + m + 1)
                        if not first(b) or m == 1:
                            dve.wait_ge(qkl_ready, KT * b + m)
                        nc.vector.tensor_scalar(full[:, 0, :], tp[:, 0, :], bq[:, m:m + 1], SCALE, ALU.add, ALU.mult)
                    else:
                        nc.vector.tensor_scalar(full[:, 1, :], tp[:, 1, :], bk[:, m:m + 1], None,
                                                ALU.add).then_inc(full_ready, 1)

                def max_unit(b, st, i):
                    g, qt = st // TILES, st % TILES
                    dve.wait_ge(s1_ready, (b * STEPS + st) * GH + i + 1)
                    nc.vector.tensor_reduce(nm[:, g % 2, qt, i:i + 1], s1p[i % 2][:, :], AXIS_X, ALU.max,
                                            negate=True).then_inc(max_done, 1)

                def ot_copy(b, g):
                    dve.wait_ge(pv_done, b * STEPS + TILES * (g + 1))
                    if not (first(b) and g == 0):
                        dve.wait_ge(tr_ready, b * GROUPS + g)
                    nc.vector.tensor_copy(ot[:, :], pvp[:, :]).then_inc(ot_ready, 1)

                def normalise_out(b, g):
                    dve.wait_ge(tr_ready, b * GROUPS + g + 1)
                    if g == 0 and not first(b):
                        dve.wait_ge(o_ps, b)
                    m4 = mp[:, :].rearrange("p (t h d) -> p t h d", t=TILES, h=GH)
                    nc.vector.reciprocal(rec[:, :, :, :], m4[:, :, :, HD:HD + 1]).then_inc(rec_ready, 1)
                    dve.wait_ge(rec_ready, b * GROUPS + g + 1)
                    out = on[:, :, g * GH * HD:(g + 1) * GH * HD].rearrange("p t (h d) -> p t h d", h=GH)
                    nc.vector.tensor_tensor(out, m4[:, :, :, 0:HD], bcast(rec[:, :, :, :], [P, TILES, GH, HD]),
                                            ALU.mult).then_inc(on_ready, 1)

                def o_low(b, k):
                    if k == 0:
                        dve.wait_ge(oh_ready, b + 1)
                    op = nc.vector.tensor_tensor(ol[:, k, :], tp[:, k, :], as_f32(oh[:, k, :]), ALU.subtract)
                    if k == KT - 1:
                        op.then_inc(ol_ready, 1)

                def y_out(b, half, split):
                    if half == 0:
                        dve.wait_ge(y_ps, b + 1)
                        dve.wait_ge(qkl_ready, KT * split)
                    t = slice(2 * half, 2 * half + 2)
                    op = nc.vector.tensor_tensor(ys[:, t, :], tpy[:, t, :], bcast(crow[:, :].unsqueeze(1), [P, 2, DM]), ALU.add)
                    if half:
                        op.then_inc(y_ready, 1)

                norm.normalise(dve, 0)
                norm.low(dve, 0)
                for m in range(KT):
                    full_part(0, m, 0)
                    full_part(0, m, 1)
                for st in range(AHEAD):
                    for i in range(GH):
                        max_unit(0, st, i)

                def body(b, before, more):
                    for st in range(STEPS):
                        for i in range(GH):
                            if st + AHEAD < STEPS:
                                max_unit(b, st + AHEAD, i)
                            elif more:
                                max_unit(b + 1, st + AHEAD - STEPS, i)
                            if more and st == 0:
                                norm.normalise(dve, b + 1, range(i, i + 1))
                            if st % TILES == 1 and i == 0:
                                if st > 1:
                                    ot_copy(b, st // TILES - 1)
                                elif before:
                                    ot_copy(b - 1, GROUPS - 1)
                            if st % TILES == 2 and i == 3:
                                if st > 2:
                                    normalise_out(b, st // TILES - 1)
                                elif before:
                                    normalise_out(b - 1, GROUPS - 1)
                            if more and (st, i) in ((2, 3), (3, 0)):
                                norm.low(dve, b + 1, range(st - 2, st - 1))
                            if more and (st, i) in ((4, 3), (5, 1), (9, 1), (9, 2)):
                                full_part(b + 1, st // 8, int((st, i) in ((5, 1), (9, 2))))
                            if before and st == 7 and i in (0, 1):
                                o_low(b - 1, i)
                            if before and st == 11 and i in (2, 3):
                                y_out(b - 1, i - 2, b + 2 if more else b + 1)
                            if before and st == 14:
                                stats.tiles(dve, b - 1, lambda: dve.wait_ge(x_done, b), range(i, i + 1))
                            if before and (st, i) == (15, 1):
                                stats.finish(dve, b - 1)

                over_sequences(dve, core.batches, body)
                last = core.batches - 1
                ot_copy(last, GROUPS - 1)
                normalise_out(last, GROUPS - 1)
                for k in range(KT):
                    o_low(last, k)
                for half in range(2):
                    y_out(last, half, core.batches)
                stats.take(dve, last, lambda: dve.wait_ge(x_done, core.batches))


GH0 = 2
CHUNK = P
SUB = 32
LEVELS = [0, 1, 2, 4, 8, 16, 32, 64]
SMALL = 6


def level_masks():
    import numpy as np

    m = np.zeros((SMALL, SUB, SUB), np.float32)
    for i, size in enumerate(LEVELS[:SMALL]):
        for s in range(SUB):
            for t in range(SUB):
                if size == 0:
                    m[i, s, t] = s == t
                else:
                    same = s // (2 * size) == t // (2 * size)
                    m[i, s, t] = same and s % (2 * size) < size <= t % (2 * size)
    return np.ascontiguousarray(np.tile(m.transpose(1, 0, 2), (P // SUB, 1, 1)))


def gla_stage(core, a, name):
    nc, s = core.nc, core.sem
    NC = TOKENS // CHUNK
    with ExitStack() as ctx:
        wih, wil = (core.sbuf(n, [P, KT, 3 * DM], F32R, ctx) for n in ("wih", "wil"))
        g1h, g1l = (core.sbuf(n, [P, KT, P], F32R, ctx) for n in ("wg1h", "wg1l"))
        g2h, g2l = (core.sbuf(n, [P, DM], F32R, ctx) for n in ("wg2h", "wg2l"))
        woh, wol = (core.sbuf(n, [P, KT, DM], F32R, ctx) for n in ("gwoh", "gwol"))
        w_in = a["w_in_t"].rearrange("(k p) m -> p k m", p=P)
        split_pair(core, name, [(w_in[:, k, :], wih[:, k, :], wil[:, k, :]) for k in range(KT)]
                   + [(a["w_g1_t"].rearrange("(k p) m -> p k m", p=P), g1h[:, :, :], g1l[:, :, :]),
                      (a["w_g2_t"], g2h[:, :], g2l[:, :])], ctx)

        wo_loaded, wo_scaled, wo_high = s(name + "_wo_loaded"), s(name + "_wo_scaled"), s(name + "_wo_high")
        with ExitStack() as inner:
            wo = core.sbuf("wo_raw", [P, KT, DM], F32, inner)
            lnw = core.sbuf("ln_w", [P, KT], F32, inner)
            with nc.Block() as block:

                @block.sync
                def _(sp):
                    sp.dma_start(wo[:, :, :], a["w_out_t"].rearrange("(k p) m -> p k m", p=P)).then_inc(wo_loaded, 16)
                    for k in range(KT):
                        sp.dma_start(lnw[:, k:k + 1], a["ln_w"][k * P:(k + 1) * P, :]).then_inc(wo_loaded, 16)

                @block.scalar
                def _(act):
                    act.wait_ge(wo_scaled, 1)
                    nc.scalar.copy(woh[:, :, :], wo[:, :, :]).then_inc(wo_high, 1)

                @block.vector
                def _(dve):
                    dve.wait_ge(wo_loaded, 16 * (1 + KT))
                    for k in range(KT):
                        op = nc.vector.tensor_scalar(wo[:, k, :], wo[:, k, :], lnw[:, k:k + 1], None, ALU.mult)
                    op.then_inc(wo_scaled, 1)
                    dve.wait_ge(wo_high, 1)
                    nc.vector.tensor_tensor(wol[:, :, :], wo[:, :, :], as_f32(woh[:, :, :]), ALU.subtract)
        rstd_block(core, name)

        W2 = GH0 * TOKENS
        masks_f = core.sbuf("level_mask_f32", [P, SMALL, SUB], F32, ctx)
        masks = core.sbuf("level_mask", [P, SMALL, SUB], U8, ctx)
        sig = core.sbuf("g_sig", [P, W2], F32, ctx)
        q = core.sbuf("g_q", [P, W2], F32, ctx)
        f = core.sbuf("g_f", [P, W2], F32, ctx)
        qp = core.sbuf("g_qp", [P, W2], F32, ctx)
        ks = core.sbuf("g_ks", [P, W2], F32, ctx)
        tot = core.sbuf("g_tot", [P, W2], F32, ctx)
        v = core.sbuf("g_v", [P, NC, DM], F32, ctx)
        gate = core.sbuf("g_gate", [P, NC, DM], F32, ctx)
        ghi, glo = (core.sbuf(n, [P, TOKENS], F32R, ctx) for n in ("ghi", "glo"))
        diag = core.sbuf("g_diag", [P, GH0, NC, SUB], F32, ctx)
        at = core.sbuf("g_at", [P, GH0, NC, CHUNK], F32, ctx)
        kst = core.sbuf("g_kst", [P, GH0, NC - 1, P], F32, ctx)
        st = core.sbuf("g_state", [P, GH0, NC - 1, P], F32, ctx)
        og = core.sbuf("g_og", [P, NC, DM], F32, ctx)
        o6 = core.sbuf("g_stat6", [P, NC, 6], F32, ctx)
        omv = core.sbuf("g_mv", [P, NC, 2], F32, ctx)
        osd = core.sbuf("g_sd", [P, NC], F32, ctx)
        ors = core.sbuf("g_rstd", [P, NC], F32, ctx)
        oh, ol = (core.sbuf(n, [P, KT, TOKENS], F32R, ctx) for n in ("g_oh", "g_ol"))

        ab = core.psum("g_a", [P, 2, TOKENS], ctx)
        hb = core.psum("g_h", [P, GH0, TOKENS], ctx)
        ob = core.psum("g_o", [P, NC, DM], ctx)
        tp = core.psum("g_tp", [P, KT, TOKENS], ctx)
        aby = ab[:, :, :].rearrange("p k (u d) -> p (k u) d", u=2)
        hbc = hb[:, :, :].rearrange("p h (c t) -> p h c t", c=NC)
        hd = hbc[:, :, :, 0:SUB]

        def total(size):
            if size == 1:
                return f[:, :]
            off = W2 - 2 * W2 // size
            return tot[:, off:off + W2 // size]

        a_free = [s(f"{name}_a{i}_free") for i in range(2)]
        lg_ps, q_ps, v_ps, g1_ps, gate_ps, y_ps = (s(f"{name}_{n}_ps") for n in ("lg", "q", "v", "g1", "gate", "y"))
        f_ready, k_ready, sig_ready, q_ready, qp_ready = (s(f"{name}_{n}") for n in ("f", "k", "sig", "q", "qp"))
        v_ready, ghi_ready, glo_ready, gate_ready = (s(f"{name}_{n}") for n in ("v", "g1hi", "g1lo", "gate"))
        level_done = s(name + "_level_done")
        merged = s(name + "_merged")
        up_q, up_k, up_t = (s(f"{name}_up_{n}") for n in ("q", "k", "t"))
        diag_copied = s(name + "_diag_copied")
        at_ready = s(name + "_at_ready")
        kst_ps, kst_ready = s(name + "_kst_ps"), s(name + "_kst_ready")
        kv_ps, s0_ready, st_ready = s(name + "_kv_ps"), s(name + "_s0_ready"), s(name + "_st_ready")
        o_ready, og_ready, o_stat, o_aggr, o_sd, o_rs, on_ready = (
            s(f"{name}_{n}") for n in ("o_ps", "og", "o_stat", "o_aggr", "o_sd", "o_rs", "on"))
        ot_ps, oh_ready, ol_ready, x_done = (s(f"{name}_{n}") for n in ("ot_ps", "oh", "ol", "x_updated"))
        turns = s(name + "_turns")
        masks_in, zeroed = s(name + "_masks"), s(name + "_zeroed")
        NL = len(LEVELS)
        norm = Norm(core, name, tp)
        stats = Stats(core, name)
        first = lambda b: isinstance(b, int) and b == 0

        with nc.Block() as block:

            @block.sync
            def _(sp):
                sp.dma_start(masks_f[:, :, :], a["level_masks"]).then_inc(masks_in, 16)

            @block.tensor
            def _(pe):
                pairs = lambda wh, wl, xh, xl: [(wh, xh), (wl, xh), (wh, xl)]

                def bank(b, i, use, uses):
                    pe.wait_ge(a_free[i], (b * uses - (0 if first(b) else 1)) + use + 1)

                def channels(b, col, i, use, done):
                    bank(b, i, use, (5, 4)[i])
                    for k in range(KT):
                        for n, (w, x) in enumerate(pairs(wih, wil, core.xh, core.xl)):
                            op = nc.tensor.matmul(ab[:, i, :], w[:, k, col:col + P], x[:, k, :],
                                                  start=(k == 0 and n == 0), stop=(k == KT - 1 and n == 2))
                    op.then_inc(done, 1)

                def v_proj(b, half):
                    bank(b, half, 2, (5, 4)[half])
                    for t in (2 * half, 2 * half + 1):
                        for k in range(KT):
                            for n, (w, x) in enumerate(pairs(wih, wil, core.xh, core.xl)):
                                op = nc.tensor.matmul(aby[:, t, :], x[:, k, t * P:(t + 1) * P], w[:, k, 0:DM],
                                                      start=(k == 0 and n == 0), stop=(k == KT - 1 and n == 2))
                    op.then_inc(v_ps, 1)

                def g1_proj(b):
                    bank(b, 0, 3, 5)
                    for k in range(KT):
                        for n, (w, x) in enumerate(pairs(g1h, g1l, core.xh, core.xl)):
                            op = nc.tensor.matmul(ab[:, 0, :], w[:, k, :], x[:, k, :],
                                                  start=(k == 0 and n == 0), stop=(k == KT - 1 and n == 2))
                    op.then_inc(g1_ps, 1)

                def gate_proj(b):
                    pe.wait_ge(glo_ready, b + 1)
                    if not first(b):
                        pe.wait_ge(og_ready, b)
                    for t in range(NC):
                        for n, (w, x) in enumerate(pairs(g2h, g2l, ghi, glo)):
                            op = nc.tensor.matmul(ob[:, t, :], x[:, t * P:(t + 1) * P], w[:, :],
                                                  start=(n == 0), stop=(n == 2))
                    op.then_inc(gate_ps, 1)

                def level(b, i):
                    size = LEVELS[i]
                    if i == 0:
                        pe.wait_ge(q_ready, 2 * b + 2)
                        pe.wait_ge(k_ready, 2 * b + 2)
                        if not first(b):
                            pe.wait_ge(st_ready, b)
                    elif i == 1:
                        pe.wait_ge(qp_ready, b + 1)
                    else:
                        pe.wait_ge(up_q, 7 * b + i - 1)
                        pe.wait_ge(up_k, 7 * b + i - 1)
                    if 1 <= i <= SMALL:
                        pe.wait_ge(merged, SMALL * b + i)
                    qq = q if i == 0 else qp
                    for h in range(GH0):
                        for c in range(NC):
                            base = h * TOKENS + c * CHUNK
                            if i < SMALL:
                                for j in range(CHUNK // SUB):
                                    r = slice(base + SUB * j, base + SUB * (j + 1))
                                    op = nc.tensor.matmul(hd[SUB * j:SUB * (j + 1), h, c, :], ks[:, r], qq[:, r],
                                                          start=True, stop=True)
                            else:
                                for j in range(0, CHUNK, 2 * size):
                                    op = nc.tensor.matmul(hbc[j:j + size, h, c, j + size:j + 2 * size],
                                                          ks[:, base + j:base + j + size],
                                                          qp[:, base + j + size:base + j + 2 * size],
                                                          start=True, stop=True)
                    op.then_inc(level_done, 1)

                def kst_t(b):
                    pe.wait_ge(up_k, 7 * b + 7)
                    if not first(b):
                        pe.wait_ge(ol_ready, b)
                    else:
                        pe.wait_ge(norm.xl_ready, 1)
                    for h in range(GH0):
                        for c in range(NC - 1):
                            base = h * TOKENS + c * CHUNK
                            op = nc.tensor.transpose(tp[:, h, c * P:(c + 1) * P], ks[:, base:base + P], core.ident[:, :])
                    op.then_inc(kst_ps, 1)

                def kv(b):
                    pe.wait_ge(kst_ready, b + 1)
                    pe.wait_ge(v_ready, 2 * b + 2)
                    pe.wait_ge(at_ready, b + 1)
                    for h in range(GH0):
                        for c in range(NC - 1):
                            op = nc.tensor.matmul(hb[:, h, c * P:(c + 1) * P], kst[:, h, c, :],
                                                  v[:, c, h * P:(h + 1) * P], start=True, stop=True)
                    op.then_inc(kv_ps, 1)

                def output(b):
                    pe.wait_ge(gate_ready, b + 1)
                    pe.wait_ge(diag_copied, b + 1)
                    pe.wait_ge(up_q, 7 * b + 7)
                    for c in range(NC):
                        for h in range(GH0):
                            out = ob[:, c, h * P:(h + 1) * P]
                            nc_last = c == 0
                            op = nc.tensor.matmul(out, at[:, h, c, :], v[:, c, h * P:(h + 1) * P], start=True, stop=nc_last)
                            if c:
                                if c == 1 and h == 0:
                                    pe.wait_ge(st_ready, b + 1)
                                base = h * TOKENS + c * CHUNK
                                op = nc.tensor.matmul(out, qp[:, base:base + P], st[:, h, c - 1, :], start=False, stop=True)
                    op.then_inc(o_ready, 1)

                def o_transpose(b):
                    pe.wait_ge(on_ready, b + 1)
                    pe.wait_ge(norm.xl_ready, b + 2 if not (isinstance(b, int) and b == core.batches - 1) else b + 1)
                    if isinstance(b, int) and b == core.batches - 1:
                        pe.wait_ge(kst_ready, core.batches)
                    for k in range(KT):
                        for t in range(NC):
                            op = nc.tensor.transpose(tp[:, k, t * P:(t + 1) * P], og[:, t, k * P:(k + 1) * P], core.ident[:, :])
                    op.then_inc(ot_ps, 1)

                def o_project(b, free):
                    pe.wait_ge(ol_ready, b + 1)
                    pe.wait_ge(a_free[0], free[0])
                    pe.wait_ge(a_free[1], free[1])
                    for t in range(NC):
                        for k in range(KT):
                            for n, (w, x) in enumerate(pairs(woh, wol, oh, ol)):
                                op = nc.tensor.matmul(aby[:, t, :], x[:, k, t * P:(t + 1) * P], w[:, k, :],
                                                      start=(k == 0 and n == 0), stop=(k == KT - 1 and n == 2))
                    op.then_inc(y_ps, 1)

                norm.transpose(pe, 0)

                def body(b, before, more):
                    pe.wait_ge(norm.xl_ready, b + 1)
                    channels(b, 2 * DM, 0, 0, lg_ps)
                    channels(b, 2 * DM + P, 1, 0, lg_ps)
                    channels(b, DM, 0, 1, q_ps)
                    channels(b, DM + P, 1, 1, q_ps)
                    v_proj(b, 0)
                    level(b, 0)
                    v_proj(b, 1)
                    level(b, 1)
                    g1_proj(b)
                    level(b, 2)
                    level(b, 3)
                    if before:
                        o_transpose(b - 1)
                    level(b, 4)
                    gate_proj(b)
                    level(b, 5)
                    if before:
                        o_project(b - 1, (5 * b + 4, 4 * b + 3))
                    level(b, 6)
                    level(b, 7)
                    kst_t(b)
                    if more:
                        norm.transpose(pe, b + 1, lambda: pe.wait_ge(kst_ready, b + 1))
                    kv(b)
                    output(b)

                over_sequences(pe, core.batches, body)
                last = core.batches - 1
                o_transpose(last)
                o_project(last, (5 * last + 4 + (last > 0), 4 * last + 3 + (last > 0)) if last else (5, 4))

            @block.scalar
            def _(act):
                act.sem_inc(a_free[0], 1)
                act.sem_inc(a_free[1], 1)
                norm.high(act, 0)

                def decay(b, h):
                    act.wait_ge(lg_ps, 2 * b + h + 1)
                    r = slice(h * TOKENS, (h + 1) * TOKENS)
                    if h == 0 and not first(b):
                        act.wait_ge(o_ready, b)
                        act.wait_ge(up_t, 7 * b)
                    nc.scalar.activation(f[:, r], ab[:, h, :], ACT.Sigmoid).then_inc(f_ready, 1)
                    nc.scalar.activation(ks[:, r], ab[:, h, :], ACT.Sigmoid, scale=-1.0).then_inc(k_ready, 1)
                    act.wait_ge(k_ready, 2 * b + h + 1)
                    act.sem_inc(a_free[h], 1)

                def q_sig(b, h):
                    act.wait_ge(q_ps, 2 * b + h + 1)
                    if not first(b):
                        act.wait_ge(q_ready, 2 * b)
                    nc.scalar.activation(sig[:, h * TOKENS:(h + 1) * TOKENS], ab[:, h, :], ACT.Sigmoid).then_inc(sig_ready, 1)

                def v_copy(b, half):
                    act.wait_ge(v_ps, 2 * b + half + 1)
                    nc.scalar.copy(v[:, 2 * half:2 * half + 2, :], aby[:, 2 * half:2 * half + 2, :]).then_inc(v_ready, 1)
                    act.wait_ge(v_ready, 2 * b + half + 1)
                    act.sem_inc(a_free[half], 1)

                def g1_high(b):
                    act.wait_ge(g1_ps, b + 1)
                    if not first(b):
                        act.wait_ge(gate_ps, b)
                    nc.scalar.copy(ghi[:, :], ab[:, 0, :]).then_inc(ghi_ready, 1)

                def gate_sig(b):
                    act.wait_ge(gate_ps, b + 1)
                    nc.scalar.activation(gate[:, :, :], ob[:, :, :], ACT.Sigmoid).then_inc(gate_ready, 1)

                def diag_copy(b):
                    act.wait_ge(merged, SMALL * b + SMALL)
                    if first(b):
                        act.wait_ge(zeroed, 2)
                    else:
                        act.wait_ge(o_ready, b)
                    for j in range(CHUNK // SUB):
                        r = slice(SUB * j, SUB * (j + 1))
                        op = nc.scalar.copy(at[r, :, :, r], diag[r, :, :, :])
                    op.then_inc(diag_copied, 1)

                def at_rest(b):
                    act.wait_ge(level_done, NL * b + NL)
                    if first(b):
                        act.wait_ge(zeroed, 2)
                    else:
                        act.wait_ge(o_ready, b)
                    for r0, n in ((0, 64), (0, 32), (64, 32)):
                        op = nc.scalar.copy(at[r0:r0 + n, :, :, r0 + n:r0 + 2 * n], hbc[r0:r0 + n, :, :, r0 + n:r0 + 2 * n])
                    op.then_inc(at_ready, 1)

                def kst_copy(b):
                    act.wait_ge(kst_ps, b + 1)
                    w = (NC - 1) * P
                    nc.scalar.copy(kst[:, :, :, :].rearrange("p h c d -> p h (c d)"), tp[:, :, 0:w]).then_inc(kst_ready, 1)

                def state0(b):
                    act.wait_ge(kv_ps, b + 1)
                    nc.scalar.copy(st[:, :, 0, :], hb[:, :, 0:P]).then_inc(s0_ready, 1)

                def o_sqrt(b):
                    act.wait_ge(o_aggr, b + 1)
                    nc.scalar.activation(osd[:, :], omv[:, :, 1], ACT.Sqrt, bias=core.eps[:, 0:1]).then_inc(o_sd, 1)

                def o_high(b):
                    act.wait_ge(ot_ps, b + 1)
                    nc.scalar.copy(oh[:, :, :], tp[:, :, :]).then_inc(oh_ready, 1)

                def body(b, before, more):
                    if before:
                        o_sqrt(b - 1)
                    decay(b, 0)
                    decay(b, 1)
                    q_sig(b, 0)
                    q_sig(b, 1)
                    v_copy(b, 0)
                    v_copy(b, 1)
                    g1_high(b)
                    if before:
                        o_high(b - 1)
                    gate_sig(b)
                    diag_copy(b)
                    at_rest(b)
                    kst_copy(b)
                    if more:
                        norm.high(act, b + 1, lambda: act.wait_ge(g1_ps, b + 1))
                    state0(b)

                over_sequences(act, core.batches, body)
                o_sqrt(core.batches - 1)
                o_high(core.batches - 1)

            @block.gpsimd
            def _(pool):
                nc.gpsimd.memset(diag[:, :, :, :], 0.0).then_inc(zeroed, 1)
                nc.gpsimd.memset(at[:, :, :, :], 0.0).then_inc(zeroed, 1)

                def raise_k(b, i):
                    size = LEVELS[i]
                    pool.wait_ge(level_done, NL * b + i + 1)
                    if i == 1:
                        pool.wait_ge(f_ready, 2 * b + 2)
                    else:
                        pool.wait_ge(up_t, 7 * b + i - 1)
                        pool.wait_ge(up_k, 7 * b + i - 1)
                    n = W2 // (2 * size)
                    left = ks[:, :].rearrange("p (n s l) -> p n s l", s=2, l=size)[:, :, 0, :]
                    tt = total(size).rearrange("p (n s) -> p n s", s=2)[:, :, 1:2]
                    nc.gpsimd.tensor_tensor(left, left, bcast(tt, [P, n, size]), ALU.mult).then_inc(up_k, 1)

                def body(b, before, more):
                    for i in range(1, NL):
                        raise_k(b, i)

                over_sequences(pool, core.batches, body)

            @block.vector
            def _(dve):
                norm.normalise(dve, 0)
                norm.low(dve, 0)
                dve.wait_ge(masks_in, 16)
                nc.vector.tensor_copy(masks[:, :, :], masks_f[:, :, :])
                dve.wait_ge(zeroed, 1)

                def gated(b):
                    dve.wait_ge(o_ready, b + 1)
                    nc.vector.tensor_tensor(og[:, :, :], ob[:, :, :], gate[:, :, :], ALU.mult).then_inc(og_ready, 1)
                    dve.wait_ge(og_ready, b + 1)
                    for t in range(NC):
                        op = nc.vector.bn_stats(o6[:, t, :], og[:, t, :])
                    op.then_inc(o_stat, 1)
                    dve.wait_ge(o_stat, b + 1)
                    hold(dve, turns)
                    for t in range(NC):
                        op = nc.vector.bn_aggr(omv[:, t, :], o6[:, t, :])
                    op.then_inc(o_aggr, 1)

                def o_norm(b):
                    dve.wait_ge(o_sd, b + 1)
                    nc.vector.reciprocal(ors[:, :], osd[:, :]).then_inc(o_rs, 1)
                    dve.wait_ge(o_rs, b + 1)
                    for t in range(NC):
                        op = nc.vector.tensor_scalar(og[:, t, :], og[:, t, :], omv[:, t, 0:1], ors[:, t:t + 1],
                                                     ALU.subtract, ALU.mult)
                    op.then_inc(on_ready, 1)

                def q_silu(b, h):
                    dve.wait_ge(sig_ready, 2 * b + h + 1)
                    r = slice(h * TOKENS, (h + 1) * TOKENS)
                    nc.vector.tensor_tensor(q[:, r], ab[:, h, :], sig[:, r], ALU.mult).then_inc(q_ready, 1)
                    dve.wait_ge(q_ready, 2 * b + h + 1)
                    dve.sem_inc(a_free[h], 1)

                def q_first(b):
                    dve.wait_ge(f_ready, 2 * b + 2)
                    nc.vector.tensor_tensor(qp[:, :], q[:, :], f[:, :], ALU.mult).then_inc(qp_ready, 1)

                def merge(b, i):
                    dve.wait_ge(level_done, NL * b + i + 1)
                    if i == 0 and not first(b):
                        dve.wait_ge(diag_copied, b)
                    if i:
                        dve.wait_ge(merged, SMALL * b + i)
                    hold(dve, turns)
                    nc.vector.copy_predicated(diag[:, :, :, :],
                                              bcast(masks[:, i, :].unsqueeze(1).unsqueeze(1), [P, GH0, NC, SUB]),
                                              hd).then_inc(merged, 1)

                def raise_q(b, i):
                    size = LEVELS[i]
                    dve.wait_ge(level_done, NL * b + i + 1)
                    if i == 1:
                        dve.wait_ge(qp_ready, b + 1)
                    else:
                        dve.wait_ge(up_q, 7 * b + i - 1)
                        dve.wait_ge(up_t, 7 * b + i - 1)
                    n = W2 // (2 * size)
                    right = qp[:, :].rearrange("p (n s l) -> p n s l", s=2, l=size)[:, :, 1, :]
                    tt = total(size).rearrange("p (n s) -> p n s", s=2)
                    nc.vector.tensor_tensor(right, right, bcast(tt[:, :, 0:1], [P, n, size]), ALU.mult).then_inc(up_q, 1)
                    if not first(b):
                        dve.wait_ge(up_k, 7 * b)
                    nc.vector.tensor_tensor(total(2 * size), tt[:, :, 0], tt[:, :, 1], ALU.mult).then_inc(up_t, 1)

                def g1_low(b):
                    dve.wait_ge(ghi_ready, b + 1)
                    nc.vector.tensor_tensor(glo[:, :], ab[:, 0, :], as_f32(ghi[:, :]), ALU.subtract).then_inc(glo_ready, 1)
                    dve.wait_ge(glo_ready, b + 1)
                    dve.sem_inc(a_free[0], 1)

                def states(b):
                    dve.wait_ge(s0_ready, b + 1)
                    dve.wait_ge(up_t, 7 * b + 7)
                    decay = total(CHUNK).rearrange("p (h c) -> p h c", h=GH0)
                    for c in range(1, NC - 1):
                        for h in range(GH0):
                            op = nc.vector.scalar_tensor_tensor(st[:, h, c, :], st[:, h, c - 1, :], decay[:, h, c:c + 1],
                                                                hb[:, h, c * P:(c + 1) * P], ALU.mult, ALU.add)
                        if c < NC - 2:
                            op.then_inc(st_step, 1)
                            dve.wait_ge(st_step, b + 1)
                    op.then_inc(st_ready, 1)

                def o_low(b):
                    dve.wait_ge(oh_ready, b + 1)
                    nc.vector.tensor_tensor(ol[:, :, :], tp[:, :, :], as_f32(oh[:, :, :]), ALU.subtract).then_inc(ol_ready, 1)

                def update(b):
                    dve.wait_ge(y_ps, b + 1)
                    xs = core.x[:, bass.ds(b * TILES, TILES), :]
                    nc.vector.tensor_tensor(xs, xs, aby, ALU.add).then_inc(x_done, 1)
                    dve.wait_ge(x_done, b + 1)
                    dve.sem_inc(a_free[0], 1)
                    dve.sem_inc(a_free[1], 1)
                    stats.take(dve, b, lambda: dve.wait_ge(x_done, b + 1))

                st_step = s(name + "_st_step")

                def body(b, before, more):
                    if before:
                        gated(b - 1)
                    q_silu(b, 0)
                    q_silu(b, 1)
                    q_first(b)
                    if before:
                        o_norm(b - 1)
                    merge(b, 0)
                    merge(b, 1)
                    raise_q(b, 1)
                    g1_low(b)
                    merge(b, 2)
                    raise_q(b, 2)
                    merge(b, 3)
                    raise_q(b, 3)
                    if before:
                        o_low(b - 1)
                    merge(b, 4)
                    raise_q(b, 4)
                    merge(b, 5)
                    raise_q(b, 5)
                    raise_q(b, 6)
                    if before:
                        update(b - 1)
                    raise_q(b, 7)
                    if more:
                        norm.normalise(dve, b + 1)
                        norm.low(dve, b + 1)
                    states(b)

                over_sequences(dve, core.batches, body)
                last = core.batches - 1
                gated(last)
                o_norm(last)
                o_low(last)
                update(last)


def final_store(core, out_dram):
    stored = core.sem("x_stored")
    rows = out_dram.rearrange("(n p) d -> p n d", p=P)
    with core.nc.Block() as block:

        @block.sync
        def _(sp):
            sp.dma_start(rows, core.x[:, :, :]).then_inc(stored, 16)
            sp.wait_ge(stored, 16)


def program(nc, a, out, batches=16, stages=("ffn", "gla", "ffn", "moe", "att", "moe")):
    with ExitStack() as ctx:
        core = Core(nc, ctx, batches)
        constants(core, a["x"])
        core.end_stage()
        weights = None
        with ExitStack() as ffn_ctx:
            for i, stage in enumerate(stages):
                name = f"{stage}{i}"
                if stage == "ffn":
                    if weights is None:
                        weights = FfnWeights(core, ffn_ctx)
                        ffn_weights(core, weights, [a[k] for k in ("w_fc", "w_proj", "u_t", "v", "fast_bt", "gate")], name)
                    ffn_stage(core, weights, name)
                elif stage == "gla":
                    gla_stage(core, a, name)
                else:
                    break
                core.end_stage()
        for i, stage in enumerate(stages):
            name = f"{stage}{i}"
            if stage == "moe":
                moe_stage(core, a, name)
            elif stage == "att":
                att_stage(core, a, name)
            else:
                continue
            core.end_stage()
        final_store(core, out)


def layout(i):
    import numpy as np

    def f32(a):
        return np.ascontiguousarray(np.asarray(a))

    arrays = {
        "x": f32(i["L0_attn_x"]).reshape(-1, 256),
        "w_fc": f32(i["L0_ffn_w_fc"]),
        "w_proj": f32(i["L0_ffn_w_proj"]),
        "u_t": f32(np.asarray(i["L0_ffn_u"]).T),
        "v": f32(i["L0_ffn_v"]),
        "fast_bt": f32(np.asarray(i["L0_ffn_fast_b"]).T),
        "gate": f32(i["L0_ffn_gate"]).reshape(1, 1),
        "w_in_t": f32(np.asarray(i["L0_attn_W_in"]).T),
        "w_out_t": f32(np.asarray(i["L0_attn_W_out"]).T),
        "w_g1_t": f32(np.asarray(i["L0_attn_W_g1"]).T),
        "w_g2_t": f32(np.asarray(i["L0_attn_W_g2"]).T),
        "ln_w": f32(i["L0_attn_ln_w"]).reshape(-1, 1),
        "router_w": f32(i["L1_ffn_router_w"]),
        "router_b": f32(i["L1_ffn_router_b"]).reshape(1, -1),
        "routed_w1": f32(i["L1_ffn_routed_w1"]),
        "routed_w3": f32(i["L1_ffn_routed_w3"]),
        "routed_w2": f32(i["L1_ffn_routed_w2"]),
        "shared_w1": f32(i["L1_ffn_shared_w1"]),
        "shared_w3": f32(i["L1_ffn_shared_w3"]),
        "shared_w2": f32(i["L1_ffn_shared_w2"]),
    }
    arrays["level_masks"] = level_masks()
    for n in ("Wq", "Wk", "Wv", "Wo"):
        arrays[n.lower() + "_t"] = f32(np.asarray(i["L1_attn_" + n]).T)
    for n in ("bq", "bk", "bv", "bo", "ocr_bias"):
        arrays[n] = f32(i["L1_attn_" + n]).reshape(1, -1)
    return arrays


def kernel(**inputs):
    import concourse.bacc as _bacc
    from concourse import mybir as _mybir
    from concourse.bass_utils import run_bass_kernel_spmd as _run

    nc = _bacc.Bacc("TRN2", target_bir_lowering=False, num_devices=1)
    arrays = layout(inputs)
    args = {name: nc.dram_tensor(name, a.shape, _mybir.dt.from_np(a.dtype), kind="ExternalInput").ap()
            for name, a in arrays.items()}
    out = nc.dram_tensor("out", arrays["x"].shape, _mybir.dt.float32, kind="ExternalOutput").ap()
    program(nc, args, out)
    r = _run(nc, [arrays], core_ids=[0])
    return r.results[0]["out"].reshape(16, 512, 256)
```

```python
import math
from contextlib import ExitStack

import concourse.bass as bass
from concourse import mybir

F32 = mybir.dt.float32
F32R = mybir.dt.float32r
U8 = mybir.dt.uint8
ALU = mybir.AluOpType
ACT = mybir.ActivationFunctionType
AXIS_X = mybir.AxisListType.X

P = 128
TOKENS = 512
TILES = TOKENS // P
DM = 256
KT = DM // P
LN_EPS = 1e-5


class Core:

    def __init__(self, nc, ctx, batches):
        self.nc, self.batches = nc, batches
        self.ctx = ctx
        self.made = 0
        self.stage_sems = []
        sb = self.sbuf
        n = batches * TILES
        self.x = sb("x_resident", [P, n, DM])
        self.stat6 = sb("ln_stat6", [P, TILES, 6])
        self.mv4 = sb("ln_mean_var4", [P, TILES, 2])
        self.mv = sb("ln_mean_var", [P, n, 2])
        self.rstd = sb("ln_rstd", [P, n, 1])
        self.eps = sb("ln_eps", [P, 1])
        self.ident = sb("identity", [P, P])
        self.ones = sb("ones", [P, P])
        self.xn = sb("xn", [P, TILES, DM])
        self.xh = sb("xnT_hi", [P, KT, TOKENS], F32R)
        self.xl = sb("xnT_lo", [P, KT, TOKENS], F32R)

    def sbuf(self, name, shape, dt=F32, ctx=None):
        self.made += 1
        return (ctx or self.ctx).enter_context(self.nc.sbuf_tensor(f"{name}_sb{self.made}", shape, dt))

    def psum(self, name, shape, ctx):
        self.made += 1
        return ctx.enter_context(self.nc.psum_tensor(f"{name}_ps{self.made}", shape, F32))

    def sem(self, name):
        self.stage_sems.append(self.nc.alloc_semaphore(name=name))
        return self.stage_sems[-1]

    def end_stage(self):
        self.nc.clear_and_free_semaphores(self.stage_sems)
        self.nc.all_engine_barrier()
        self.stage_sems = []


def hold(engine, turns):
    engine.sem_inc(turns, 1)


def as_f32(ap):
    return ap.bitcast(F32)


def bcast(ap, shape):
    return ap.to_broadcast(shape)


def constants(core):
    nc, s = core.nc, core.sem
    ident_zero = s("ident_zero")
    with nc.Block() as block:

        @block.gpsimd
        def _(pool):
            nc.gpsimd.memset(core.ident[:, :], 0.0).then_inc(ident_zero, 1)
            nc.gpsimd.memset(core.ones[:, :], 1.0)
            nc.gpsimd.memset(core.eps[:, :], LN_EPS)
            pool.wait_ge(ident_zero, 1)
            nc.gpsimd.affine_select(out=core.ident[:, :], in_=core.ident[:, :], compare_op=ALU.not_equal,
                                    fill=1.0, base=0, pattern=[[-1, P]], channel_multiplier=1)


class Norm:

    def __init__(self, core, name, banks, ctx=None):
        self.c = core
        self.xh, self.xl = [core.xh], [core.xl]
        if ctx is not None:
            self.xh.append(core.sbuf("xnT_hi2", [P, KT, TOKENS], F32R, ctx))
            self.xl.append(core.sbuf("xnT_lo2", [P, KT, TOKENS], F32R, ctx))
        self.tp = banks
        self.xn_ready = core.sem(name + "_xn_ready")
        self.tp_ready = core.sem(name + "_tp_ready")
        self.xh_ready = core.sem(name + "_xh_ready")
        self.xl_ready = core.sem(name + "_xl_ready")

    def normalise(self, dve, b, tiles=range(TILES)):
        c = self.c
        if not (isinstance(b, int) and b == 0) and tiles[0] == 0:
            dve.wait_ge(self.tp_ready, b)
        for t in tiles:
            n = b * TILES + t
            op = c.nc.vector.tensor_scalar(c.xn[:, t, :], c.x[:, n, :], c.mv[:, n, 0:1], c.rstd[:, n, :],
                                           ALU.subtract, ALU.mult)
        if tiles[-1] == TILES - 1:
            op.then_inc(self.xn_ready, 1)

    def transpose(self, pe, b, tp_free=None, halves=range(KT)):
        c = self.c
        if halves[0] == 0:
            pe.wait_ge(self.xn_ready, b + 1)
            if not (isinstance(b, int) and b == 0):
                pe.wait_ge(self.xl_ready, b)
            if tp_free is not None:
                tp_free()
        for k in halves:
            for t in range(TILES):
                op = c.nc.tensor.transpose(self.tp[:, k, t * P:(t + 1) * P], c.xn[:, t, k * P:(k + 1) * P],
                                           c.ident[:, :])
        if halves[-1] == KT - 1:
            op.then_inc(self.tp_ready, 1)

    def high(self, act, b, readers_done=None, halves=range(KT), p=0):
        c = self.c
        k = slice(halves[0], halves[-1] + 1)
        if k.start == 0:
            act.wait_ge(self.tp_ready, b + 1)
            if readers_done is not None:
                readers_done()
        op = c.nc.scalar.copy(self.xh[p][:, k, :], self.tp[:, k, :])
        if k.stop == KT:
            op.then_inc(self.xh_ready, 1)

    def low(self, dve, b, halves=range(KT), p=0):
        c = self.c
        k = slice(halves[0], halves[-1] + 1)
        if k.start == 0:
            dve.wait_ge(self.xh_ready, b + 1)
        op = c.nc.vector.tensor_tensor(self.xl[p][:, k, :], self.tp[:, k, :], as_f32(self.xh[p][:, k, :]), ALU.subtract)
        if k.stop == KT:
            op.then_inc(self.xl_ready, 1)


def rstd_block(core, name):
    nc = core.nc
    sqrt_ready = core.sem(name + "_sqrt_ready")
    with nc.Block() as block:

        @block.scalar
        def _(act):
            nc.scalar.activation(core.rstd[:, :, 0], core.mv[:, :, 1], ACT.Sqrt,
                                 bias=core.eps[:, 0:1]).then_inc(sqrt_ready, 1)

        @block.vector
        def _(dve):
            dve.wait_ge(sqrt_ready, 1)
            nc.vector.reciprocal(core.rstd[:, :, 0], core.rstd[:, :, 0])


class Stats:

    def __init__(self, core, name):
        self.c = core
        self.stats = core.sem(name + "_bn_stats_ready")
        self.turns = core.sem(name + "_stats_turns")
        self.aggr = core.sem(name + "_bn_aggr_ready")

    def tiles(self, dve, b, updated, tiles=range(TILES)):
        c = self.c
        if tiles[0] == 0:
            updated()
            hold(dve, self.turns)
        for t in tiles:
            op = c.nc.vector.bn_stats(c.stat6[:, t, :], c.x[:, b * TILES + t, :])
        if tiles[-1] == TILES - 1:
            op.then_inc(self.stats, 1)

    def finish(self, dve, b):
        c = self.c
        dve.wait_ge(self.stats, b + 1)
        hold(dve, self.turns)
        for t in range(TILES):
            op = c.nc.vector.bn_aggr(c.mv4[:, t, :], c.stat6[:, t, :])
        op.then_inc(self.aggr, 1)
        dve.wait_ge(self.aggr, 2 * b + 1)
        c.nc.vector.tensor_scalar(c.mv[:, bass.ds(b * TILES, TILES), :], c.mv4[:, :, :], 0.0, None,
                                  ALU.add).then_inc(self.aggr, 1)

    def take(self, dve, b, updated):
        self.tiles(dve, b, updated)
        self.finish(dve, b)


def over_sequences(engine, batches, body):
    body(0, False, batches > 1)
    if batches > 2:
        with engine.Fori(1, batches - 1) as b:
            body(b, True, True)
    if batches > 1:
        body(batches - 1, True, False)


def over_pairs(engine, batches, body):
    body(0, 0, False, batches > 1)
    if batches > 2:
        assert batches % 2 == 0
        with engine.Fori(0, batches // 2 - 1) as pair:
            body(pair * 2 + 1, 1, True, True)
            body(pair * 2 + 2, 0, True, True)
    if batches > 1:
        body(batches - 1, 1, True, False)


HIDDEN = 1024
JT = HIDDEN // P
RANK = 16
X_PARTS = 4
SCALE_MIN = 1e-5


class FfnWeights:
    def __init__(self, core, ctx):
        self.fc_h = core.sbuf("w_fc_hi", [P, KT, HIDDEN], F32R, ctx)
        self.fc_l = core.sbuf("w_fc_lo", [P, KT, HIDDEN], F32R, ctx)
        self.proj = core.sbuf("w_proj_tern", [P, JT, DM], F32R, ctx)
        self.half_scale = core.sbuf("half_scale", [P, DM], F32, ctx)


def ffn_weights(core, w, dram, x_dram, name):
    nc, s = core.nc, core.sem
    w_fc, w_proj, u_t, v, fast_bt, gate = dram
    loaded = s(name + "_w_loaded")
    dve_step = s(name + "_w_dve_step")
    lowrank_ready = s(name + "_w_lowrank")
    tr_ready, high_ready, low_ready = s(name + "_w_transposed"), s(name + "_w_high"), s(name + "_w_low")
    bv_ready, row_ready, ptr_ready, pcopy = s(name + "_w_bv"), s(name + "_w_row"), s(name + "_w_ptr"), s(name + "_w_pcopy")
    fc_done = s(name + "_w_fc_done")
    proj_done = s(name + "_w_proj_done")
    x_loaded = [s(f"{name}_x_loaded{i}") for i in range(X_PARTS)]
    n_x = core.batches * TILES // X_PARTS
    with ExitStack() as ctx:
        wf = core.sbuf("wf_nat", [P, JT, DM], F32, ctx)
        wp = core.sbuf("wp_nat", [P, KT, HIDDEN], F32, ctx)
        ut = core.sbuf("u_t", [RANK, HIDDEN], F32, ctx)
        vs = core.sbuf("v_sb", [RANK, DM], F32, ctx)
        bt = core.sbuf("fast_bt", [RANK, RANK], F32, ctx)
        gt = core.sbuf("gate_sb", [RANK, 1], F32, ctx)
        bv = core.sbuf("gate_b_v", [RANK, DM], F32, ctx)
        neg = core.sbuf("w_neg", [P, HIDDEN], F32, ctx)
        tern = core.sbuf("w_tern", [P, HIDDEN], F32, ctx)
        NS = JT + KT
        ssum = core.sbuf("s_sum", [P, NS], F32, ctx)
        scale = core.sbuf("s_scale", [P, NS], F32, ctx)
        ph = core.sbuf("s_half", [P, NS], F32, ctx)
        nh = core.sbuf("s_neg_half", [P, NS], F32, ctx)
        weff = core.sbuf("w_eff", [P, JT, DM], F32, ctx)
        ptern = core.sbuf("p_tern", [P, KT, HIDDEN], F32, ctx)
        diag = core.sbuf("s_diag", [P, KT, P], F32, ctx)
        ps = [core.psum(f"wps{i}", [P, 512], ctx) for i in range(4)]
        with nc.Block() as block:

            @block.sync
            def _(sp):
                sp.dma_start(wf[:, :, :], w_fc.rearrange("(j p) d -> p j d", p=P)).then_inc(loaded, 16)
                sp.dma_start(wp[:, :, :], w_proj.rearrange("(k p) h -> p k h", p=P)).then_inc(loaded, 16)
                sp.dma_start(ut[:, :], u_t).then_inc(loaded, 16)
                sp.dma_start(vs[:, :], v).then_inc(loaded, 16)
                sp.dma_start(bt[:, :], fast_bt).then_inc(loaded, 16)
                sp.dma_start(gt[:, :], gate.to_broadcast([RANK, 1])).then_inc(loaded, 16)
                rows = x_dram.rearrange("(n p) d -> p n d", p=P)
                for i in range(X_PARTS):
                    part = slice(i * n_x, (i + 1) * n_x)
                    sp.dma_start(core.x[:, part, :], rows[:, part, :]).then_inc(x_loaded[i], 16)

            ALL = 16 * 6

            @block.tensor
            def _(pe):
                pe.wait_ge(loaded, ALL)
                nc.tensor.matmul(ps[0][0:RANK, 0:DM], bt[:, :], vs[:, :], start=True, stop=True).then_inc(bv_ready, 1)
                for j in range(JT):
                    pe.wait_ge(bv_ready, 2)
                    if j >= 2:
                        pe.wait_ge(fc_done, j - 1)
                    nc.tensor.matmul(ps[2 + j % 2][:, 0:DM], ut[:, j * P:(j + 1) * P], bv[:, :],
                                     start=True, stop=True).then_inc(lowrank_ready, 1)
                n = 0
                for j in range(JT):
                    pe.wait_ge(fc_done, j + 1)
                    if n >= 2:
                        pe.wait_ge(low_ready, n - 1)
                    for k in range(KT):
                        op = nc.tensor.transpose(ps[n % 2][:, k * P:(k + 1) * P], weff[:, j, k * P:(k + 1) * P],
                                                 core.ident[:, :])
                    op.then_inc(tr_ready, 1)
                    n += 1
                pe.wait_ge(proj_done, 1)
                for j in range(JT):
                    if j < 2:
                        pe.wait_ge(low_ready, JT)
                    else:
                        pe.wait_ge(pcopy, j - 1)
                    for k in range(KT):
                        op = nc.tensor.transpose(ps[j % 2][:, k * P:(k + 1) * P], ptern[:, k, j * P:(j + 1) * P],
                                                 core.ident[:, :])
                    op.then_inc(ptr_ready, 1)
                for k in range(KT):
                    op = nc.tensor.matmul(ps[2][:, k * P:(k + 1) * P], core.ones[:, :], diag[:, k, :],
                                          start=True, stop=True)
                op.then_inc(row_ready, 1)

            @block.scalar
            def _(act):
                for j in range(JT):
                    act.wait_ge(tr_ready, j + 1)
                    nc.scalar.copy(w.fc_h[:, :, j * P:(j + 1) * P],
                                   ps[j % 2][:, 0:DM].rearrange("p (k m) -> p k m", k=KT)).then_inc(high_ready, 1)
                for j in range(JT):
                    act.wait_ge(ptr_ready, j + 1)
                    nc.scalar.copy(w.proj[:, j, :], ps[j % 2][:, 0:DM]).then_inc(pcopy, 1)
                act.wait_ge(row_ready, 1)
                nc.scalar.mul(w.half_scale[:, :], ps[2][:, 0:DM], 0.5)

            @block.vector
            def _(dve):
                count = [0]

                def link(op):
                    count[0] += 1
                    op.then_inc(dve_step, 1)
                    dve.wait_ge(dve_step, count[0])

                dve.wait_ge(loaded, ALL)
                dve.wait_ge(bv_ready, 1)
                nc.vector.tensor_scalar(bv[:, :], ps[0][0:RANK, 0:DM], gt[:, 0:1], None, ALU.mult).then_inc(bv_ready, 1)
                blocks = [(wf[:, j, :], DM) for j in range(JT)] + [(wp[:, k, :], HIDDEN) for k in range(KT)]
                for i, (a, n) in enumerate(blocks):
                    link(nc.vector.tensor_reduce(ssum[:, i:i + 1], a, AXIS_X, ALU.add, apply_absolute_value=True))
                link(nc.vector.tensor_scalar(scale[:, 0:JT], ssum[:, 0:JT], 1.0 / DM, SCALE_MIN, ALU.mult, ALU.max))
                link(nc.vector.tensor_scalar(scale[:, JT:NS], ssum[:, JT:NS], 1.0 / HIDDEN, SCALE_MIN, ALU.mult, ALU.max))
                link(nc.vector.tensor_scalar(ph[:, :], scale[:, :], 0.5, None, ALU.mult))
                link(nc.vector.tensor_scalar(nh[:, :], scale[:, :], -0.5, None, ALU.mult))
                for i, (a, n) in enumerate(blocks):
                    link(nc.vector.tensor_scalar(neg[:, 0:n], a, nh[:, i:i + 1], None, ALU.is_lt))
                    out = tern[:, 0:n] if i < JT else ptern[:, i - JT, :]
                    link(nc.vector.scalar_tensor_tensor(out, a, ph[:, i:i + 1], neg[:, 0:n], ALU.is_gt, ALU.subtract))
                    if i < JT:
                        dve.wait_ge(lowrank_ready, i + 1)
                        nc.vector.scalar_tensor_tensor(weff[:, i, :], tern[:, 0:n], scale[:, i:i + 1],
                                                       ps[2 + i % 2][:, 0:DM], ALU.mult, ALU.add).then_inc(fc_done, 1)
                        dve.wait_ge(fc_done, i + 1)
                for k in range(KT):
                    op = nc.vector.tensor_scalar(diag[:, k, :], core.ident[:, :], scale[:, JT + k:JT + k + 1], None,
                                                 ALU.mult)
                op.then_inc(proj_done, 1)
                for j in range(JT):
                    dve.wait_ge(high_ready, j + 1)
                    nc.vector.tensor_tensor(w.fc_l[:, :, j * P:(j + 1) * P],
                                            ps[j % 2][:, 0:DM].rearrange("p (k m) -> p k m", k=KT),
                                            as_f32(w.fc_h[:, :, j * P:(j + 1) * P]), ALU.subtract).then_inc(low_ready, 1)
    return x_loaded


def ffn_stage(core, w, name, x_loaded=None):
    nc, s = core.nc, core.sem
    RING, LAG = JT, 4
    fresh = x_loaded is not None
    J0 = 2 if fresh else 1
    if fresh:
        x_ready = s(name + "_x_ready")
        sd_ready = s(name + "_sd_ready")
        rs_ready = s(name + "_rs_ready")
        turns = s(name + "_turns")
        own = Stats(core, name + "_own")
    else:
        rstd_block(core, name)
    h_ready = s(name + "_h_ready")
    r_ready = s(name + "_relu_ready")
    sq_ready = s(name + "_sq_ready")
    high_ready = s(name + "_high_ready")
    low_ready = s(name + "_low_ready")
    proj_done = s(name + "_proj_done")
    y_free = s(name + "_y_free")
    x_done = s(name + "_x_updated")
    with ExitStack() as ctx:
        hp = [core.psum(f"{name}_hp{i}", [P, TOKENS], ctx) for i in range(2)]
        ypair = [core.psum(f"{name}_y{i}", [P, TILES, DM], ctx) for i in range(2)]
        tp = core.psum(f"{name}_tp", [P, KT, TOKENS], ctx)
        relu = core.sbuf("f_relu", [P, 2, TOKENS], F32, ctx)
        sq = core.sbuf("f_sq", [P, 2, TOKENS], F32, ctx)
        sqh = core.sbuf("f_sq_hi", [P, RING, TOKENS], F32R, ctx)
        sql = core.sbuf("f_sq_lo", [P, RING, TOKENS], F32R, ctx)
        ys = core.sbuf("f_y_scaled", [P, TILES, DM], F32, ctx)
        norm = Norm(core, name, tp, ctx)
        stats = Stats(core, name)
        with nc.Block() as block:

            @block.sync
            def _(sp):
                if fresh:
                    for loaded in x_loaded:
                        sp.wait_ge(loaded, 16)
                        sp.sem_inc(x_ready, core.batches // X_PARTS)

            @block.tensor
            def _(pe):
                norm.transpose(pe, 0)
                pe.sem_inc(proj_done, RING)

                def fc(b, p, j):
                    if j == 0:
                        pe.wait_ge(norm.xl_ready, b + 1)
                    pe.wait_ge(sq_ready, b * JT + j + 1)
                    mm = [(w.fc_h, norm.xh[p]), (w.fc_l, norm.xh[p]), (w.fc_h, norm.xl[p])]
                    for k in range(KT):
                        for i, (a, x) in enumerate(mm):
                            op = nc.tensor.matmul(hp[j % 2][:, :], a[:, k, j * P:(j + 1) * P], x[:, k, :],
                                                  start=(k == 0 and i == 0), stop=(k == KT - 1 and i == 2))
                    op.then_inc(h_ready, 1)

                def proj(b, p, j):
                    y = ypair[p]
                    pe.wait_ge(low_ready, b * JT + j + 3)
                    if j == 0:
                        pe.wait_ge(y_free, b + 1)
                    for t in range(TILES):
                        for i, r in enumerate((sqh, sql)):
                            op = nc.tensor.matmul(y[:, t, :], r[:, j, t * P:(t + 1) * P], w.proj[:, j, :],
                                                  start=(j == 0 and t % 2 == 0 and i == 0),
                                                  stop=(j == JT - 1 and i == 1), skip_group_check=True)
                    op.then_inc(proj_done, 1)

                def body(b, p, before, more):
                    for j in range(JT):
                        fc(b, p, j)
                        if j >= LAG:
                            proj(b, p, j - LAG)
                        elif before:
                            proj(b - 1, 1 - p, JT - LAG + j)
                        if more and j == J0 + 2:
                            norm.transpose(pe, b + 1)

                over_pairs(pe, core.batches, body)
                last = core.batches - 1
                for j in range(JT - LAG, JT):
                    proj(last, last % 2, j)

            @block.scalar
            def _(act):
                def deviation(b):
                    act.wait_ge(own.aggr, 2 * b + 2)
                    hold(act, turns)
                    tiles = bass.ds(b * TILES, TILES)
                    nc.scalar.activation(core.rstd[:, tiles, 0], core.mv[:, tiles, 1], ACT.Sqrt,
                                         bias=core.eps[:, 0:1]).then_inc(sd_ready, 1)

                if fresh:
                    deviation(0)
                norm.high(act, 0)

                def relu_of(b, j):
                    act.wait_ge(h_ready, b * JT + j + 1)
                    nc.scalar.activation(relu[:, j % 2, :], hp[j % 2][:, :], ACT.Relu).then_inc(r_ready, 1)

                def high_of(b, j):
                    act.wait_ge(sq_ready, b * JT + j + 3)
                    act.wait_ge(proj_done, b * JT + j + 1)
                    nc.scalar.copy(sqh[:, j, :], sq[:, j % 2, :]).then_inc(high_ready, 1)

                def body(b, p, before, more):
                    for j in range(JT):
                        relu_of(b, j)
                        if fresh and more and j == 1:
                            deviation(b + 1)
                        if j >= 1:
                            high_of(b, j - 1)
                        elif before:
                            high_of(b - 1, JT - 1)
                        if more and j in (J0 + 3, J0 + 4):
                            norm.high(act, b + 1, halves=range(j - J0 - 3, j - J0 - 2), p=1 - p)

                over_pairs(act, core.batches, body)
                high_of(core.batches - 1, JT - 1)

            @block.gpsimd
            def _(pool):
                pool.sem_inc(low_ready, 2)

                def body(b, before, more):
                    for j in range(JT):
                        pool.wait_ge(high_ready, b * JT + j + 1)
                        nc.gpsimd.tensor_tensor(sql[:, j, :], sq[:, j % 2, :], as_f32(sqh[:, j, :]),
                                                ALU.subtract).then_inc(low_ready, 1)
                        if before and j == 4:
                            add(b - 1)

                def add(b):
                    pool.wait_ge(y_free, b + 3)
                    xs = core.x[:, bass.ds(b * TILES, TILES), :]
                    nc.gpsimd.tensor_tensor(xs, xs, ys[:, :, :], ALU.add).then_inc(x_done, 1)

                over_sequences(pool, core.batches, body)
                add(core.batches - 1)

            @block.vector
            def _(dve):
                dve.sem_inc(sq_ready, 2)
                dve.sem_inc(y_free, 2)

                def own_stats(b):
                    own.take(dve, b, lambda: dve.wait_ge(x_ready, b + 1))

                def reciprocals(b):
                    dve.wait_ge(sd_ready, b + 1)
                    hold(dve, turns)
                    r = core.rstd[:, bass.ds(b * TILES, TILES), 0]
                    nc.vector.reciprocal(r, r).then_inc(rs_ready, 1)
                    dve.wait_ge(rs_ready, b + 1)

                if fresh:
                    own_stats(0)
                    reciprocals(0)
                norm.normalise(dve, 0)
                norm.low(dve, 0)

                def square(b, j):
                    dve.wait_ge(r_ready, b * JT + j + 1)
                    dve.wait_ge(low_ready, b * JT + j + 1)
                    nc.vector.tensor_tensor(sq[:, j % 2, :], hp[j % 2][:, :], relu[:, j % 2, :],
                                            ALU.mult).then_inc(sq_ready, 1)

                def scale(b, p):
                    dve.wait_ge(proj_done, b * JT + JT + RING)
                    nc.vector.tensor_tensor(ys[:, :, :], ypair[p][:, :, :],
                                            bcast(w.half_scale[:, :].unsqueeze(1), [P, TILES, DM]),
                                            ALU.mult).then_inc(y_free, 1)

                def body(b, p, before, more):
                    for j in range(JT):
                        if more and j in (J0 + 4, J0 + 5):
                            norm.low(dve, b + 1, range(j - J0 - 4, j - J0 - 3), 1 - p)
                        square(b, j)
                        if before and j == 4:
                            scale(b - 1, 1 - p)
                        if before and j in (6, 7):
                            stats.tiles(dve, b - 1, lambda: dve.wait_ge(x_done, b), range(2 * j - 12, 2 * j - 10))
                        if before and j == 7:
                            stats.finish(dve, b - 1)
                        if fresh and more and j == 0:
                            own_stats(b + 1)
                        if fresh and more and j == J0:
                            reciprocals(b + 1)
                        if more and j in (J0, J0 + 1):
                            half = 2 * (j - J0)
                            norm.normalise(dve, b + 1, range(half, half + 2))

                over_pairs(dve, core.batches, body)
                last = core.batches - 1
                scale(last, last % 2)
                stats.take(dve, core.batches - 1, lambda: dve.wait_ge(x_done, core.batches))


EXPERTS, SHARED = 8, 2
ALL_EXPERTS = EXPERTS + SHARED
TOP_K = 2


def prepare(core, name, parts):
    nc, s = core.nc, core.sem
    loaded = [s(f"{name}_w_loaded{i}") for i in range(len(parts))]
    sqrt_ready, gained, high = s(name + "_sqrt_ready"), s(name + "_w_gained"), s(name + "_w_high")
    gains = [len(part) > 3 for part in parts]
    with ExitStack() as inner:
        gain = core.sbuf(name + "_gain", [P, KT], F32, inner)
        values = [core.sbuf(f"{name}_w_values{i}", list(part[1].shape), F32, inner) for i, part in enumerate(parts)]
        values = [v[:, :] if len(v.shape) == 2 else v[:, :, :] for v in values]
        with nc.Block() as block:

            @block.sync
            def _(sp):
                for i, (src, hi, lo, *factors) in enumerate(parts):
                    sp.dma_start(values[i], src).then_inc(loaded[i], 16)
                    for f in factors:
                        for k in range(KT):
                            sp.dma_start(gain[:, k:k + 1], f[k * P:(k + 1) * P, :]).then_inc(loaded[i], 16)

            @block.scalar
            def _(act):
                nc.scalar.activation(core.rstd[:, :, 0], core.mv[:, :, 1], ACT.Sqrt,
                                     bias=core.eps[:, 0:1]).then_inc(sqrt_ready, 1)
                for i, (src, hi, lo, *factors) in enumerate(parts):
                    if gains[i]:
                        act.wait_ge(gained, sum(gains[:i + 1]))
                    else:
                        act.wait_ge(loaded[i], 16)
                    nc.scalar.copy(hi, values[i]).then_inc(high, 1)

            @block.vector
            def _(dve):
                dve.wait_ge(sqrt_ready, 1)
                nc.vector.reciprocal(core.rstd[:, :, 0], core.rstd[:, :, 0])
                for i, (src, hi, lo, *factors) in enumerate(parts):
                    v = values[i]
                    if gains[i]:
                        dve.wait_ge(loaded[i], 16 * (1 + KT))
                        for k in range(KT):
                            op = nc.vector.tensor_scalar(v[:, k, :], v[:, k, :], gain[:, k:k + 1], None, ALU.mult)
                        op.then_inc(gained, 1)
                    dve.wait_ge(high, i + 1)
                    nc.vector.tensor_tensor(lo, v, as_f32(hi), ALU.subtract)


def moe_stage(core, a, name, out=None):
    nc, s = core.nc, core.sem
    E, H = ALL_EXPERTS, P
    RING, LAG = 6, 2
    with ExitStack() as ctx:
        w1h, w1l, w3h, w3l = (core.sbuf(n, [P, E, KT, H], F32R, ctx) for n in ("w1h", "w1l", "w3h", "w3l"))
        w2h, w2l = (core.sbuf(n, [P, E, DM], F32R, ctx) for n in ("w2h", "w2l"))
        rw = core.sbuf("router_w_hi_lo", [P, KT, 2, EXPERTS], F32R, ctx)
        parts = [(a["router_w"].rearrange("(k p) e -> p k e", p=P), rw[:, :, 0, :], rw[:, :, 1, :])]
        for kind, lo, hi in (("routed", 0, 4), ("routed", 4, 8), ("shared", EXPERTS, E)):
            src = slice(lo, hi) if kind == "routed" else slice(0, SHARED)
            for n, h, l in (("w1", w1h, w1l), ("w3", w3h, w3l)):
                parts.append((a[f"{kind}_{n}"][src].rearrange("e (k p) h -> p (e k) h", p=P),
                              *(x[:, lo:hi, :, :].rearrange("p e k h -> p (e k) h") for x in (h, l))))
            parts.append((a[f"{kind}_w2"][src].rearrange("e h d -> h e d"), w2h[:, lo:hi, :], w2l[:, lo:hi, :]))
        prepare(core, name, parts)

        rb = core.sbuf("router_b", [P, EXPERTS], F32, ctx)
        earlier = core.sbuf("earlier", [P, EXPERTS, EXPERTS], F32, ctx)
        rb_loaded, earlier_one, earlier_ready = s(name + "_rb_loaded"), s(name + "_e_one"), s(name + "_earlier")
        lg = core.sbuf("logits", [P, TILES, EXPERTS], F32, ctx)
        big = [TILES, EXPERTS, EXPERTS]
        above, notless = core.sbuf("above", [P] + big, F32, ctx), core.sbuf("notless", [P] + big, F32, ctx)
        rank = core.sbuf("rank", [P, TILES, EXPERTS], F32, ctx)
        chosen = core.sbuf("chosen", [P, TILES, EXPERTS], F32, ctx)
        picked = core.sbuf("picked", [P, TILES, EXPERTS], F32, ctx)
        both = core.sbuf("both", [P, TILES, 1], F32, ctx)
        margin = core.sbuf("margin", [P, TILES, EXPERTS], F32, ctx)
        share = core.sbuf("share", [P, TILES, EXPERTS], F32, ctx)
        gates = core.sbuf("gates", [P, TILES, EXPERTS], F32, ctx)
        silu = core.sbuf("m_silu", [P, 2, TOKENS], F32, ctx)
        act_f = core.sbuf("m_act", [P, 2, TOKENS], F32, ctx)
        ah = core.sbuf("m_act_hi", [P, RING, TOKENS], F32R, ctx)
        al = core.sbuf("m_act_lo", [P, RING, TOKENS], F32R, ctx)
        h1 = [core.psum(f"{name}_h1{i}", [P, TOKENS], ctx) for i in range(2)]
        h3 = [core.psum(f"{name}_h3{i}", [P, TOKENS], ctx) for i in range(2)]
        y = core.psum(f"{name}_y", [P, TILES, DM], ctx)
        tp = core.psum(f"{name}_tp", [P, KT, TOKENS], ctx)
        logit_ps = tp[:, 0, 0:TILES * 2 * EXPERTS].rearrange("p (t i e) -> p t i e", t=TILES, i=2)

        h_ready = s(name + "_h_ready")
        silu_ready = s(name + "_silu_ready")
        act_ready = s(name + "_act_ready")
        high_ready = s(name + "_high_ready")
        low_ready = s(name + "_low_ready")
        y_ready = s(name + "_y_ready")
        y_free = s(name + "_y_free")
        logits_ready = s(name + "_logits_ready")
        margin_ready = s(name + "_margin_ready")
        share_ready = s(name + "_share_ready")
        route = s(name + "_route_step")
        YS = 2 * (EXPERTS + 1)
        stored, turns = s(name + "_x_stored"), s(name + "_turns")
        norm = Norm(core, name, tp, ctx)
        stats = Stats(core, name)
        ROUTE = 10
        ROUTER_MMS = TILES * KT * 2

        def slot(e):
            return e % RING

        with nc.Block() as block:

            @block.sync
            def _(sp):
                sp.dma_start(rb[:, :], a["router_b"].to_broadcast([P, EXPERTS])).then_inc(rb_loaded, 16)
                if out is not None:
                    rows = out.rearrange("(n p) d -> p n d", p=P)

                    def body(b, before, more):
                        sp.wait_ge(y_free, b * YS + YS + 2)
                        hold(sp, turns)
                        tiles = bass.ds(b * TILES, TILES)
                        sp.dma_start(rows[:, tiles, :], core.x[:, tiles, :]).then_inc(stored, 16)

                    over_sequences(sp, core.batches, body)
                    sp.wait_ge(stored, 16 * core.batches)

            @block.tensor
            def _(pe):
                norm.transpose(pe, 0)

                def router(b, p, n):
                    t, k, low = n // (2 * KT), n // 2 % KT, n % 2
                    if low:
                        op = nc.tensor.matmul(logit_ps[:, t, 0, :], norm.xl[p][:, k, t * P:(t + 1) * P], rw[:, k, 0, :],
                                              start=False, stop=(k == KT - 1), skip_group_check=True)
                    else:
                        op = nc.tensor.matmul(logit_ps[:, t, :, :], norm.xh[p][:, k, t * P:(t + 1) * P], rw[:, k, :, :],
                                              start=(n == 0), stop=(k == KT - 1), skip_group_check=True)
                    if n == ROUTER_MMS - 1:
                        op.then_inc(logits_ready, 1)

                def hidden(b, p, e):
                    if e == 0:
                        pe.wait_ge(norm.xl_ready, b + 1)
                    pe.wait_ge(act_ready, b * E + e + 1)
                    n = 0
                    for wh, wl, out in ((w1h, w1l, h1), (w3h, w3l, h3)):
                        for k in range(KT):
                            for i, (w, x) in enumerate([(wh, norm.xh[p]), (wl, norm.xh[p]), (wh, norm.xl[p])]):
                                op = nc.tensor.matmul(out[e % 2][:, :], w[:, e, k, :], x[:, k, :],
                                                      start=(k == 0 and i == 0), stop=(k == KT - 1 and i == 2))
                                if out is h3 and k == KT - 1 and i == 2:
                                    op.then_inc(h_ready, 1)
                                if e == 0:
                                    for _ in range(1 if n < 8 else 2):
                                        router(b, p, n)
                                        n += 1

                def output(b, e):
                    pe.wait_ge(low_ready, b * E + e + 3)
                    for half in range(2):
                        if e <= EXPERTS:
                            pe.wait_ge(y_free, b * YS + 2 * e + half + 1)
                        for t in (2 * half, 2 * half + 1):
                            for i, (x, w) in enumerate([(ah, w2h), (ah, w2l), (al, w2h)]):
                                op = nc.tensor.matmul(y[:, t, :], x[:, slot(e), t * P:(t + 1) * P], w[:, e, :],
                                                      start=(e <= EXPERTS and t % 2 == 0 and i == 0),
                                                      stop=(i == 2 and e != EXPERTS), skip_group_check=True)
                        if e != EXPERTS:
                            op.then_inc(y_ready, 1)

                def body(b, p, before, more):
                    for e in range(E):
                        hidden(b, p, e)
                        if e >= LAG:
                            output(b, e - LAG)
                        elif before:
                            output(b - 1, E - LAG + e)
                        if more and e == 4:
                            norm.transpose(pe, b + 1, lambda: pe.wait_ge(route, b * ROUTE + 2))

                over_pairs(pe, core.batches, body)
                for e in range(E - LAG, E):
                    output(core.batches - 1, e)

            @block.scalar
            def _(act):
                norm.high(act, 0)

                def silu_of(b, e):
                    act.wait_ge(h_ready, b * E + e + 1)
                    nc.scalar.activation(silu[:, e % 2, :], h1[e % 2][:, :], ACT.Silu).then_inc(silu_ready, 1)

                def high_of(b, e):
                    act.wait_ge(act_ready, b * E + e + 3)
                    if e >= RING:
                        act.wait_ge(y_ready, b * YS + 2 * (e - RING + 1))
                    elif before_any(b):
                        ago = E - 1 - (E - 1 - e) % RING
                        act.wait_ge(y_ready, b * YS - YS + 2 * (min(ago, EXPERTS) + 1))
                    nc.scalar.copy(ah[:, slot(e), :], act_f[:, e % 2, :]).then_inc(high_ready, 1)

                def before_any(b):
                    return not (isinstance(b, int) and b == 0)

                def body(b, p, before, more):
                    for e in range(E):
                        silu_of(b, e)
                        if e >= 1:
                            high_of(b, e - 1)
                        elif before:
                            high_of(b - 1, E - 1)
                        if e == 1:
                            act.wait_ge(margin_ready, b + 1)
                            nc.scalar.activation(share[:, :, :], margin[:, :, :], ACT.Sigmoid).then_inc(share_ready, 1)
                        if more and e in (5, 6):
                            norm.high(act, b + 1, halves=range(e - 5, e - 4), p=1 - p)

                over_pairs(act, core.batches, body)
                high_of(core.batches - 1, E - 1)

            @block.gpsimd
            def _(pool):
                pool.sem_inc(low_ready, 2)
                nc.gpsimd.memset(earlier[:, :, :], 1.0).then_inc(earlier_one, 1)
                pool.wait_ge(earlier_one, 1)
                nc.gpsimd.affine_select(out=earlier[:, :, :], in_=earlier[:, :, :], compare_op=ALU.is_gt, fill=0.0,
                                        base=0, pattern=[[1, EXPERTS], [-1, EXPERTS]],
                                        channel_multiplier=0).then_inc(earlier_ready, 1)

                def body(b, before, more):
                    for e in range(E):
                        pool.wait_ge(high_ready, b * E + e + 1)
                        nc.gpsimd.tensor_tensor(al[:, slot(e), :], act_f[:, e % 2, :], as_f32(ah[:, slot(e), :]),
                                                ALU.subtract).then_inc(low_ready, 1)

                over_sequences(pool, core.batches, body)

            @block.vector
            def _(dve):
                dve.sem_inc(act_ready, 2)
                dve.sem_inc(y_free, 2)
                norm.normalise(dve, 0)
                norm.low(dve, 0)
                dve.wait_ge(rb_loaded, 16)
                dve.wait_ge(earlier_ready, 1)

                def router(b):
                    step = [0]

                    def link(op):
                        step[0] += 1
                        op.then_inc(route, 1)
                        dve.wait_ge(route, b * ROUTE + step[0])

                    dve.wait_ge(logits_ready, b + 1)
                    if not (isinstance(b, int) and b == 0):
                        dve.wait_ge(share_ready, b)
                    link(nc.vector.tensor_tensor(lg[:, :, :], logit_ps[:, :, 0, :],
                                                 bcast(rb[:, :].unsqueeze(1), [P, TILES, EXPERTS]), ALU.add))
                    link(nc.vector.tensor_tensor(lg[:, :, :], logit_ps[:, :, 1, :], lg[:, :, :], ALU.add))
                    other = bcast(lg[:, :, :].unsqueeze(2), [P] + big)
                    own = bcast(lg[:, :, :].unsqueeze(3), [P] + big)
                    nc.vector.tensor_tensor(above[:, :, :, :], other, own, ALU.is_gt)
                    link(nc.vector.tensor_tensor(notless[:, :, :, :], other, own, ALU.is_ge))
                    link(nc.vector.tensor_tensor(notless[:, :, :, :], notless[:, :, :, :],
                                                 bcast(earlier[:, :, :].unsqueeze(1), [P] + big), ALU.mult))
                    link(nc.vector.tensor_tensor(above[:, :, :, :], above[:, :, :, :], notless[:, :, :, :], ALU.max))
                    link(nc.vector.tensor_reduce(rank[:, :, :], above[:, :, :, :], AXIS_X, ALU.add))
                    link(nc.vector.tensor_scalar(chosen[:, :, :], rank[:, :, :], float(TOP_K), None, ALU.is_lt))
                    link(nc.vector.tensor_tensor(picked[:, :, :], chosen[:, :, :], lg[:, :, :], ALU.mult))
                    link(nc.vector.tensor_reduce(both[:, :, :], picked[:, :, :], AXIS_X, ALU.add))
                    nc.vector.scalar_tensor_tensor(margin[:, :, :], lg[:, :, :], 2.0,
                                                   bcast(both[:, :, :], [P, TILES, EXPERTS]), ALU.mult,
                                                   ALU.subtract).then_inc(margin_ready, 1)

                def gate(b):
                    dve.wait_ge(share_ready, b + 1)
                    nc.vector.scalar_tensor_tensor(gates[:, :, :], share[:, :, :], 0.5, chosen[:, :, :], ALU.mult,
                                                   ALU.mult).then_inc(route, 1)
                    dve.wait_ge(route, b * ROUTE + ROUTE)

                def product(b, e):
                    dve.wait_ge(silu_ready, b * E + e + 1)
                    dve.wait_ge(low_ready, b * E + e + 1)
                    nc.vector.tensor_tensor(act_f[:, e % 2, :], h3[e % 2][:, :], silu[:, e % 2, :],
                                            ALU.mult).then_inc(act_ready, 1)

                def add(b, e):
                    for half in range(2):
                        dve.wait_ge(y_ready, b * YS + 2 * e + half + 1)
                        if e:
                            dve.wait_ge(y_free, b * YS + 2 * e + half + 1)
                        for t in (2 * half, 2 * half + 1):
                            xt = core.x[:, b * TILES + t, :]
                            gain = gates[:, t, e:e + 1] if e < EXPERTS else 0.5
                            op = nc.vector.scalar_tensor_tensor(xt, y[:, t, :], gain, xt, ALU.mult, ALU.add)
                        op.then_inc(y_free, 1)

                def body(b, p, before, more):
                    for e in range(E):
                        if e > LAG:
                            add(b, e - LAG - 1)
                        elif e == 0 and before:
                            add(b - 1, EXPERTS - 1)
                        elif e == 2 and before:
                            add(b - 1, EXPERTS)
                        if e == 2:
                            gate(b)
                        product(b, e)
                        if e == 0:
                            router(b)
                        if before and e == 4 and out is None:
                            stats.take(dve, b - 1, lambda: dve.wait_ge(y_free, b * YS + 2))
                        if more and e == 3:
                            norm.normalise(dve, b + 1)
                        if more and e in (6, 7):
                            norm.low(dve, b + 1, range(e - 6, e - 5), 1 - p)

                over_pairs(dve, core.batches, body)
                add(core.batches - 1, EXPERTS - 1)
                add(core.batches - 1, EXPERTS)
                if out is None:
                    stats.take(dve, core.batches - 1, lambda: dve.wait_ge(y_free, core.batches * YS + 2))


HEADS = 16
HD = DM // HEADS
GROUPS, GH = 4, 4
STEPS = GROUPS * TILES
BAND, BAND_VAL = 2, 0.1
XT_AT = [(1, 2), (2, 1)]
QK_AT = [[(3, 2), (4, 0), (4, 1), (4, 2)], [(8, 0), (8, 1), (8, 2), (9, 0)]]
OT_AT = [(6, 1), (6, 2)]
Y_AT = [(10, 0), (10, 1), (10, 2), (11, 0)]
V_AT = [(13, 2), (14, 1), (15, 0), (15, 2)]
AHEAD = 7
STACK = 3 * HD


def att_stage(core, a, name):
    nc, s = core.nc, core.sem
    SCALE = HD ** -0.5
    WIDE = P + 2 * BAND
    with ExitStack() as ctx:
        wh, wl = {}, {}
        parts = []
        for n in ("q", "k", "v", "o"):
            wh[n] = core.sbuf(f"W{n}_hi", [P, KT, DM], F32R, ctx)
            wl[n] = core.sbuf(f"W{n}_lo", [P, KT, DM], F32R, ctx)
            parts.append((a[f"w{n}_t"].rearrange("(k p) m -> p k m", p=P), wh[n][:, :, :], wl[n][:, :, :]))
        prepare(core, name, parts)

        bq, bk, ocr, bv = (core.sbuf(n, [P, KT], F32, ctx) for n in ("bq_sb", "bk_sb", "ocr_sb", "bv_sb"))
        crow = core.sbuf("out_bias", [P, DM], F32, ctx)
        bvs = core.sbuf("bv_spread", [P, KT, P], F32R, ctx)
        bvl = core.sbuf("bv_spread_lo", [P, KT, P], F32R, ctx)
        band = core.sbuf("band", [P, WIDE], F32, ctx)
        qs = core.sbuf("q_stack", [P, KT, GH, TOKENS], F32R, ctx)
        ks = core.sbuf("k_stack", [P, KT, GH, TOKENS], F32R, ctx)
        one_f = core.sbuf("one_f", [P, 1], F32, ctx)
        full = core.sbuf("qk_full", [P, 2, TOKENS], F32, ctx)
        qkh, qkl = (core.sbuf(n, [P, KT, 2, TOKENS], F32R, ctx) for n in ("qk_hi", "qk_lo"))
        scratch = nc.dram_tensor("qk_scratch", (KT, 2, 3, HD, HEADS // KT, TOKENS), F32).ap()
        nm = core.sbuf("neg_max", [P, 2, GH, TILES], F32, ctx)
        nmt = core.sbuf("neg_max_t", [TILES * GH, 2, P], F32R, ctx)
        vaug = core.sbuf("v_ones", [P, TILES, HEADS, 2 * HD], F32, ctx)
        prob = core.sbuf("prob", [P, TILES, GH, TOKENS], F32, ctx)
        ot = core.sbuf("o_t", [P, TOKENS], F32, ctx)
        rec = core.sbuf("sum_rec", [P, TILES, GH, 1], F32, ctx)
        on = core.sbuf("o_norm", [P, TILES, DM], F32, ctx)
        oh, ol = (core.sbuf(n, [P, KT, TOKENS], F32R, ctx) for n in ("oh", "ol"))
        ys = full[:, :, :].rearrange("p k (u d) -> p (k u) d", u=2)

        s1p = [core.psum(f"s1_{i}", [P, TOKENS], ctx) for i in range(2)]
        s2p = [core.psum(f"s2_{i}", [P, TOKENS], ctx) for i in range(2)]
        pvp = core.psum("pv", [P, TOKENS], ctx)
        mp = core.psum("misc", [P, TOKENS], ctx)
        tp = core.psum("tp", [P, KT, TOKENS], ctx)
        tpy = tp[:, :, :].rearrange("p k (u d) -> p (k u) d", u=2)

        turns = s(name + "_turns")
        loaded_b, spread, spread_h, spread_done = s(name + "_biases"), s(name + "_spread"), s(name + "_spread_h"), s(name + "_spread_l")
        crow_ps, crow_ready = s(name + "_crow_ps"), s(name + "_crow")
        pool_step, ks_one, va_one = s(name + "_pool_step"), s(name + "_ks_one"), s(name + "_va_one")
        s1_ready = s(name + "_s1_ready")
        max_done = s(name + "_max_done")
        s2_ready = s(name + "_s2_ready")
        exp_done = s(name + "_exp_done")
        band_done = s(name + "_band_done")
        pv_done = s(name + "_pv_done")
        nm_ready = s(name + "_nm_ready")
        nmt_ready = s(name + "_nmt_ready")
        rowed = [s(f"{name}_max_row{g}") for g in range(GROUPS)]
        loaded = [s(f"{name}_stack{g}") for g in range(GROUPS)]
        written = [s(f"{name}_written{m}") for m in range(KT)]
        ot_ready = s(name + "_ot_ready")
        tr_ready = s(name + "_tr_ready")
        rec_ready = s(name + "_rec_ready")
        on_ready = s(name + "_on_ready")
        qk_ps = s(name + "_qk_in_psum")
        v_ps, o_ps, y_ps = (s(f"{name}_{n}_in_psum") for n in "voy")
        full_ready = s(name + "_full_ready")
        qkh_ready = s(name + "_qk_hi")
        qkl_ready = s(name + "_qk_lo")
        v_ready = s(name + "_v_ready")
        oh_ready, ol_ready = s(name + "_oh_ready"), s(name + "_ol_ready")
        y_ready = s(name + "_y_ready")
        x_done = s(name + "_x_updated")
        norm = Norm(core, name, tp)
        stats = Stats(core, name)
        PER_LOAD, PER_WRITE = 16 * 2, 16 * 6
        first = lambda b: isinstance(b, int) and b == 0

        def stack_rows(g, n):
            return slice(64 * (g % 2), 64 * (g % 2) + n)

        with nc.Block() as block:

            @block.sync
            def _(sp):
                for d, n in ((bq, "bq"), (bk, "bk"), (ocr, "ocr_bias"), (bv, "bv")):
                    for k in range(KT):
                        sp.dma_start(d[:, k:k + 1], a[n][:, k * P:(k + 1) * P].rearrange("a p -> p a")).then_inc(loaded_b, 16)
                sp.dma_start(crow[:, :], a["bo"].to_broadcast([P, DM])).then_inc(loaded_b, 16)
                sp.wait_ge(ks_one, 2)

                def write(b, m, part, ready):
                    sp.wait_ge(ready, KT * b + m + 1)
                    hold(sp, turns)
                    if part == 0 and not first(b):
                        for g in (2 * m, 2 * m + 1):
                            sp.wait_ge(loaded[g], PER_LOAD * b)
                    src = (qkh, qkl)[part]
                    for x, slots in enumerate((((0, 1), (0, 2)), ((2,), (1,)))[part]):
                        for slot in slots:
                            sp.dma_start(scratch[m, x, slot].rearrange("r h c -> h r c"),
                                         as_f32(src[:, m, x, :])).then_inc(written[m], 16)

                def load(b, g):
                    m = g // 2
                    sp.wait_ge(written[m], PER_WRITE * b + PER_WRITE)
                    hold(sp, turns)
                    if not first(b):
                        sp.wait_ge(s2_ready, (b - 1) * STEPS * GH + TILES * GH * (g + 1))
                    heads = slice(GH * (g % 2), GH * (g % 2) + GH)
                    for x, stack in enumerate((qs, ks)):
                        sp.dma_start(as_f32(stack[stack_rows(g, STACK), m, :, :]),
                                     scratch[m, x, :, :, heads, :]).then_inc(loaded[g], 16)

                def max_row(b, g):
                    sp.wait_ge(nmt_ready, b * GROUPS + g + 1)
                    row = 64 * (g % 2) + STACK
                    sp.dma_start(as_f32(qs[row:row + 1, g // 2, :, :]), as_f32(nmt[:, g % 2, :])).then_inc(rowed[g], 16)

                for m in range(KT):
                    write(0, m, 0, qkh_ready)
                    write(0, m, 1, qkl_ready)
                    load(0, 2 * m)
                    load(0, 2 * m + 1)
                max_row(0, 0)

                def body(b, before, more):
                    max_row(b, 1)
                    if more:
                        write(b + 1, 0, 0, qkh_ready)
                        write(b + 1, 0, 1, qkl_ready)
                    max_row(b, 2)
                    if more:
                        load(b + 1, 0)
                        load(b + 1, 1)
                        write(b + 1, 1, 0, qkh_ready)
                        write(b + 1, 1, 1, qkl_ready)
                    max_row(b, 3)
                    if more:
                        load(b + 1, 2)
                        max_row(b + 1, 0)
                        load(b + 1, 3)

                over_sequences(sp, core.batches, body)

            @block.gpsimd
            def _(pool):
                nc.gpsimd.memset(one_f[:, :], 1.0).then_inc(pool_step, 1)
                nc.gpsimd.memset(band[:, :], 1.0).then_inc(pool_step, 1)
                nc.gpsimd.memset(vaug[:, :, :, :], 1.0).then_inc(va_one, 1)
                nc.gpsimd.memset(as_f32(ks[:, :, :, :]), 1.0).then_inc(ks_one, 1)
                nc.gpsimd.memset(as_f32(qs[:, :, :, :]), 0.0).then_inc(ks_one, 1)
                pool.wait_ge(pool_step, 2)
                factor = math.exp(BAND_VAL)
                nc.gpsimd.memset(band[:, :], factor).then_inc(pool_step, 1)
                pool.wait_ge(pool_step, 3)
                nc.gpsimd.affine_select(out=band[:, :], in_=band[:, :], compare_op=ALU.is_ge, fill=1.0, base=0,
                                        pattern=[[1, WIDE]], channel_multiplier=-1).then_inc(pool_step, 1)
                pool.wait_ge(pool_step, 4)
                nc.gpsimd.affine_select(out=band[:, :], in_=band[:, :], compare_op=ALU.is_ge, fill=1.0, base=2 * BAND,
                                        pattern=[[-1, WIDE]], channel_multiplier=1).then_inc(pool_step, 1)
                pool.wait_ge(pool_step, 5)

                def band_factor(b, st):
                    kt = st % TILES
                    pool.wait_ge(exp_done, (b * STEPS + st) * GH + GH + 2)
                    lo, hi = max(0, kt * P - BAND), min(TOKENS, kt * P + P + BAND)
                    off = lo - (kt * P - BAND)
                    pr = prob[:, kt, :, lo:hi]
                    nc.gpsimd.tensor_tensor(pr, pr, bcast(band[:, off:off + hi - lo].unsqueeze(1), [P, GH, hi - lo]),
                                            ALU.mult).then_inc(band_done, 1)

                def low_part(b, m):
                    pool.wait_ge(qkh_ready, KT * b + m + 1)
                    if not first(b):
                        pool.wait_ge(written[m], PER_WRITE * b)
                    nc.gpsimd.tensor_tensor(qkl[:, m, :, :], full[:, :, :], as_f32(qkh[:, m, :, :]),
                                            ALU.subtract).then_inc(qkl_ready, 1)

                def add(b):
                    pool.wait_ge(y_ready, b + 2)
                    xs = core.x[:, bass.ds(b * TILES, TILES), :]
                    nc.gpsimd.tensor_tensor(xs, xs, ys, ALU.add).then_inc(x_done, 1)

                low_part(0, 0)
                low_part(0, 1)

                def body(b, before, more):
                    for st in range(STEPS):
                        band_factor(b, st)
                        if more and st in (4, 9):
                            low_part(b + 1, st // 8)
                        if before and st == 12:
                            add(b - 1)

                over_sequences(pool, core.batches, body)
                add(core.batches - 1)

            @block.tensor
            def _(pe):
                pe.wait_ge(spread_done, 2)
                n = 0
                for x, w in ((bvs, "h"), (bvs, "l"), (bvl, "h")):
                    for k in range(KT):
                        op = nc.tensor.matmul(tpy[:, 0, :], x[:, k, :], (wh if w == "h" else wl)["o"][:, k, :],
                                              start=(n == 0), stop=(n == 5))
                        n += 1
                op.then_inc(crow_ps, 1)
                pe.wait_ge(crow_ready, 1)

                def qk_proj(b, m, parts=range(4), after_o=False):
                    if parts[0] == 0 and m == 0:
                        pe.wait_ge(norm.xl_ready, b + 1)
                    elif parts[0] == 0:
                        pe.wait_ge(full_ready, 2 * (KT * b + m))
                        if after_o:
                            pe.wait_ge(ol_ready, b - 1)
                    for part in parts:
                        x, k = part // 2, part % 2
                        n = "qk"[x]
                        for i, (w, act) in enumerate([(wh, core.xh), (wl, core.xh), (wh, core.xl)]):
                            op = nc.tensor.matmul(tp[:, x, :], w[n][:, k, m * P:(m + 1) * P], act[:, k, :],
                                                  start=(k == 0 and i == 0), stop=(k == KT - 1 and i == 2))
                    if parts[-1] == 3:
                        op.then_inc(qk_ps, 1)

                def tokens(t, xh, xl, n, done):
                    for k in range(KT):
                        for i, (x, w) in enumerate([(xh, wh), (xh, wl), (xl, wh)]):
                            op = nc.tensor.matmul(tpy[:, t, :], x[:, k, t * P:(t + 1) * P], w[n][:, k, :],
                                                  start=(k == 0 and i == 0), stop=(k == KT - 1 and i == 2))
                    if t == TILES - 1:
                        op.then_inc(done, 1)

                def v_proj(b, t, after_y):
                    if t == 0 and after_y:
                        pe.wait_ge(y_ready, b)
                    elif t == 0:
                        pe.wait_ge(full_ready, 2 * (KT * b + KT))
                    tokens(t, core.xh, core.xl, "v", v_ps)

                def s1_unit(b, st, i):
                    g, qt = st // TILES, st % TILES
                    if qt == 0 and i == 0:
                        pe.wait_ge(loaded[g], PER_LOAD * b + PER_LOAD)
                    pe.wait_ge(max_done, (b * STEPS + st) * GH + i + 1)
                    r = stack_rows(g, STACK)
                    nc.tensor.matmul(s1p[i % 2][:, :], qs[r, g // 2, i, qt * P:(qt + 1) * P], ks[r, g // 2, i, :],
                                     start=True, stop=True).then_inc(s1_ready, 1)

                def s2_unit(b, st, i):
                    g, kt = st // TILES, st % TILES
                    if kt == 0 and i == 0:
                        pe.wait_ge(rowed[g], 16 * b + 16)
                    pe.wait_ge(exp_done, (b * STEPS + st) * GH + i + 1)
                    r = stack_rows(g, 64)
                    nc.tensor.matmul(s2p[i % 2][:, :], ks[r, g // 2, i, kt * P:(kt + 1) * P], qs[r, g // 2, i, :],
                                     start=True, stop=True).then_inc(s2_ready, 1)

                def max_t(b, g):
                    pe.wait_ge(max_done, (b * GROUPS + g) * TILES * GH + TILES * GH + 2)
                    if first(b) and g in (1, 2):
                        pe.wait_ge(nmt_ready, g)
                    elif not (first(b) and g == 0):
                        pe.wait_ge(on_ready, b * GROUPS + g - 2)
                    nc.tensor.transpose(mp[0:TILES * GH, 0:P], nm[:, g % 2, :, :].rearrange("p h t -> p (h t)"),
                                        core.ident[:, :]).then_inc(nm_ready, 1)

                def pv(b, st):
                    g, kt = st // TILES, st % TILES
                    pe.wait_ge(band_done, b * STEPS + st + 1)
                    if st == 0:
                        pe.wait_ge(v_ready, b + 1)
                    if kt == 0 and not (first(b) and g == 0):
                        pe.wait_ge(ot_ready, b * GROUPS + g)
                    for i in range(GH):
                        op = nc.tensor.matmul(pvp[2 * HD * i:2 * HD * (i + 1), :], vaug[:, kt, GH * g + i, :], prob[:, kt, i, :],
                                              start=(kt == 0), stop=(kt == TILES - 1))
                    op.then_inc(pv_done, 1)

                def out_t(b, g):
                    pe.wait_ge(ot_ready, b * GROUPS + g + 1)
                    if isinstance(b, int) and b == core.batches - 1 and g >= 2:
                        pe.wait_ge(on_ready, b * GROUPS + g)
                    else:
                        pe.wait_ge(nmt_ready, b * GROUPS + g + 3)
                    for qt in range(TILES):
                        op = nc.tensor.transpose(mp[:, qt * P:(qt + 1) * P], ot[:, qt * P:(qt + 1) * P], core.ident[:, :])
                    op.then_inc(tr_ready, 1)

                def o_transpose(b, k, sem, count):
                    if k == 0:
                        pe.wait_ge(on_ready, b * GROUPS + GROUPS)
                        pe.wait_ge(sem, count)
                    for t in range(TILES):
                        op = nc.tensor.transpose(tp[:, k, t * P:(t + 1) * P], on[:, t, k * P:(k + 1) * P], core.ident[:, :])
                    if k == KT - 1:
                        op.then_inc(o_ps, 1)

                def o_project(b, t):
                    if t == 0:
                        pe.wait_ge(ol_ready, b + 1)
                    tokens(t, oh, ol, "o", y_ps)

                norm.transpose(pe, 0)
                qk_proj(0, 0)
                qk_proj(0, 1)
                for t in range(TILES):
                    v_proj(0, t, False)
                for st in range(AHEAD):
                    for i in range(GH):
                        s1_unit(0, st, i)
                    if st == TILES - 1:
                        max_t(0, 0)

                def body(b, before, more):
                    for st in range(STEPS):
                        ahead = st + AHEAD
                        for i in range(GH):
                            s2_unit(b, st, i)
                            if ahead < STEPS:
                                s1_unit(b, ahead, i)
                            elif more:
                                s1_unit(b + 1, ahead - STEPS, i)
                            at = (st, i)
                            if i == 3 and st:
                                pv(b, st - 1)
                            elif i == 3 and before:
                                pv(b - 1, STEPS - 1)
                            if st % TILES == 1 and i == 1:
                                if st + TILES < STEPS:
                                    max_t(b, st // TILES + 1)
                                elif more:
                                    max_t(b + 1, 0)
                            if st % TILES == 2 and i == 0:
                                if st > 2:
                                    out_t(b, st // TILES - 1)
                                elif before:
                                    out_t(b - 1, GROUPS - 1)
                            if more and at in XT_AT:
                                n = XT_AT.index(at)
                                norm.transpose(pe, b + 1, lambda: pe.wait_ge(v_ready, b + 1), range(n, n + 1))
                            if more and at in QK_AT[0]:
                                n = QK_AT[0].index(at)
                                qk_proj(b + 1, 0, range(n, n + 1))
                            if more and at in QK_AT[1]:
                                n = QK_AT[1].index(at)
                                qk_proj(b + 1, 1, range(n, n + 1), before)
                            if before and at in OT_AT:
                                if more:
                                    o_transpose(b - 1, OT_AT.index(at), full_ready, 2 * (KT * b + KT + 1))
                                else:
                                    o_transpose(b - 1, OT_AT.index(at), v_ready, b + 1)
                            if before and at in Y_AT:
                                o_project(b - 1, Y_AT.index(at))
                            if more and at in V_AT:
                                v_proj(b + 1, V_AT.index(at), before)

                over_sequences(pe, core.batches, body)
                last = core.batches - 1
                pv(last, STEPS - 1)
                out_t(last, GROUPS - 1)
                for k in range(KT):
                    o_transpose(last, k, *((y_ready, last + 1) if last else (v_ready, 1)))
                for t in range(TILES):
                    o_project(last, t)

            @block.scalar
            def _(act):
                act.wait_ge(spread, 1)
                nc.scalar.copy(bvs[:, :, :], full[:, :, 0:P]).then_inc(spread_h, 1)
                norm.high(act, 0)

                def k_full(b, m):
                    act.wait_ge(qk_ps, KT * b + m + 1)
                    if not first(b) or m == 1:
                        act.wait_ge(qkl_ready, KT * b + m)
                    nc.scalar.activation(full[:, 1, :], tp[:, 1, :], ACT.Identity, bias=bk[:, m:m + 1]).then_inc(full_ready, 1)

                def ot_copy(b, g):
                    act.wait_ge(pv_done, b * STEPS + TILES * (g + 1))
                    if not (first(b) and g == 0):
                        act.wait_ge(tr_ready, b * GROUPS + g)
                    nc.scalar.copy(ot[:, :], pvp[:, :]).then_inc(ot_ready, 1)

                def high_part(b, m, x):
                    if x == 0:
                        act.wait_ge(full_ready, 2 * (KT * b + m + 1))
                        if not first(b):
                            act.wait_ge(written[m], PER_WRITE * b)
                    op = nc.scalar.copy(qkh[:, m, x, :], full[:, x, :])
                    if x:
                        op.then_inc(qkh_ready, 1)

                def exp_unit(b, st, i):
                    kt = st % TILES
                    n = b * STEPS + st
                    act.wait_ge(s2_ready, n * GH + i + 1)
                    if i == 0 and not (first(b) and st < TILES):
                        act.wait_ge(pv_done, n - TILES + 1)
                    nc.scalar.activation(prob[:, kt, i, :], s2p[i % 2][:, :], ACT.Exp).then_inc(exp_done, 1)

                def max_copy(b, g):
                    act.wait_ge(nm_ready, b * GROUPS + g + 1)
                    if not (first(b) and g < 2):
                        if g >= 2:
                            act.wait_ge(rowed[g - 2], 16 * b + 16)
                        else:
                            act.wait_ge(rowed[g + 2], 16 * b)
                    nc.scalar.copy(nmt[:, g % 2, :], mp[0:TILES * GH, 0:P]).then_inc(nmt_ready, 1)

                def v_copy(b):
                    act.wait_ge(v_ps, b + 1)
                    if first(b):
                        act.wait_ge(va_one, 1)
                    else:
                        act.wait_ge(pv_done, b * STEPS)
                    for t in range(TILES):
                        op = nc.scalar.copy(vaug[:, t, :, 0:HD], tpy[:, t, :].rearrange("p (h d) -> p h d", h=HEADS))
                    op.then_inc(v_ready, 1)

                def o_high(b, k):
                    if k == 0:
                        act.wait_ge(o_ps, b + 1)
                    op = nc.scalar.copy(oh[:, k, :], tp[:, k, :])
                    if k == KT - 1:
                        op.then_inc(oh_ready, 1)

                act.wait_ge(loaded_b, 16 * (4 * KT + 1))
                for m in range(KT):
                    k_full(0, m)
                    for x in range(2):
                        high_part(0, m, x)
                max_copy(0, 0)

                def body(b, before, more):
                    for st in range(STEPS):
                        for i in range(GH):
                            exp_unit(b, st, i)
                            if st == 0 and i == 3:
                                v_copy(b)
                            if st % TILES == 1 and i == 0:
                                if st > 1:
                                    ot_copy(b, st // TILES - 1)
                                elif before:
                                    ot_copy(b - 1, GROUPS - 1)
                            if more and (st, i) in ((4, 3), (9, 1)):
                                k_full(b + 1, st // 8)
                            if st % TILES == 1 and i == 1:
                                if st + TILES < STEPS:
                                    max_copy(b, st // TILES + 1)
                                elif more:
                                    max_copy(b + 1, 0)
                            if more and st == 2 and i in (1, 2):
                                norm.high(act, b + 1, lambda: act.wait_ge(v_ps, b + 1), range(i - 1, i))
                            if more and (st, i) in ((5, 1), (5, 2), (9, 2), (9, 3)):
                                high_part(b + 1, st // 8, int((st, i) in ((5, 2), (9, 3))))
                            if before and (st, i) in ((6, 3), (7, 0)):
                                o_high(b - 1, st - 6)

                act.sem_inc(exp_done, 2)
                over_sequences(act, core.batches, body)
                ot_copy(core.batches - 1, GROUPS - 1)
                for k in range(KT):
                    o_high(core.batches - 1, k)

            @block.vector
            def _(dve):
                dve.wait_ge(loaded_b, 16 * (4 * KT + 1))
                dve.wait_ge(pool_step, 2)
                nc.vector.tensor_tensor(bq[:, :], bq[:, :], ocr[:, :], ALU.add)
                for k in range(KT):
                    op = nc.vector.tensor_scalar(full[:, k, 0:P], core.ones[:, :], bv[:, k:k + 1], None, ALU.mult)
                op.then_inc(spread, 1)
                dve.wait_ge(spread_h, 1)
                nc.vector.tensor_tensor(bvl[:, :, :], full[:, :, 0:P], as_f32(bvs[:, :, :]), ALU.subtract).then_inc(spread_done, 2)
                dve.wait_ge(crow_ps, 1)
                nc.vector.tensor_tensor(crow[:, :], crow[:, :], tpy[:, 0, :], ALU.add).then_inc(crow_ready, 1)
                dve.sem_inc(max_done, 2)
                dve.sem_inc(y_ready, 1)

                def q_full(b, m):
                    dve.wait_ge(qk_ps, KT * b + m + 1)
                    if not first(b) or m == 1:
                        dve.wait_ge(qkl_ready, KT * b + m)
                    nc.vector.tensor_scalar(full[:, 0, :], tp[:, 0, :], bq[:, m:m + 1], SCALE, ALU.add,
                                            ALU.mult).then_inc(full_ready, 1)

                def max_unit(b, st, i):
                    g, qt = st // TILES, st % TILES
                    dve.wait_ge(s1_ready, (b * STEPS + st) * GH + i + 1)
                    nc.vector.tensor_reduce(nm[:, g % 2, i, qt:qt + 1], s1p[i % 2][:, :], AXIS_X, ALU.max,
                                            negate=True).then_inc(max_done, 1)

                def normalise_out(b, g):
                    dve.wait_ge(tr_ready, b * GROUPS + g + 1)
                    if g == 0 and not first(b):
                        dve.wait_ge(o_ps, b)
                    m4 = mp[:, :].rearrange("p (t h d) -> p t h d", t=TILES, h=GH)
                    nc.vector.reciprocal(rec[:, :, :, :], m4[:, :, :, HD:HD + 1]).then_inc(rec_ready, 1)
                    dve.wait_ge(rec_ready, b * GROUPS + g + 1)
                    out = on[:, :, g * GH * HD:(g + 1) * GH * HD].rearrange("p t (h d) -> p t h d", h=GH)
                    nc.vector.tensor_tensor(out, m4[:, :, :, 0:HD], bcast(rec[:, :, :, :], [P, TILES, GH, HD]),
                                            ALU.mult).then_inc(on_ready, 1)

                def o_low(b, k):
                    if k == 0:
                        dve.wait_ge(oh_ready, b + 1)
                    op = nc.vector.tensor_tensor(ol[:, k, :], tp[:, k, :], as_f32(oh[:, k, :]), ALU.subtract)
                    if k == KT - 1:
                        op.then_inc(ol_ready, 1)

                def y_out(b, half, split):
                    if half == 0:
                        dve.wait_ge(y_ps, b + 1)
                        dve.wait_ge(qkl_ready, KT * split)
                    t = slice(2 * half, 2 * half + 2)
                    op = nc.vector.tensor_tensor(ys[:, t, :], tpy[:, t, :], bcast(crow[:, :].unsqueeze(1), [P, 2, DM]), ALU.add)
                    if half:
                        op.then_inc(y_ready, 1)

                norm.normalise(dve, 0)
                norm.low(dve, 0)
                for m in range(KT):
                    q_full(0, m)
                for st in range(AHEAD):
                    for i in range(GH):
                        max_unit(0, st, i)

                def body(b, before, more):
                    for st in range(STEPS):
                        for i in range(GH):
                            if st + AHEAD < STEPS:
                                max_unit(b, st + AHEAD, i)
                            elif more:
                                max_unit(b + 1, st + AHEAD - STEPS, i)
                            if more and st == 0:
                                norm.normalise(dve, b + 1, range(i, i + 1))
                            if st % TILES == 2 and i == 3:
                                if st > 2:
                                    normalise_out(b, st // TILES - 1)
                                elif before:
                                    normalise_out(b - 1, GROUPS - 1)
                            if more and (st, i) in ((2, 3), (3, 0)):
                                norm.low(dve, b + 1, range(st - 2, st - 1))
                            if more and (st, i) in ((4, 3), (9, 1)):
                                q_full(b + 1, st // 8)
                            if before and st == 7 and i in (0, 1):
                                o_low(b - 1, i)
                            if before and st == 11 and i in (2, 3):
                                y_out(b - 1, i - 2, b + 2 if more else b + 1)
                            if before and st == 14:
                                stats.tiles(dve, b - 1, lambda: dve.wait_ge(x_done, b), range(i, i + 1))
                            if before and (st, i) == (15, 1):
                                stats.finish(dve, b - 1)

                over_sequences(dve, core.batches, body)
                last = core.batches - 1
                normalise_out(last, GROUPS - 1)
                for k in range(KT):
                    o_low(last, k)
                for half in range(2):
                    y_out(last, half, core.batches)
                stats.take(dve, last, lambda: dve.wait_ge(x_done, core.batches))


GH0 = 2
CHUNK = P
SUB = 32
LEVELS = [0, 1, 2, 4, 8, 16, 32, 64]
SMALL = 6


def level_masks():
    import numpy as np

    m = np.zeros((SMALL, SUB, SUB), np.float32)
    for i, size in enumerate(LEVELS[:SMALL]):
        for s in range(SUB):
            for t in range(SUB):
                if size == 0:
                    m[i, s, t] = s == t
                else:
                    same = s // (2 * size) == t // (2 * size)
                    m[i, s, t] = same and s % (2 * size) < size <= t % (2 * size)
    return np.ascontiguousarray(np.tile(m.transpose(1, 0, 2), (P // SUB, 1, 1)))


def gla_stage(core, a, name):
    nc, s = core.nc, core.sem
    NC = TOKENS // CHUNK
    with ExitStack() as ctx:
        wih, wil = (core.sbuf(n, [P, KT, 3 * DM], F32R, ctx) for n in ("wih", "wil"))
        g1h, g1l = (core.sbuf(n, [P, KT, P], F32R, ctx) for n in ("wg1h", "wg1l"))
        g2h, g2l = (core.sbuf(n, [P, DM], F32R, ctx) for n in ("wg2h", "wg2l"))
        woh, wol = (core.sbuf(n, [P, KT, DM], F32R, ctx) for n in ("gwoh", "gwol"))
        wide = lambda n: a[n].rearrange("(k p) m -> p k m", p=P)
        prepare(core, name, [(wide("w_in_t"), wih[:, :, :], wil[:, :, :]),
                             (wide("w_g1_t"), g1h[:, :, :], g1l[:, :, :]),
                             (a["w_g2_t"], g2h[:, :], g2l[:, :]),
                             (wide("w_out_t"), woh[:, :, :], wol[:, :, :], a["ln_w"])])

        W2 = GH0 * TOKENS
        masks_f = core.sbuf("level_mask_f32", [P, SMALL, SUB], F32, ctx)
        masks = core.sbuf("level_mask", [P, SMALL, SUB], U8, ctx)
        sig = core.sbuf("g_sig", [P, W2], F32, ctx)
        q = core.sbuf("g_q", [P, W2], F32, ctx)
        f = core.sbuf("g_f", [P, W2], F32, ctx)
        qp = core.sbuf("g_qp", [P, W2], F32, ctx)
        ks = core.sbuf("g_ks", [P, W2], F32, ctx)
        tot = core.sbuf("g_tot", [P, W2], F32, ctx)
        v = core.sbuf("g_v", [P, NC, DM], F32, ctx)
        gate = core.sbuf("g_gate", [P, NC, DM], F32, ctx)
        ghi, glo = (core.sbuf(n, [P, TOKENS], F32R, ctx) for n in ("ghi", "glo"))
        diag = core.sbuf("g_diag", [P, GH0, NC, SUB], F32, ctx)
        at = core.sbuf("g_at", [P, GH0, NC, CHUNK], F32, ctx)
        kst = core.sbuf("g_kst", [P, GH0, NC - 1, P], F32, ctx)
        st = core.sbuf("g_state", [P, GH0, NC - 1, P], F32, ctx)
        og = core.sbuf("g_og", [P, NC, DM], F32, ctx)
        o6 = core.sbuf("g_stat6", [P, NC, 6], F32, ctx)
        omv = core.sbuf("g_mv", [P, NC, 2], F32, ctx)
        osd = core.sbuf("g_sd", [P, NC], F32, ctx)
        ors = core.sbuf("g_rstd", [P, NC], F32, ctx)
        oh, ol = (core.sbuf(n, [P, KT, TOKENS], F32R, ctx) for n in ("g_oh", "g_ol"))

        ab = core.psum("g_a", [P, 2, TOKENS], ctx)
        hb = core.psum("g_h", [P, GH0, TOKENS], ctx)
        ob = core.psum("g_o", [P, NC, DM], ctx)
        tp = core.psum("g_tp", [P, KT, TOKENS], ctx)
        aby = ab[:, :, :].rearrange("p k (u d) -> p (k u) d", u=2)
        hbc = hb[:, :, :].rearrange("p h (c t) -> p h c t", c=NC)
        hd = hbc[:, :, :, 0:SUB]

        def total(size):
            if size == 1:
                return f[:, :]
            off = W2 - 2 * W2 // size
            return tot[:, off:off + W2 // size]

        a_free = [s(f"{name}_a{i}_free") for i in range(2)]
        lg_ps, q_ps, v_ps, g1_ps, gate_ps, y_ps = (s(f"{name}_{n}_ps") for n in ("lg", "q", "v", "g1", "gate", "y"))
        f_ready, k_ready, sig_ready, q_ready, qp_ready = (s(f"{name}_{n}") for n in ("f", "k", "sig", "q", "qp"))
        v_ready, ghi_ready, glo_ready, gate_ready = (s(f"{name}_{n}") for n in ("v", "g1hi", "g1lo", "gate"))
        level_done = s(name + "_level_done")
        merged = s(name + "_merged")
        up_q, up_k, up_t = (s(f"{name}_up_{n}") for n in ("q", "k", "t"))
        diag_copied = s(name + "_diag_copied")
        at_ready = s(name + "_at_ready")
        kst_ps, kst_ready = s(name + "_kst_ps"), s(name + "_kst_ready")
        kv_ps, s0_ready, st_ready = s(name + "_kv_ps"), s(name + "_s0_ready"), s(name + "_st_ready")
        o_ready, og_ready, o_stat, o_aggr, o_sd, o_rs, on_ready = (
            s(f"{name}_{n}") for n in ("o_ps", "og", "o_stat", "o_aggr", "o_sd", "o_rs", "on"))
        ot_ps, oh_ready, ol_ready, x_done = (s(f"{name}_{n}") for n in ("ot_ps", "oh", "ol", "x_updated"))
        turns, st_step = s(name + "_turns"), s(name + "_st_step")
        masks_in, zeroed = s(name + "_masks"), s(name + "_zeroed")
        NL = len(LEVELS)
        norm = Norm(core, name, tp)
        stats = Stats(core, name)
        first = lambda b: isinstance(b, int) and b == 0

        with nc.Block() as block:

            @block.sync
            def _(sp):
                sp.dma_start(masks_f[:, :, :], a["level_masks"]).then_inc(masks_in, 16)

            @block.tensor
            def _(pe):
                pairs = lambda wh, wl, xh, xl: [(wh, xh), (wl, xh), (wh, xl)]

                def bank(b, i, use, uses):
                    pe.wait_ge(a_free[i], (b * uses - (0 if first(b) else 1)) + use + 1)

                def channels(b, col, i, use, done):
                    bank(b, i, use, (5, 4)[i])
                    for k in range(KT):
                        for n, (w, x) in enumerate(pairs(wih, wil, core.xh, core.xl)):
                            op = nc.tensor.matmul(ab[:, i, :], w[:, k, col:col + P], x[:, k, :],
                                                  start=(k == 0 and n == 0), stop=(k == KT - 1 and n == 2))
                    op.then_inc(done, 1)

                def v_proj(b, half):
                    bank(b, half, 2, (5, 4)[half])
                    for t in (2 * half, 2 * half + 1):
                        for k in range(KT):
                            for n, (w, x) in enumerate(pairs(wih, wil, core.xh, core.xl)):
                                op = nc.tensor.matmul(aby[:, t, :], x[:, k, t * P:(t + 1) * P], w[:, k, 0:DM],
                                                      start=(k == 0 and n == 0), stop=(k == KT - 1 and n == 2))
                    op.then_inc(v_ps, 1)

                def g1_proj(b):
                    bank(b, 0, 3, 5)
                    for k in range(KT):
                        for n, (w, x) in enumerate(pairs(g1h, g1l, core.xh, core.xl)):
                            op = nc.tensor.matmul(ab[:, 0, :], w[:, k, :], x[:, k, :],
                                                  start=(k == 0 and n == 0), stop=(k == KT - 1 and n == 2))
                    op.then_inc(g1_ps, 1)

                def gate_proj(b):
                    pe.wait_ge(glo_ready, b + 1)
                    if not first(b):
                        pe.wait_ge(og_ready, b)
                    for t in range(NC):
                        for n, (w, x) in enumerate(pairs(g2h, g2l, ghi, glo)):
                            op = nc.tensor.matmul(ob[:, t, :], x[:, t * P:(t + 1) * P], w[:, :],
                                                  start=(n == 0), stop=(n == 2))
                    op.then_inc(gate_ps, 1)

                def level(b, i):
                    size = LEVELS[i]
                    if i == 0:
                        pe.wait_ge(q_ready, 2 * b + 2)
                        pe.wait_ge(k_ready, 2 * b + 2)
                        if not first(b):
                            pe.wait_ge(st_ready, b)
                    elif i == 1:
                        pe.wait_ge(qp_ready, b + 1)
                    else:
                        pe.wait_ge(up_q, 7 * b + i - 1)
                        pe.wait_ge(up_k, 7 * b + i - 1)
                    if 1 <= i <= SMALL:
                        pe.wait_ge(merged, SMALL * b + i)
                    qq = q if i == 0 else qp
                    for h in range(GH0):
                        for c in range(NC):
                            base = h * TOKENS + c * CHUNK
                            if i < SMALL:
                                for j in range(CHUNK // SUB):
                                    r = slice(base + SUB * j, base + SUB * (j + 1))
                                    op = nc.tensor.matmul(hd[SUB * j:SUB * (j + 1), h, c, :], ks[:, r], qq[:, r],
                                                          start=True, stop=True)
                            else:
                                for j in range(0, CHUNK, 2 * size):
                                    op = nc.tensor.matmul(hbc[j:j + size, h, c, j + size:j + 2 * size],
                                                          ks[:, base + j:base + j + size],
                                                          qp[:, base + j + size:base + j + 2 * size],
                                                          start=True, stop=True)
                    op.then_inc(level_done, 1)

                def lg_proj(b, h):
                    pe.wait_ge(norm.xl_ready, b + 1)
                    channels(b, 2 * DM + h * P, h, 0, lg_ps)

                def q_proj(b, h):
                    channels(b, DM + h * P, h, 1, q_ps)

                def kst_t(b, more):
                    pe.wait_ge(up_k, 7 * b + 7)
                    if more:
                        pe.wait_ge(norm.xl_ready, b + 2)
                    elif first(b):
                        pe.wait_ge(norm.xl_ready, 1)
                    else:
                        pe.wait_ge(ol_ready, b)
                    for h in range(GH0):
                        for c in range(NC - 1):
                            base = h * TOKENS + c * CHUNK
                            op = nc.tensor.transpose(tp[:, h, c * P:(c + 1) * P], ks[:, base:base + P], core.ident[:, :])
                    op.then_inc(kst_ps, 1)

                def kv(b):
                    pe.wait_ge(kst_ready, b + 1)
                    pe.wait_ge(v_ready, 2 * b + 2)
                    pe.wait_ge(at_ready, b + 1)
                    for h in range(GH0):
                        for c in range(NC - 1):
                            op = nc.tensor.matmul(hb[:, h, c * P:(c + 1) * P], kst[:, h, c, :],
                                                  v[:, c, h * P:(h + 1) * P], start=True, stop=True)
                    op.then_inc(kv_ps, 1)

                def output(b):
                    pe.wait_ge(gate_ready, b + 1)
                    pe.wait_ge(diag_copied, b + 1)
                    pe.wait_ge(up_q, 7 * b + 7)
                    for c in range(NC):
                        for h in range(GH0):
                            out = ob[:, c, h * P:(h + 1) * P]
                            op = nc.tensor.matmul(out, at[:, h, c, :], v[:, c, h * P:(h + 1) * P], start=True, stop=(c == 0))
                            if c:
                                if c == 1 and h == 0:
                                    pe.wait_ge(st_ready, b + 1)
                                base = h * TOKENS + c * CHUNK
                                op = nc.tensor.matmul(out, qp[:, base:base + P], st[:, h, c - 1, :], start=False, stop=True)
                    op.then_inc(o_ready, 1)

                def o_transpose(b):
                    pe.wait_ge(on_ready, b + 1)
                    pe.wait_ge(kst_ready, b + 1)
                    for k in range(KT):
                        for t in range(NC):
                            op = nc.tensor.transpose(tp[:, k, t * P:(t + 1) * P], og[:, t, k * P:(k + 1) * P], core.ident[:, :])
                    op.then_inc(ot_ps, 1)

                def o_project(b, half, free):
                    if half == 0:
                        pe.wait_ge(ol_ready, b + 1)
                    pe.wait_ge(a_free[half], free[half])
                    for t in (2 * half, 2 * half + 1):
                        for k in range(KT):
                            for n, (w, x) in enumerate(pairs(woh, wol, oh, ol)):
                                op = nc.tensor.matmul(aby[:, t, :], x[:, k, t * P:(t + 1) * P], w[:, k, :],
                                                      start=(k == 0 and n == 0), stop=(k == KT - 1 and n == 2))
                    if half:
                        op.then_inc(y_ps, 1)

                norm.transpose(pe, 0)
                for h in range(GH0):
                    lg_proj(0, h)
                for h in range(GH0):
                    q_proj(0, h)

                def body(b, before, more):
                    v_proj(b, 0)
                    level(b, 0)
                    v_proj(b, 1)
                    level(b, 1)
                    g1_proj(b)
                    level(b, 2)
                    if before:
                        o_transpose(b - 1)
                    level(b, 3)
                    gate_proj(b)
                    level(b, 4)
                    if before:
                        o_project(b - 1, 0, (5 * b + 4, 4 * b + 3))
                    level(b, 5)
                    if more and before:
                        norm.transpose(pe, b + 1, lambda: pe.wait_ge(ol_ready, b))
                    elif more:
                        norm.transpose(pe, b + 1)
                    level(b, 6)
                    if before:
                        o_project(b - 1, 1, (5 * b + 4, 4 * b + 3))
                    level(b, 7)
                    if more:
                        lg_proj(b + 1, 0)
                    kst_t(b, more)
                    if more:
                        lg_proj(b + 1, 1)
                    kv(b)
                    if more:
                        q_proj(b + 1, 0)
                    output(b)
                    if more:
                        q_proj(b + 1, 1)

                over_sequences(pe, core.batches, body)
                last = core.batches - 1
                o_transpose(last)
                for half in range(2):
                    o_project(last, half, (5 * last + 4 + (last > 0), 4 * last + 3 + (last > 0)) if last else (5, 4))

            @block.scalar
            def _(act):
                act.sem_inc(a_free[0], 1)
                act.sem_inc(a_free[1], 1)
                norm.high(act, 0)

                def decay(b, h):
                    act.wait_ge(lg_ps, 2 * b + h + 1)
                    r = slice(h * TOKENS, (h + 1) * TOKENS)
                    if h == 0 and not first(b):
                        act.wait_ge(kst_ps, b)
                        act.wait_ge(up_t, 7 * b)
                        act.wait_ge(up_k, 7 * b)
                    nc.scalar.activation(f[:, r], ab[:, h, :], ACT.Sigmoid).then_inc(f_ready, 1)
                    nc.scalar.activation(ks[:, r], ab[:, h, :], ACT.Sigmoid, scale=-1.0).then_inc(k_ready, 1)
                    act.wait_ge(k_ready, 2 * b + h + 1)
                    act.sem_inc(a_free[h], 1)

                def q_sig(b, h):
                    act.wait_ge(q_ps, 2 * b + h + 1)
                    if not first(b):
                        act.wait_ge(q_ready, 2 * b)
                    nc.scalar.activation(sig[:, h * TOKENS:(h + 1) * TOKENS], ab[:, h, :], ACT.Sigmoid).then_inc(sig_ready, 1)

                def v_copy(b, half):
                    act.wait_ge(v_ps, 2 * b + half + 1)
                    nc.scalar.copy(v[:, 2 * half:2 * half + 2, :], aby[:, 2 * half:2 * half + 2, :]).then_inc(v_ready, 1)
                    act.wait_ge(v_ready, 2 * b + half + 1)
                    act.sem_inc(a_free[half], 1)

                def g1_high(b):
                    act.wait_ge(g1_ps, b + 1)
                    if not first(b):
                        act.wait_ge(gate_ps, b)
                    nc.scalar.copy(ghi[:, :], ab[:, 0, :]).then_inc(ghi_ready, 1)

                def gate_sig(b):
                    act.wait_ge(gate_ps, b + 1)
                    nc.scalar.activation(gate[:, :, :], ob[:, :, :], ACT.Sigmoid).then_inc(gate_ready, 1)

                def diag_copy(b):
                    act.wait_ge(merged, SMALL * b + SMALL)
                    if first(b):
                        act.wait_ge(zeroed, 2)
                    else:
                        act.wait_ge(o_ready, b)
                    for j in range(CHUNK // SUB):
                        r = slice(SUB * j, SUB * (j + 1))
                        op = nc.scalar.copy(at[r, :, :, r], diag[r, :, :, :])
                    op.then_inc(diag_copied, 1)

                def at_rest(b):
                    act.wait_ge(level_done, NL * b + NL)
                    if first(b):
                        act.wait_ge(zeroed, 2)
                    else:
                        act.wait_ge(o_ready, b)
                    for r0, n in ((0, 64), (0, 32), (64, 32)):
                        op = nc.scalar.copy(at[r0:r0 + n, :, :, r0 + n:r0 + 2 * n], hbc[r0:r0 + n, :, :, r0 + n:r0 + 2 * n])
                    op.then_inc(at_ready, 1)

                def kst_copy(b):
                    act.wait_ge(kst_ps, b + 1)
                    w = (NC - 1) * P
                    nc.scalar.copy(kst[:, :, :, :].rearrange("p h c d -> p h (c d)"), tp[:, :, 0:w]).then_inc(kst_ready, 1)

                def state0(b):
                    act.wait_ge(kv_ps, b + 1)
                    nc.scalar.copy(st[:, :, 0, :], hb[:, :, 0:P]).then_inc(s0_ready, 1)

                def o_sqrt(b):
                    act.wait_ge(o_aggr, b + 1)
                    nc.scalar.activation(osd[:, :], omv[:, :, 1], ACT.Sqrt, bias=core.eps[:, 0:1]).then_inc(o_sd, 1)

                def o_high(b):
                    act.wait_ge(ot_ps, b + 1)
                    nc.scalar.copy(oh[:, :, :], tp[:, :, :]).then_inc(oh_ready, 1)

                def body(b, before, more):
                    q_sig(b, 0)
                    q_sig(b, 1)
                    if before:
                        o_sqrt(b - 1)
                    v_copy(b, 0)
                    v_copy(b, 1)
                    g1_high(b)
                    if before:
                        o_high(b - 1)
                    gate_sig(b)
                    if more:
                        norm.high(act, b + 1, lambda: act.wait_ge(g1_ps, b + 1))
                    diag_copy(b)
                    at_rest(b)
                    kst_copy(b)
                    if more:
                        decay(b + 1, 0)
                    state0(b)
                    if more:
                        decay(b + 1, 1)

                decay(0, 0)
                decay(0, 1)

                over_sequences(act, core.batches, body)
                o_sqrt(core.batches - 1)
                o_high(core.batches - 1)

            @block.gpsimd
            def _(pool):
                nc.gpsimd.memset(diag[:, :, :, :], 0.0).then_inc(zeroed, 1)
                nc.gpsimd.memset(at[:, :, :, :], 0.0).then_inc(zeroed, 1)

                def raise_k(b, i):
                    size = LEVELS[i]
                    pool.wait_ge(level_done, NL * b + i + 1)
                    if i == 1:
                        pool.wait_ge(f_ready, 2 * b + 2)
                    else:
                        pool.wait_ge(up_t, 7 * b + i - 1)
                        pool.wait_ge(up_k, 7 * b + i - 1)
                    n = W2 // (2 * size)
                    left = ks[:, :].rearrange("p (n s l) -> p n s l", s=2, l=size)[:, :, 0, :]
                    tt = total(size).rearrange("p (n s) -> p n s", s=2)[:, :, 1:2]
                    nc.gpsimd.tensor_tensor(left, left, bcast(tt, [P, n, size]), ALU.mult).then_inc(up_k, 1)

                def body(b, before, more):
                    for i in range(1, NL):
                        raise_k(b, i)

                over_sequences(pool, core.batches, body)

            @block.vector
            def _(dve):
                norm.normalise(dve, 0)
                norm.low(dve, 0)
                dve.wait_ge(masks_in, 16)
                nc.vector.tensor_copy(masks[:, :, :], masks_f[:, :, :])
                dve.wait_ge(zeroed, 1)

                def gated(b):
                    dve.wait_ge(o_ready, b + 1)
                    nc.vector.tensor_tensor(og[:, :, :], ob[:, :, :], gate[:, :, :], ALU.mult).then_inc(og_ready, 1)

                def gated_stats(b):
                    dve.wait_ge(og_ready, b + 1)
                    hold(dve, turns)
                    for t in range(NC):
                        op = nc.vector.bn_stats(o6[:, t, :], og[:, t, :])
                    op.then_inc(o_stat, 1)
                    dve.wait_ge(o_stat, b + 1)
                    hold(dve, turns)
                    for t in range(NC):
                        op = nc.vector.bn_aggr(omv[:, t, :], o6[:, t, :])
                    op.then_inc(o_aggr, 1)

                def o_norm(b):
                    dve.wait_ge(o_sd, b + 1)
                    nc.vector.reciprocal(ors[:, :], osd[:, :]).then_inc(o_rs, 1)
                    dve.wait_ge(o_rs, b + 1)
                    for t in range(NC):
                        op = nc.vector.tensor_scalar(og[:, t, :], og[:, t, :], omv[:, t, 0:1], ors[:, t:t + 1],
                                                     ALU.subtract, ALU.mult)
                    op.then_inc(on_ready, 1)

                def q_silu(b, h):
                    dve.wait_ge(sig_ready, 2 * b + h + 1)
                    r = slice(h * TOKENS, (h + 1) * TOKENS)
                    nc.vector.tensor_tensor(q[:, r], ab[:, h, :], sig[:, r], ALU.mult).then_inc(q_ready, 1)
                    dve.wait_ge(q_ready, 2 * b + h + 1)
                    dve.sem_inc(a_free[h], 1)

                def q_first(b):
                    dve.wait_ge(f_ready, 2 * b + 2)
                    nc.vector.tensor_tensor(qp[:, :], q[:, :], f[:, :], ALU.mult).then_inc(qp_ready, 1)

                def merge(b, i):
                    dve.wait_ge(level_done, NL * b + i + 1)
                    if i == 0 and not first(b):
                        dve.wait_ge(diag_copied, b)
                    if i:
                        dve.wait_ge(merged, SMALL * b + i)
                    hold(dve, turns)
                    nc.vector.copy_predicated(diag[:, :, :, :],
                                              bcast(masks[:, i, :].unsqueeze(1).unsqueeze(1), [P, GH0, NC, SUB]),
                                              hd).then_inc(merged, 1)

                def raise_q(b, i):
                    size = LEVELS[i]
                    dve.wait_ge(level_done, NL * b + i + 1)
                    if i == 1:
                        dve.wait_ge(qp_ready, b + 1)
                    else:
                        dve.wait_ge(up_q, 7 * b + i - 1)
                        dve.wait_ge(up_t, 7 * b + i - 1)
                    n = W2 // (2 * size)
                    right = qp[:, :].rearrange("p (n s l) -> p n s l", s=2, l=size)[:, :, 1, :]
                    tt = total(size).rearrange("p (n s) -> p n s", s=2)
                    nc.vector.tensor_tensor(right, right, bcast(tt[:, :, 0:1], [P, n, size]), ALU.mult).then_inc(up_q, 1)
                    if not first(b):
                        dve.wait_ge(up_k, 7 * b)
                    nc.vector.tensor_tensor(total(2 * size), tt[:, :, 0], tt[:, :, 1], ALU.mult).then_inc(up_t, 1)

                def g1_low(b):
                    dve.wait_ge(ghi_ready, b + 1)
                    nc.vector.tensor_tensor(glo[:, :], ab[:, 0, :], as_f32(ghi[:, :]), ALU.subtract).then_inc(glo_ready, 1)
                    dve.wait_ge(glo_ready, b + 1)
                    dve.sem_inc(a_free[0], 1)

                def states(b):
                    dve.wait_ge(s0_ready, b + 1)
                    dve.wait_ge(up_t, 7 * b + 7)
                    decay = total(CHUNK).rearrange("p (h c) -> p h c", h=GH0)
                    for c in range(1, NC - 1):
                        for h in range(GH0):
                            op = nc.vector.scalar_tensor_tensor(st[:, h, c, :], st[:, h, c - 1, :], decay[:, h, c:c + 1],
                                                                hb[:, h, c * P:(c + 1) * P], ALU.mult, ALU.add)
                        if c < NC - 2:
                            op.then_inc(st_step, 1)
                            dve.wait_ge(st_step, b + 1)
                    op.then_inc(st_ready, 1)

                def o_low(b):
                    dve.wait_ge(oh_ready, b + 1)
                    nc.vector.tensor_tensor(ol[:, :, :], tp[:, :, :], as_f32(oh[:, :, :]), ALU.subtract).then_inc(ol_ready, 1)

                def update(b):
                    dve.wait_ge(y_ps, b + 1)
                    xs = core.x[:, bass.ds(b * TILES, TILES), :]
                    nc.vector.tensor_tensor(xs, xs, aby, ALU.add).then_inc(x_done, 1)
                    dve.wait_ge(x_done, b + 1)
                    dve.sem_inc(a_free[0], 1)
                    dve.sem_inc(a_free[1], 1)

                def new_stats(b):
                    stats.take(dve, b, lambda: dve.wait_ge(x_done, b + 1))

                def body(b, before, more):
                    q_silu(b, 0)
                    if before:
                        gated(b - 1)
                    q_silu(b, 1)
                    q_first(b)
                    if before:
                        gated_stats(b - 1)
                    merge(b, 0)
                    if before:
                        o_norm(b - 1)
                    merge(b, 1)
                    raise_q(b, 1)
                    g1_low(b)
                    merge(b, 2)
                    raise_q(b, 2)
                    merge(b, 3)
                    raise_q(b, 3)
                    if before:
                        o_low(b - 1)
                    merge(b, 4)
                    raise_q(b, 4)
                    if more:
                        norm.normalise(dve, b + 1)
                    merge(b, 5)
                    raise_q(b, 5)
                    if more:
                        norm.low(dve, b + 1)
                    raise_q(b, 6)
                    if before:
                        update(b - 1)
                    raise_q(b, 7)
                    if before:
                        new_stats(b - 1)
                    states(b)

                over_sequences(dve, core.batches, body)
                last = core.batches - 1
                gated(last)
                gated_stats(last)
                o_norm(last)
                o_low(last)
                update(last)
                new_stats(last)


def program(nc, a, out, batches=16):
    with ExitStack() as ctx:
        core = Core(nc, ctx, batches)
        constants(core)
        core.end_stage()
        with ExitStack() as ffn_ctx:
            weights = FfnWeights(core, ffn_ctx)
            x_loaded = ffn_weights(core, weights, [a[k] for k in ("w_fc", "w_proj", "u_t", "v", "fast_bt", "gate")],
                                   a["x"], "ffn0")
            ffn_stage(core, weights, "ffn0", x_loaded)
            core.end_stage()
            gla_stage(core, a, "gla")
            core.end_stage()
            ffn_stage(core, weights, "ffn1")
            core.end_stage()
        moe_stage(core, a, "moe0")
        core.end_stage()
        att_stage(core, a, "att")
        core.end_stage()
        moe_stage(core, a, "moe1", out)




def layout(i):
    import numpy as np

    def f32(a):
        return np.ascontiguousarray(np.asarray(a))

    arrays = {
        "x": f32(i["L0_attn_x"]).reshape(-1, 256),
        "w_fc": f32(i["L0_ffn_w_fc"]),
        "w_proj": f32(i["L0_ffn_w_proj"]),
        "u_t": f32(np.asarray(i["L0_ffn_u"]).T),
        "v": f32(i["L0_ffn_v"]),
        "fast_bt": f32(np.asarray(i["L0_ffn_fast_b"]).T),
        "gate": f32(i["L0_ffn_gate"]).reshape(1, 1),
        "w_in_t": f32(np.asarray(i["L0_attn_W_in"]).T),
        "w_out_t": f32(np.asarray(i["L0_attn_W_out"]).T),
        "w_g1_t": f32(np.asarray(i["L0_attn_W_g1"]).T),
        "w_g2_t": f32(np.asarray(i["L0_attn_W_g2"]).T),
        "ln_w": f32(i["L0_attn_ln_w"]).reshape(-1, 1),
        "router_w": f32(i["L1_ffn_router_w"]),
        "router_b": f32(i["L1_ffn_router_b"]).reshape(1, -1),
        "routed_w1": f32(i["L1_ffn_routed_w1"]),
        "routed_w3": f32(i["L1_ffn_routed_w3"]),
        "routed_w2": f32(i["L1_ffn_routed_w2"]),
        "shared_w1": f32(i["L1_ffn_shared_w1"]),
        "shared_w3": f32(i["L1_ffn_shared_w3"]),
        "shared_w2": f32(i["L1_ffn_shared_w2"]),
    }
    arrays["level_masks"] = level_masks()
    for n in ("Wq", "Wk", "Wv", "Wo"):
        arrays[n.lower() + "_t"] = f32(np.asarray(i["L1_attn_" + n]).T)
    for n in ("bq", "bk", "bv", "bo", "ocr_bias"):
        arrays[n] = f32(i["L1_attn_" + n]).reshape(1, -1)
    return arrays


def kernel(**inputs):
    import concourse.bacc as _bacc
    from concourse import mybir as _mybir
    from concourse.bass_utils import run_bass_kernel_spmd as _run

    nc = _bacc.Bacc("TRN2", target_bir_lowering=False, num_devices=1)
    arrays = layout(inputs)
    args = {name: nc.dram_tensor(name, a.shape, _mybir.dt.from_np(a.dtype), kind="ExternalInput").ap()
            for name, a in arrays.items()}
    out = nc.dram_tensor("out", arrays["x"].shape, _mybir.dt.float32, kind="ExternalOutput").ap()
    program(nc, args, out)
    r = _run(nc, [arrays], core_ids=[0])
    return r.results[0]["out"].reshape(16, 512, 256)
```
